# Optimizing a Trainium2 kernel written in Bass

```python
import numpy as np
import jax
import jax.numpy as jnp

def _softmax(x, axis=-1):
    return jax.nn.softmax(x, axis=axis)

def _gelu(x):
    return jax.nn.gelu(x, approximate=True)

def _silu(x):
    return jax.nn.silu(x)

def _sigmoid(x):
    return jax.nn.sigmoid(x)

def _layernorm(x, axis=-1, eps=1e-05):
    m = jnp.mean(x, axis=axis, keepdims=True)
    v = jnp.var(x, axis=axis, keepdims=True)
    return (x - m) / jnp.sqrt(v + eps)

def _scatter_add(tgt, idx, src, axis=0):
    return tgt.at[idx].add(src)

def _segment_sum(src, seg, n):
    return jax.ops.segment_sum(src, seg, n)
kernel_name = 'mk_early_fusion_d1_tok_img256_r4_ef3f9c'

def setup_inputs(seed: int=0):
    np.random.seed(seed)
    _w = jnp.asarray

    def _rec_inputs():
        import jax
        import jax.numpy as jnp
        _rk = jax.random.key(seed)
        x = -0.000928989 + 1.00043 * jax.random.normal(jax.random.fold_in(_rk, 1), (64, 64, 64, 1), jnp.float32)
        txt = 0.142909 + 0.418953 * jax.random.normal(jax.random.fold_in(_rk, 2), (64, 32, 64), jnp.float32)
        return (x, txt)
    x, txt = _rec_inputs()

    def _L0_tok_setup():
        import jax, jax.numpy as jnp
        import numpy as np
        B, S, D_A, D_V, D_U, L, M1, M2 = (16, 64, 3, 32, 1, 4, 12, 12)
        MID = 4 * D_U

        def conv1x1(x, w, b):
            return jnp.einsum('bixy,oi->boxy', x, w) + b[None, :, None, None]

        def fourier_layer(x, fw_i):
            Bm, C, M, N = x.shape
            x_ft = jnp.fft.rfft2(x, s=(M, N), norm='ortho')
            w_lo = fw_i[0, ..., 0] + 1j * fw_i[0, ..., 1]
            w_hi = fw_i[1, ..., 0] + 1j * fw_i[1, ..., 1]
            lo = jnp.einsum('bixy,ioxy->boxy', x_ft[:, :, :M1, :M2], w_lo)
            hi = jnp.einsum('bixy,ioxy->boxy', x_ft[:, :, -M1:, :M2], w_hi)
            out_ft = jnp.zeros(x_ft.shape, dtype=x_ft.dtype)
            out_ft = out_ft.at[:, :, :M1, :M2].set(lo)
            out_ft = out_ft.at[:, :, -M1:, :M2].set(hi)
            return jnp.fft.irfft2(out_ft, s=(M, N), norm='ortho')

        def make_grid(b, sx, sy):
            gx = jnp.broadcast_to(jnp.linspace(0.0, 1.0, sx)[None, :, None], (b, sx, sy))
            gy = jnp.broadcast_to(jnp.linspace(0.0, 1.0, sy)[None, None, :], (b, sx, sy))
            return jnp.stack([gx, gy], axis=-1)
        key = jax.random.key(seed)
        ks = jax.random.split(key, 12)
        sc_v = 1.0 / np.sqrt(D_V)
        inp = {'x': jax.random.normal(ks[0], (B, S, S, D_A - 2), dtype=jnp.float32), 'p_w': jax.random.normal(ks[1], (D_V, D_A), dtype=jnp.float32) / np.sqrt(D_A), 'p_b': jnp.zeros((D_V,), dtype=jnp.float32), 'fw': jax.random.normal(ks[2], (L, 2, D_V, D_V, M1, M2, 2), dtype=jnp.float32) * sc_v, 'w1_w': jax.random.normal(ks[3], (L, D_V, D_V), dtype=jnp.float32) * sc_v, 'w1_b': jnp.zeros((L, D_V), dtype=jnp.float32), 'w2_w': jax.random.normal(ks[4], (L, D_V, D_V), dtype=jnp.float32) * sc_v, 'w2_b': jnp.zeros((L, D_V), dtype=jnp.float32), 'q1_w': jax.random.normal(ks[5], (MID, D_V), dtype=jnp.float32) * sc_v, 'q1_b': jnp.zeros((MID,), dtype=jnp.float32), 'q2_w': jax.random.normal(ks[6], (D_U, MID), dtype=jnp.float32) / np.sqrt(MID), 'q2_b': jnp.zeros((D_U,), dtype=jnp.float32)}
        return inp
    _L0_tok_all = _L0_tok_setup()
    _L0_tok_in = {k: v for k, v in _L0_tok_all.items() if k in ('p_w', 'p_b', 'fw', 'w1_w', 'w1_b', 'w2_w', 'w2_b', 'q1_w', 'q1_b', 'q2_w', 'q2_b')}
    del _L0_tok_all

    def _L0_attn_setup():
        import jax, jax.numpy as jnp
        import numpy as np
        TEMPERATURE = 1.0
        W_BLEND = 0.8
        EPS = 1e-12

        def _l2norm(x):
            n = jnp.sqrt(jnp.sum(x * x, axis=-1, keepdims=True))
            return x / jnp.maximum(n, EPS)
        key = jax.random.key(seed)
        feats = jax.random.normal(key, (4, 512, 64), dtype=jnp.float32)
        return {'feats': feats}
    _L0_attn_all = _L0_attn_setup()
    _L0_attn_in = {k: v for k, v in _L0_attn_all.items() if k in ()}
    del _L0_attn_all

    def _L0_ffn_setup():
        import jax, jax.numpy as jnp
        import numpy as np
        D_MODEL = 64
        EXPERT_DIM = 128
        NUM_EXPERTS = 8
        TOP_K = 2
        SEQ_LEN = 512
        BATCH = 2
        key = jax.random.key(seed)
        ks = jax.random.split(key, 8)
        s = 0.02
        x = jax.random.normal(ks[0], (SEQ_LEN, BATCH, D_MODEL), dtype=jnp.float32)
        Wg = jax.random.normal(ks[1], (D_MODEL, NUM_EXPERTS), dtype=jnp.float32) * s
        bg = jax.random.normal(ks[2], (NUM_EXPERTS,), dtype=jnp.float32) * s
        bias = jnp.zeros((NUM_EXPERTS,), dtype=jnp.float32)
        W1 = jax.random.normal(ks[3], (NUM_EXPERTS, D_MODEL, EXPERT_DIM), dtype=jnp.float32) * s
        b1 = jax.random.normal(ks[4], (NUM_EXPERTS, EXPERT_DIM), dtype=jnp.float32) * s
        W2 = jax.random.normal(ks[5], (NUM_EXPERTS, EXPERT_DIM, D_MODEL), dtype=jnp.float32) * s
        b2 = jax.random.normal(ks[6], (NUM_EXPERTS, D_MODEL), dtype=jnp.float32) * s
        return {'x': x, 'Wg': Wg, 'bg': bg, 'bias': bias, 'W1': W1, 'b1': b1, 'W2': W2, 'b2': b2}
    _L0_ffn_all = _L0_ffn_setup()
    _L0_ffn_in = {k: v for k, v in _L0_ffn_all.items() if k in ('Wg', 'bg', 'bias', 'W1', 'b1', 'W2', 'b2')}
    del _L0_ffn_all
    return {'x': x, 'txt': txt, 'L0_tok_p_w': _L0_tok_in['p_w'], 'L0_tok_p_b': _L0_tok_in['p_b'], 'L0_tok_fw': _L0_tok_in['fw'], 'L0_tok_w1_w': _L0_tok_in['w1_w'], 'L0_tok_w1_b': _L0_tok_in['w1_b'], 'L0_tok_w2_w': _L0_tok_in['w2_w'], 'L0_tok_w2_b': _L0_tok_in['w2_b'], 'L0_tok_q1_w': _L0_tok_in['q1_w'], 'L0_tok_q1_b': _L0_tok_in['q1_b'], 'L0_tok_q2_w': _L0_tok_in['q2_w'], 'L0_tok_q2_b': _L0_tok_in['q2_b'], 'L0_ffn_Wg': _L0_ffn_in['Wg'], 'L0_ffn_bg': _L0_ffn_in['bg'], 'L0_ffn_bias': _L0_ffn_in['bias'], 'L0_ffn_W1': _L0_ffn_in['W1'], 'L0_ffn_b1': _L0_ffn_in['b1'], 'L0_ffn_W2': _L0_ffn_in['W2'], 'L0_ffn_b2': _L0_ffn_in['b2']}

def reference(x, txt, L0_tok_p_w, L0_tok_p_b, L0_tok_fw, L0_tok_w1_w, L0_tok_w1_b, L0_tok_w2_w, L0_tok_w2_b, L0_tok_q1_w, L0_tok_q1_b, L0_tok_q2_w, L0_tok_q2_b, L0_ffn_Wg, L0_ffn_bg, L0_ffn_bias, L0_ffn_W1, L0_ffn_b1, L0_ffn_W2, L0_ffn_b2):
    import jax
    import jax.numpy as jnp

    def _L0_tok_ref(x, p_w, p_b, fw, w1_w, w1_b, w2_w, w2_b, q1_w, q1_b, q2_w, q2_b):
        import jax, jax.numpy as jnp
        import numpy as np
        B, S, D_A, D_V, D_U, L, M1, M2 = (16, 64, 3, 32, 1, 4, 12, 12)
        MID = 4 * D_U

        def conv1x1(x, w, b):
            return jnp.einsum('bixy,oi->boxy', x, w) + b[None, :, None, None]

        def fourier_layer(x, fw_i):
            Bm, C, M, N = x.shape
            x_ft = jnp.fft.rfft2(x, s=(M, N), norm='ortho')
            w_lo = fw_i[0, ..., 0] + 1j * fw_i[0, ..., 1]
            w_hi = fw_i[1, ..., 0] + 1j * fw_i[1, ..., 1]
            lo = jnp.einsum('bixy,ioxy->boxy', x_ft[:, :, :M1, :M2], w_lo)
            hi = jnp.einsum('bixy,ioxy->boxy', x_ft[:, :, -M1:, :M2], w_hi)
            out_ft = jnp.zeros(x_ft.shape, dtype=x_ft.dtype)
            out_ft = out_ft.at[:, :, :M1, :M2].set(lo)
            out_ft = out_ft.at[:, :, -M1:, :M2].set(hi)
            return jnp.fft.irfft2(out_ft, s=(M, N), norm='ortho')

        def make_grid(b, sx, sy):
            gx = jnp.broadcast_to(jnp.linspace(0.0, 1.0, sx)[None, :, None], (b, sx, sy))
            gy = jnp.broadcast_to(jnp.linspace(0.0, 1.0, sy)[None, None, :], (b, sx, sy))
            return jnp.stack([gx, gy], axis=-1)
        b, sx, sy = (x.shape[0], x.shape[1], x.shape[2])
        grid = make_grid(b, sx, sy)
        h = jnp.concatenate([x, grid], axis=-1)
        h = jnp.transpose(h, (0, 3, 1, 2))
        h = conv1x1(h, p_w, p_b)
        for i in range(L):
            x1 = fourier_layer(h, fw[i])
            x1 = jax.nn.relu(conv1x1(x1, w1_w[i], w1_b[i]))
            x1 = conv1x1(x1, w2_w[i], w2_b[i])
            h = h + x1
        h = conv1x1(h, q1_w, q1_b)
        h = jax.nn.relu(h)
        h = conv1x1(h, q2_w, q2_b)
        return jnp.squeeze(h)

    def _L0_attn_ref(feats):
        import jax, jax.numpy as jnp
        import numpy as np
        TEMPERATURE = 1.0
        W_BLEND = 0.8
        EPS = 1e-12

        def _l2norm(x):
            n = jnp.sqrt(jnp.sum(x * x, axis=-1, keepdims=True))
            return x / jnp.maximum(n, EPS)
        B, N, C = feats.shape
        f = _l2norm(feats.reshape(B * N, C))
        scores = jnp.matmul(f, f.T) / TEMPERATURE
        attn = jax.nn.softmax(scores, axis=-1)
        feats_att = jnp.matmul(attn, f)
        feats_fcm = f * W_BLEND + feats_att * (1.0 - W_BLEND)
        return _l2norm(feats_fcm.reshape(B, N, C))

    def _L0_ffn_ref(x, Wg, bg, bias, W1, b1, W2, b2):
        import jax, jax.numpy as jnp
        import numpy as np
        D_MODEL = 64
        EXPERT_DIM = 128
        NUM_EXPERTS = 8
        TOP_K = 2
        SEQ_LEN = 512
        BATCH = 2
        x_flat = x.reshape(-1, D_MODEL)
        gate_logits = x_flat @ Wg + bg + bias
        topk_vals, topk_idx = jax.lax.top_k(gate_logits, TOP_K)
        topk_w = jax.nn.softmax(topk_vals, axis=-1)
        combine = (jax.nn.one_hot(topk_idx, NUM_EXPERTS, dtype=x.dtype) * topk_w[..., None]).sum(axis=1)
        h = jax.nn.relu(jnp.einsum('td,edh->teh', x_flat, W1) + b1)
        y = jnp.einsum('teh,ehd->ted', h, W2) + b2
        out = jnp.einsum('ted,te->td', y, combine)
        return out.reshape(x.shape)
    h = _L0_tok_ref(x, L0_tok_p_w, L0_tok_p_b, L0_tok_fw, L0_tok_w1_w, L0_tok_w1_b, L0_tok_w2_w, L0_tok_w2_b, L0_tok_q1_w, L0_tok_q1_b, L0_tok_q2_w, L0_tok_q2_b)
    h = jnp.concatenate([h, txt], axis=1)
    h = h + _L0_attn_ref(_layernorm(h, axis=-1))
    h = h + _L0_ffn_ref(_layernorm(h, axis=-1), L0_ffn_Wg, L0_ffn_bg, L0_ffn_bias, L0_ffn_W1, L0_ffn_b1, L0_ffn_W2, L0_ffn_b2)
    return h

_drawn_inputs = setup_inputs


def setup_inputs(seed=0):
    import zlib

    import numpy as np

    out = dict(_drawn_inputs(seed))
    spreads = {'L0_tok_p_b': (0.0, 0.1),
     'L0_tok_w1_b': (0.0, 0.1),
     'L0_tok_w2_b': (0.0, 0.1),
     'L0_tok_q1_b': (0.0, 0.1),
     'L0_ffn_bias': (0.0, 0.268)}
    factors = {'L0_ffn_bg': 7.379, 'L0_ffn_b1': 8.0}
    for name, (base, spread) in spreads.items():
        noise = np.random.default_rng([zlib.crc32(name.encode()), seed]).standard_normal(out[name].shape)
        drawn = base * np.exp(spread * noise) if base else spread * noise
        out[name] = jnp.asarray(drawn.astype(out[name].dtype))
    for name, factor in factors.items():
        out[name] = (out[name] * factor).astype(out[name].dtype)
    return out
```

```python
from contextlib import ExitStack

import numpy as np

import concourse.bass as bass
from concourse import mybir

ALU = mybir.AluOpType
ACT = mybir.ActivationFunctionType
AX = mybir.AxisListType
F32 = mybir.dt.float32
F16 = mybir.dt.float16

P = 128
B = 64
S = 64
C = 32
L = 4
MODES = 12
KX = 2 * MODES
MID = 4
OCT = 8
NOCT = C // OCT
N = OCT * B
XP = 16
CH = MODES * B
HC = CH // 2
TXT = 32
SEQ = S + TXT
D = 64
NT = 48
E = 8
HID = 128

T_DB, T_EA, T_D1, T_D2, T_ID, T_BM, T_M32, T_GX, T_GY, T_SEL, T_END = np.cumsum(
    [0, 2 * P, 2 * P, 64, 64, P, 16, 32, 32, 1, E * P]).tolist()


def constant_table():
    t = np.zeros((P, T_END), np.float64)
    y = np.arange(S)
    ky = np.arange(MODES)
    kx = np.r_[np.arange(MODES), np.arange(S - MODES, S)]
    phi = 2 * np.pi * np.outer(ky, y) / S
    theta = 2 * np.pi * np.outer(kx, y) / S
    twice = np.where(ky == 0, 1.0, 2.0)[:, None]
    for g in range(2):
        for x2 in range(2):
            for ro, m in enumerate((twice * np.cos(phi) / 8, -twice * np.sin(phi) / 8)):
                r = 64 * g + 24 * x2 + MODES * ro
                c = T_DB + P * g + S * x2
                t[r:r + MODES, c:c + S] = m
        re, im = 64 * g, 64 * g + KX
        c = T_EA + P * g
        t[re:re + KX, c:c + S] = np.cos(theta) / 8
        t[im:im + KX, c:c + S] = -np.sin(theta) / 8
        t[re:re + KX, c + S:c + P] = np.sin(theta) / 8
        if g == 0:
            t[48, c:c + S] = 8.0
        t[im:im + KX, c + S:c + P] = np.cos(theta) / 8
    for x2 in range(2):
        c = T_D1 + 24 * x2
        t[64 * x2:64 * x2 + S, c:c + MODES] = np.cos(phi).T / 8
        t[64 * x2:64 * x2 + S, c + MODES:c + 24] = -np.sin(phi).T / 8
    t[0:S, T_D2:T_D2 + KX] = np.cos(theta).T / 8
    t[S:P, T_D2:T_D2 + KX] = np.sin(theta).T / 8
    t[0:S, T_D2 + KX:T_D2 + 48] = -np.sin(theta).T / 8
    t[S:P, T_D2 + KX:T_D2 + 48] = np.cos(theta).T / 8
    t[:, T_ID:T_ID + P] = np.eye(P)
    p = np.arange(P)
    t[:, T_BM:T_BM + 16] = p[:, None] % 16 == np.arange(16)
    q = np.arange(32)
    t[:, T_M32:T_M32 + 32] = (p[:, None] // 64 == q // 16) & (p[:, None] % 16 == q % 16)
    for xp in range(32):
        t[:, T_GX + xp] = (2 * xp + p // 64) / (S - 1)
    t[:, T_GY] = (p % 64) / (S - 1)
    for e in range(E):
        t[[e, 32 + e], T_SEL + P * e:T_SEL + P * (e + 1)] = 2.0 ** -10
    return t.astype(np.float32)


def paced(eng, first, lo, hi, last, step):
    for k in range(first, lo):
        step(k, k % 2, k // 2)
    with eng.Fori(lo // 2, hi // 2) as i:
        for p in range(2):
            step(i * 2 + p, p, i)
    for k in range(hi, last):
        step(k, k % 2, k // 2)


def wait_alone(eng, sem, value, passed):
    eng.wait_ge(sem, value)
    if not isinstance(value, int):
        eng.sem_inc(passed, 1)


def inside(k, lo, hi):
    return not isinstance(k, int) or lo <= k < hi


def operator_stage(nc, A, scratch, tokens_out):
    with ExitStack() as ctx:
        def sb(name, shape, dt=F32):
            return ctx.enter_context(nc.sbuf_tensor(name, shape, dt))

        def sem(name):
            return ctx.enter_context(nc.semaphore(name))

        tab = sb("tab", [P, T_SEL])
        spec = sb("spec", [P, MODES, CH])
        field = sb("field", [P, XP * N])
        half = sb("half", [P, XP, N])
        qacc = sb("qacc", [P, XP, N])
        zt = sb("zt", [P, MODES // 2, N])
        u = sb("u", [P, 2, 3, N])
        tt = sb("tt", [P, 3, 2, N])
        rr = sb("rr", [P, 2, N])
        r = sb("r", [P, 2, 2, N])
        rt = sb("rt", [P, 2, 2, N])
        w1all = sb("w1all", [P, L, P])
        w2all = sb("w2all", [P, L, P])
        w1s = sb("w1s", [P, P])
        w2s = sb("w2s", [P, P])
        b2all = sb("b2all", [P, L, MODES])
        gall = sb("gall", [P, 1 + L * NOCT, MID, 16])
        gs = sb("gs", [P, MID * 16])
        wg = sb("wg", [C, 1 + L, C])
        q1t = sb("q1t", [C, MID])
        b2t = sb("b2t", [C, L])
        q1b = sb("q1b", [P, 1])
        q2c = sb("q2c", [P, 1])
        q2m = sb("q2m", [P, 32])
        q2b = sb("q2b", [32, 1])
        qb = sb("qb", [P, 2])
        wch, rs, fst, zc, zo = (field[:, 2 * CH * i:2 * CH * (i + 1)].rearrange("p (s n) -> p s n", s=2)
                                for i in range(5))
        wrep = half[0:C, 0:5, :].rearrange("p k n -> p (k n)")[:, 0:(1 + L * NOCT) * P]
        q1rep = half[0:C, 5, 0:64]

        ps = ctx.enter_context(nc.psum_tensor("ps", [P, 8, 512], F32))
        ps_b = [ps[:, 0, :], ps[:, 1, :]]
        ps_t = [ps[:, 2, :], ps[:, 3, :]]
        ps_q, ps_f = ps[:, 4, :], ps[:, 5, :]
        ps_a = [ps[:, 6, :], ps[:, 7, :]]
        ps_w2, ps_mix, ps_w1 = (ps[:, 2 * i:2 * i + 2, 0:HC] for i in range(3))

        def db(g):
            return tab[:, T_DB + P * g:T_DB + P * (g + 1)]

        def ea(g):
            return tab[:, T_EA + P * g:T_EA + P * (g + 1)]

        def by_channel(ap):
            return ap.rearrange("p (c o b) -> p o c b", c=4, o=OCT)

        def by_channel_out(ap):
            return ap.rearrange("p (o c b) -> p o c b", c=4, o=OCT)

        def by_images(ap):
            return ap.rearrange("p (o c b) -> p c o b", c=4, o=OCT)

        def by_images_out(ap):
            return ap.rearrange("p (c o b) -> p c o b", c=4, o=OCT)

        d1, d2 = tab[:, T_D1:T_D1 + 64], tab[:, T_D2:T_D2 + 64]
        ident, bmask = tab[:, T_ID:T_ID + P], tab[:, T_BM:T_BM + 16]

        const_ld, zeroed = sem("const_ld"), sem("zeroed")
        sp_passed, pool_passed, pe_passed = sem("sp_passed"), sem("pool_passed"), sem("pe_passed")
        x_ld = [sem("x_ld0"), sem("x_ld1")]
        g_mm, g_ok, b_ok, qb_mm, qb_ok = (sem(n) for n in ("g_mm", "g_ok", "b_ok", "qb_mm", "qb_ok"))
        w_ld, rs_ld = [sem("w_ld0"), sem("w_ld1")], [sem("rs_ld0"), sem("rs_ld1")]
        w_neg, w2_mm, f_new, f_cp = (sem(n) for n in ("w_neg", "w2_mm", "f_new", "f_cp"))
        mix_mm, zc_ev, w1_mm, zo_ev, wts = (sem(n) for n in ("mix_mm", "zc_ev", "w1_mm", "zo_ev", "wts"))
        z_st = [sem("z_st0"), sem("z_st1")]
        zt_ld, a_mm = sem("zt_ld"), sem("a_mm")
        a_ev = [sem("a_ev0"), sem("a_ev1")]
        u_st, ut_ld, b_mm = [sem("u_st0"), sem("u_st1")], sem("ut_ld"), sem("b_mm")
        r_ok, t_mm, rt_ok = ([sem(f"{n}{g}") for g in range(2)] for n in ("r_ok", "t_mm", "rt_ok"))
        q_mm, q_ad, y_mm, y_ev, t_st = (sem(n) for n in ("q_mm", "q_ad", "y_mm", "y_ev", "t_st"))
        tt_ld = [sem(f"tt_ld{i}") for i in range(3)]
        x_mm, x_ev = sem("x_mm"), [sem("x_ev0"), sem("x_ev1")]
        r_st = [sem("r_st0"), sem("r_st1")]
        gs_ok = sem("gs_ok")
        q_act, q2_mm, h_ev, h_st = (sem(n) for n in ("q_act", "q2_mm", "h_ev", "h_st"))
        NCONST = 8 + 4 * 3

        z_d, u_d, t_d, r_d = (scratch[n] for n in ("z", "u", "t", "r"))

        def prime(eng, *sems):
            for s in sems:
                eng.sem_inc(s, 1)

        block = ctx.enter_context(nc.Block())

        def layers(eng, octets, spectral, epilogue):
            spectral(0, True)
            with eng.Fori(0, L - 1) as l:
                octets(l, True)
                spectral(l + 1, False)
            octets(L - 1, False)
            epilogue()

        def store_half(sp, m):
            for hb in range(2):
                wait_alone(sp, y_ev, m * XP + 8 * (hb + 1), sp_passed)
                if hb == 0 and not (isinstance(m, int) and m == 0):
                    for s in range(3):
                        wait_alone(sp, tt_ld[s], m * 64, sp_passed)
                for g in range(2):
                    for x2 in range(2):
                        row, x0 = 64 * g + 24 * x2, 32 * g + 16 * hb + x2
                        dst = t_d[x0:x0 + 15:2, :, :, :].rearrange("k r y n -> (r y) k n")
                        sp.dma_start(dst, half[row:row + 24, 8 * hb:8 * hb + 8, :]).then_inc(t_st, 16)

        def evac(eng, out, in_):
            return nc.scalar.copy(out, in_) if eng is nc.scalar else nc.vector.tensor_copy(out, in_)

        def stage_a_evac(eng, m, par):
            on = nc.scalar if par == 0 else nc.vector
            for ky in range(par, MODES, 2):
                eng.wait_ge(a_mm, m * MODES + ky + 1 + 1)
                bt = ky // 3
                if not (isinstance(m, int) and m == 0 and bt < 2):
                    eng.wait_ge(u_st[bt % 2], m * 64 + 32 * (bt // 2) + 1)
                evac(on, u[:, bt % 2, ky % 3, :], ps_a[par]).then_inc(a_ev[par], 1)

        def forward_x_evac(eng, m, par):
            on = nc.scalar if par == 0 else nc.vector
            for j in range(par, 6, 2):
                eng.wait_ge(x_mm, m * 6 + j + 1)
                if not (isinstance(m, int) and m == 0 and j < 2):
                    eng.wait_ge(r_st[par], m * 96 + 32 * (j // 2))
                evac(on, rr[:, par, :], ps_a[par]).then_inc(x_ev[par], 1)

        @block.sync
        def _(sp):
            prime(sp, *u_st)
            def const(dst, src):
                sp.dma_start(dst, src).then_inc(const_ld, 16)

            const(tab[:, :], A["table"][:, 0:T_SEL])
            sp.wait_ge(zeroed, 1)
            for i in range(4):
                const(w1all[32 * i:32 * i + 32, :, 32 * i:32 * i + 32], A["w1t"].rearrange("l i o -> i l o"))
                const(w2all[32 * i:32 * i + 32, 1:L, 32 * i:32 * i + 32],
                      A["w2t"].rearrange("l i o -> i l o")[:, 0:L - 1, :])
                const(w2all[32 * i:32 * i + MID, 0, 32 * i:32 * i + 32], A["pt"])
            const(wg[:, 1:1 + L, :], A["w2"].rearrange("l o i -> o l i"))
            const(wg[:, 0, 0:OCT], A["pc"])
            const(q1t[:, :], A["q1t"])
            const(b2t[:, :], A["b2t"])
            const(q1b[:, :], A["q1b"])
            const(q2c[:, :], A["q2c"])
            const(q2b[:, :], A["q2b"])

            xv = A["xt"]
            def x_step(k, p, i):
                if not (isinstance(k, int) and k < 2):
                    wait_alone(sp, y_mm, k - 1, sp_passed)
                for g in range(2):
                    sp.dma_start(by_channel(r[:, p, g, :])[:, 0], xv[g * XP + k, :, :].rearrange("p (c b) -> p c b", c=4)).then_inc(x_ld[p], 16)
            paced(sp, 0, 2, XP, XP, x_step)
            store_half(sp, 0)

            def spectral(l, first):
                if not first:
                    wait_alone(sp, b_mm, l * (2 * XP * NOCT) + 1, sp_passed)
                for s in range(2):
                    wait_alone(sp, r_st[s], 96 if first else l * (96 * NOCT) + 96, sp_passed)

                def load(c, p, i):
                    if not (first and isinstance(c, int) and c < 2):
                        wait_alone(sp, mix_mm, l * MODES + c - 1, sp_passed)
                    sp.dma_start(wch[:, p, :], A["fwt"][l, :, c, :]).then_inc(w_ld[p], 16)
                    for h in range(2):
                        for ri in range(2):
                            row, n = 64 * h + 32 * ri, (OCT if first else C)
                            src = r_d[0:n, KX * ri + MODES * h + c, :]
                            sp.dma_start(rs[row:row + n, p, :], src).then_inc(rs_ld[p], 16)
                paced(sp, 0, 2, MODES, MODES, load)

            def octets(l, forward):
                def u_store(n, bt, m):
                    wait_alone(sp, a_ev[0], m * 6 + (3 * bt + 2) // 2 + 1 + 1, sp_passed)
                    wait_alone(sp, a_ev[1], m * 6 + (3 * bt + 3) // 2 + 1, sp_passed)
                    for ri in range(2):
                        sp.dma_start(u_d[:, ri, 3 * bt:3 * bt + 3, :], u[64 * ri:64 * ri + 64, bt % 2, :, :]
                                     ).then_inc(u_st[bt % 2], 16)

                def field_load(m):
                    for s in range(2):
                        wait_alone(sp, u_st[s], m * 64 + 64 + 1, sp_passed)
                    if not (isinstance(m, int) and m == 0):
                        wait_alone(sp, b_mm, m * (2 * XP) + 1, sp_passed)
                    for g in range(2):
                        for x2 in range(2):
                            row = 64 * g + 24 * x2
                            src = u_d[g * 32 + x2:g * 32 + x2 + 31:2, :, :, :].rearrange("k r y n -> (r y) k n")
                            dst = field[row:row + 24, :].rearrange("p (k n) -> p k n", k=XP)
                            sp.dma_start(dst, src).then_inc(ut_ld, 16)

                def one(n, more):
                    m = l * NOCT + n
                    if forward:
                        store_half(sp, m + 1)
                    if more:
                        for bt in range(4):
                            u_store(n + 1, bt, m + 1)
                        field_load(m + 1)

                wait_alone(sp, f_cp, l * MODES + MODES, sp_passed)
                for s in range(2):
                    wait_alone(sp, z_st[s], l * (64 * 6) + 64 * 6, sp_passed)
                for bt in range(4):
                    u_store(0, bt, l * NOCT)
                field_load(l * NOCT)
                with sp.Fori(0, NOCT - 1) as n:
                    one(n, True)
                one(NOCT - 1, False)

            def epilogue():
                wait_alone(sp, h_ev, XP, sp_passed)
                hd = tokens_out.rearrange("(c b) (g k x) y -> g c b k (x y)", c=4, g=2, k=XP)
                hs = half[0:32, :, :].rearrange("p k (c n) -> p k c n", c=4)
                for g in range(2):
                    for c in range(4):
                        sp.dma_start(hd[g, c], hs[16 * g:16 * g + 16, :, c, :]).then_inc(h_st, 16)
                wait_alone(sp, h_st, 16 * 8, sp_passed)

            layers(sp, octets, spectral, epilogue)

        @block.gpsimd
        def _(pool):
            def forward_x(m, new_modes):
                wait_alone(pool, t_st, m * 128 + 128, pool_passed)
                def load(j):
                    if not (isinstance(m, int) and m == 0 and j < 3):
                        wait_alone(pool, x_mm, m * 6 + j - 2, pool_passed)
                    for ri in range(2):
                        pool.dma_start(tt[64 * ri:64 * ri + 64, j % 3, :, :], t_d[:, ri, 2 * j:2 * j + 2, :]
                                       ).then_inc(tt_ld[j % 3], 16)
                for j in range(3):
                    load(j)
                for j in range(6):
                    if j + 3 < 6:
                        load(j + 3)
                    wait_alone(pool, x_ev[j % 2], m * 3 + j // 2 + 1, pool_passed)
                    for g in range(2):
                        dst = new_modes[:, :, 64 * (2 * j + g):64 * (2 * j + g) + 64].rearrange("o k b -> k o b")
                        pool.dma_start(dst, rr[64 * g:64 * g + 48, j % 2, :].rearrange("p (o b) -> p o b", o=OCT)
                                       ).then_inc(r_st[j % 2], 16)

            forward_x(0, r_d[0:OCT])

            def spectral(l, first):
                def step(c, p, i):
                    if inside(c, 0, 12):
                        wait_alone(pool, w_ld[p], (l * 6 + i) * 16 + 16, pool_passed)
                        if not (first and isinstance(c, int) and c < 2):
                            wait_alone(pool, f_cp, l * MODES + (c - 1 if inside(c, 1, 13) else 0), pool_passed)
                        for h in range(2):
                            rows = wch[64 * h + 32:64 * h + 64, p, :].rearrange("p (m o) -> p m o", o=64)[:, :, 0:C]
                            nc.gpsimd.tensor_scalar(rows, rows, -1.0, None, ALU.mult).then_inc(w_neg, 1)
                    if inside(c, 1, 13):
                        wait_alone(pool, f_new, (l * MODES + c) * 2, pool_passed)
                        wait_alone(pool, w_neg, (l * MODES + (c + 1 if inside(c, 0, 12) else 12)) * 2, pool_passed)
                        nc.gpsimd.tensor_copy(spec[:, c - 1, :], fst[:, 1 - p, :]).then_inc(f_cp, 1)
                    if inside(c, 3, 15):
                        wait_alone(pool, zo_ev, l * MODES + c - 2, pool_passed)
                        for h in range(2):
                            for ri in range(2):
                                row = 64 * h + 32 * ri
                                pool.dma_start(z_d[:, KX * ri + MODES * h + c - 3, :],
                                               zo[row:row + 32, 1 - p, :]).then_inc(z_st[1 - p], 16)
                paced(pool, 0, 4, 12, 15, step)

            def zt_load(l, n):
                m = l * NOCT + n
                if not (isinstance(m, int) and m == 0):
                    wait_alone(pool, a_mm, m * MODES + 1, pool_passed)
                src = z_d[bass.ds(n * OCT, OCT)]
                for g in range(2):
                    for i in range(6):
                        ky = 2 * i + g
                        pool.dma_start(zt[64 * g:64 * g + 48, i, :].rearrange("p (o b) -> p o b", o=OCT),
                                       src[:, :, B * ky:B * ky + B].rearrange("o k b -> k o b")
                                       ).then_inc(zt_ld, 16)
                pool.dma_start(zt[48:49, 0, :], A["b1w"][bass.ds(l, 1), bass.ds(n * N, N)]).then_inc(zt_ld, 16)

            def octets(l, forward):
                for s in range(2):
                    wait_alone(pool, z_st[s], l * (64 * 6) + 64 * 6, pool_passed)
                zt_load(l, 0)

                def one(n, more):
                    if more:
                        zt_load(l, n + 1)
                    if forward:
                        forward_x(l * NOCT + n + 1, r_d[bass.ds(n * OCT, OCT)])
                with pool.Fori(0, NOCT - 1) as n:
                    one(n, True)
                one(NOCT - 1, False)

            layers(pool, octets, spectral, lambda: None)

        @block.scalar
        def _(act):
            prime(act, a_ev[0])
            def main(m, o_b, forward):
                init = o_b is None
                def step(k, p, i):
                    if inside(k, 0, XP):
                        if not (isinstance(m, int) and isinstance(k, int) and k < 2):
                            act.wait_ge(y_mm if forward else t_mm[0], m * XP + k - 1)
                        if init:
                            act.wait_ge(x_ld[p], i * 32 + 32)
                            rc = by_channel(r[:, p, 0, :])
                            nc.scalar.activation(rc[:, 1], rc[:, 3], ACT.Copy,
                                                 scale=tab[:, bass.ds(k + T_GX, 1)]).then_inc(r_ok[0], 1)
                        else:
                            act.wait_ge(b_mm, (o_b * XP + k) * 2 + 1 + 1)
                            nc.scalar.activation(by_images_out(r[:, p, 0, :]), by_images(ps_b[0]), ACT.Relu).then_inc(r_ok[0], 1)
                    if inside(k, 1, XP + 1):
                        act.wait_ge(t_mm[0], m * XP + k)
                        if not (isinstance(m, int) and isinstance(k, int) and k < 3):
                            act.wait_ge(q_mm, m * XP + k - 2)
                        nc.scalar.copy(rt[:, 1 - p, 0, :], ps_t[0]).then_inc(rt_ok[0], 1)
                        if forward:
                            act.wait_ge(y_mm, m * XP + k)
                            if isinstance(k, int) and k == 1 and not (isinstance(m, int)):
                                act.wait_ge(t_st, m * 128)
                            nc.scalar.copy(half[:, k - 1, :], ps_f).then_inc(y_ev, 1)
                paced(act, 0, 4, 16, 18, step)

            act.wait_ge(const_ld, 16 * NCONST)
            act.wait_ge(zeroed, 2)
            main(0, None, True)
            forward_x_evac(act, 0, 0)

            def spectral(l, first):
                def step(c, p, i):
                    act.wait_ge(mix_mm, l * MODES + c + 1)
                    if not (first and isinstance(c, int) and c < 2):
                        act.wait_ge(w1_mm, l * MODES + c - 1)
                    nc.scalar.copy(zc[:, p, :].rearrange("p (a n) -> p a n", a=2), ps_mix).then_inc(zc_ev, 1)
                paced(act, 0, 2, 12, 12, step)

            def octets(l, forward):
                stage_a_evac(act, l * NOCT, 0)

                def one(n, more):
                    m = l * NOCT + n
                    main(m + 1, m, forward)
                    if more:
                        stage_a_evac(act, m + 1, 0)
                    if forward:
                        forward_x_evac(act, m + 1, 0)
                with act.Fori(0, NOCT - 1) as n:
                    one(n, True)
                one(NOCT - 1, False)

            def epilogue():
                act.wait_ge(qb_ok, 1)
                def step(k, p, i):
                    act.wait_ge(q_ad, (1 + L * NOCT) * XP)
                    nc.scalar.activation(qacc[:, k, :], qacc[:, k, :], ACT.Relu, bias=qb[:, 0:1]).then_inc(q_act, 1)
                paced(act, 0, 0, XP, XP, step)
            layers(act, octets, spectral, epilogue)

        @block.vector
        def _(dve):
            prime(dve, a_ev[1])
            v = nc.vector
            for buf in (w1all, w2all):
                v.memset(buf[:, :, :], 0.0)
            v.memset(b2all[:, :, :], 0.0)
            v.memset(wg[:, 0, :], 0.0).then_inc(zeroed, 1)
            v.memset(spec[:, :, :], 0.0)
            v.memset(field[:, :], 0.0)
            v.memset(zt[:, :, :], 0.0)
            for p in range(2):
                for g in range(2):
                    rc = by_channel(r[:, p, g, :])
                    v.memset(rc[:, 3], 1.0)
                    for j in range(4, OCT):
                        last = v.memset(rc[:, j], 0.0)
            last.then_inc(zeroed, 1)
            dve.wait_ge(const_ld, 16 * NCONST)
            dve.wait_ge(zeroed, 2)
            for p in range(2):
                for g in range(2):
                    rc = by_channel(r[:, p, g, :])
                    v.tensor_scalar(rc[:, 2], rc[:, 3],
                                    tab[:, T_GY:T_GY + 1], None, ALU.mult)
            v.tensor_scalar(b2all[0:C, 1:L, 0], b2t[:, 0:L - 1], 64.0, None, ALU.mult)
            wcols = wrep.rearrange("p (n b) -> p n b", b=16)
            v.tensor_copy(wcols[:, 0:OCT], wg[:, 0, 0:OCT, None].broadcast_to([C, OCT, 16]))
            v.tensor_copy(wcols[:, OCT:], wg[:, 1:, :].rearrange("p l c -> p (l c)")[:, :, None].broadcast_to([C, L * C, 16]))
            v.tensor_copy(q1rep.rearrange("p (n b) -> p n b", b=16), q1t[:, :, None].broadcast_to([C, MID, 16])).then_inc(b_ok, 1)
            for i in range(1 + L * NOCT):
                dve.wait_ge(g_mm, i + 1)
                gp = ps_b[i % 2][:, 0:MID]
                v.tensor_tensor(gall[:, i, :, :], gp[:, :, None].broadcast_to([P, MID, 16]),
                                bmask[:, None, :].broadcast_to([P, MID, 16]), ALU.mult).then_inc(g_ok, 1)
            v.tensor_scalar(q2m[:, :], tab[:, T_M32:T_M32 + 32], q2c[:, 0:1], None, ALU.mult).then_inc(b_ok, 1)
            dve.wait_ge(qb_mm, 1)
            v.tensor_reduce(qb[:, 1:2], ps_q[:, 0:L], AX.X, ALU.add).then_inc(b_ok, 1)
            dve.wait_ge(b_ok, 3)
            v.tensor_tensor(qb[:, 0:1], qb[:, 1:2], q1b[:, :], ALU.add).then_inc(qb_ok, 1)

            def main(m, o_b, forward):
                init = o_b is None
                if init:
                    dve.wait_ge(g_ok, 1 + L * NOCT)
                    v.tensor_copy(gs[:, :], gall[:, 0, :, :].rearrange("p a b -> p (a b)")).then_inc(gs_ok, 1)
                else:
                    dve.wait_ge(q_mm, m * XP)
                    v.tensor_copy(gs[:, :].rearrange("p (a b) -> p a b", a=MID),
                                  gall[:, bass.ds(m, 1), :, :].rearrange("p m a b -> p (m a) b")).then_inc(gs_ok, 1)

                def step(k, p, i):
                    if inside(k, 0, XP):
                        if not (isinstance(m, int) and isinstance(k, int) and k < 2):
                            dve.wait_ge(y_mm if forward else t_mm[1], m * XP + k - 1)
                        if init:
                            dve.wait_ge(x_ld[p], i * 32 + 32)
                            rc = by_channel(r[:, p, 1, :])
                            v.tensor_scalar(rc[:, 1], rc[:, 3],
                                            tab[:, bass.ds(k + (T_GX + XP), 1)], None, ALU.mult).then_inc(r_ok[1], 1)
                        else:
                            dve.wait_ge(b_mm, (o_b * XP + k) * 2 + 2 + 1)
                            v.tensor_scalar(by_images_out(r[:, p, 1, :]), by_images(ps_b[1]), 0.0, None, ALU.max).then_inc(r_ok[1], 1)
                    if inside(k, 1, XP + 1):
                        dve.wait_ge(t_mm[1], m * XP + k)
                        if not (isinstance(m, int) and isinstance(k, int) and k < 3):
                            dve.wait_ge(q_mm, m * XP + k - 2)
                        v.tensor_copy(rt[:, 1 - p, 1, :], ps_t[1]).then_inc(rt_ok[1], 1)
                    if inside(k, 2, XP + 2):
                        dve.wait_ge(q_mm, m * XP + k - 1)
                        if init:
                            v.tensor_copy(qacc[:, k - 2, :], ps_q).then_inc(q_ad, 1)
                        else:
                            v.tensor_tensor(qacc[:, k - 2, :], ps_q, qacc[:, k - 2, :], ALU.add).then_inc(q_ad, 1)
                paced(dve, 0, 4, 16, 18, step)

            main(0, None, True)
            forward_x_evac(dve, 0, 1)

            def spectral(l, first):
                if not first:
                    dve.wait_ge(w1_mm, l * MODES)
                v.tensor_copy(w1s[:, :], w1all[:, bass.ds(l, 1), :].rearrange("p l o -> p (l o)")).then_inc(wts, 1)
                v.tensor_copy(w2s[:, :], w2all[:, bass.ds(l, 1), :].rearrange("p l o -> p (l o)")).then_inc(wts, 1)

                def step(c, p, i):
                    if inside(c, 0, MODES):
                        dve.wait_ge(w2_mm, l * MODES + c + 1)
                        if not (first and isinstance(c, int) and c < 2):
                            dve.wait_ge(mix_mm, l * MODES + c - 1)
                            dve.wait_ge(f_cp, l * MODES + c - 1)
                        v.tensor_tensor(fst[:, p, :].rearrange("p (a n) -> p a n", a=2), ps_w2,
                                        spec[:, c, :].rearrange("p (a n) -> p a n", a=2), ALU.add).then_inc(f_new, 1)
                        dve.wait_ge(f_new, (l * MODES + c) * 2 + 1)
                        v.tensor_scalar(fst[:, p, 0:B], fst[:, p, 0:B],
                                        b2all[:, l, bass.ds(c, 1)] if isinstance(l, int) else
                                        b2all[:, bass.ds(l, 1), bass.ds(c, 1)].rearrange("p l c -> p (l c)"),
                                        None, ALU.add).then_inc(f_new, 1)
                    if inside(c, 2, MODES + 2):
                        dve.wait_ge(w1_mm, l * MODES + c - 1)
                        if not (first and isinstance(c, int) and c < 4):
                            dve.wait_ge(z_st[p], (l * 6 + i) * 64 - 64)
                        v.tensor_copy(zo[:, p, :].rearrange("p (a n) -> p a n", a=2), ps_w1).then_inc(zo_ev, 1)
                paced(dve, 0, 4, 12, 14, step)

            def octets(l, forward):
                stage_a_evac(dve, l * NOCT, 1)

                def one(n, more):
                    m = l * NOCT + n
                    main(m + 1, m, forward)
                    if more:
                        stage_a_evac(dve, m + 1, 1)
                    if forward:
                        forward_x_evac(dve, m + 1, 1)
                with dve.Fori(0, NOCT - 1) as n:
                    one(n, True)
                one(NOCT - 1, False)

            def epilogue():
                def step(k, p, i):
                    dve.wait_ge(q2_mm, k + 1)
                    v.tensor_scalar(half[0:32, k, :], ps_a[p][0:32, :], q2b[:, 0:1], None, ALU.add).then_inc(h_ev, 1)
                paced(dve, 0, 0, XP, XP, step)
            layers(dve, octets, spectral, epilogue)

        @block.tensor
        def _(pe):
            prime(pe, a_mm, b_mm)
            mm = nc.tensor.matmul
            pe.wait_ge(const_ld, 16 * NCONST)
            pe.wait_ge(zeroed, 2)
            pe.wait_ge(b_ok, 1)
            for i in range(1 + L * NOCT):
                if i >= 2:
                    pe.wait_ge(g_ok, i - 1)
                mm(ps_b[i % 2][:, 0:MID], wrep[:, P * i:P * i + P], q1t[:, :],
                   start=True, stop=True).then_inc(g_mm, 1)
            for g in range(2):
                last = mm(ps_q[64 * g:64 * g + 64, 0:L], q1rep,
                          b2t[:, :], start=True, stop=True)
            last.then_inc(qb_mm, 1)
            pe.wait_ge(qb_ok, 1)
            pe.wait_ge(g_ok, 1 + L * NOCT)

            def main(m, o_b, forward):
                def step(k, p, i):
                    if o_b is not None and inside(k, 0, XP):
                        if isinstance(k, int) and k == 0:
                            pe.wait_ge(ut_ld, o_b * 64 + 64)
                        for g in range(2):
                            pe.wait_ge(r_ok[g], m * XP + k)
                            rhs = field[:, bass.ds(k * N, N)] if not isinstance(k, int) else field[:, k * N:k * N + N]
                            mm(ps_b[g], db(g), rhs, start=True, stop=True).then_inc(b_mm, 1)
                    if inside(k, 1, XP + 1):
                        for g in range(2):
                            pe.wait_ge(r_ok[g], m * XP + k)
                            if not (isinstance(m, int) and isinstance(k, int) and k < 2):
                                pe.wait_ge(rt_ok[g], m * XP + k - 1)
                            for c in range(4):
                                cols = slice(P * c, P * c + P)
                                last = nc.tensor.transpose(ps_t[g][:, cols], r[:, 1 - p, g, cols], ident)
                            last.then_inc(t_mm[g], 1)
                        if forward:
                            if not (isinstance(m, int) and isinstance(k, int) and k < 2):
                                pe.wait_ge(y_ev, m * XP + k - 1)
                            for g in range(2):
                                last = mm(by_channel_out(ps_f[64 * g:64 * g + 64, :]), d1, by_channel(r[:, 1 - p, g, :]), start=True, stop=True)
                            last.then_inc(y_mm, 1)
                    if inside(k, 2, XP + 2):
                        if isinstance(k, int) and k == 2:
                            pe.wait_ge(gs_ok, m + 1)
                        if not (isinstance(m, int) and isinstance(k, int) and k < 3):
                            pe.wait_ge(q_ad, m * XP + k - 2)
                        for g in range(2):
                            pe.wait_ge(rt_ok[g], m * XP + k - 1)
                            last = mm(ps_q[64 * g:64 * g + 64, :], gs[:, :], rt[:, p, g, :], start=True, stop=True)
                        last.then_inc(q_mm, 1)
                paced(pe, 0, 4, 16, 18, step)

            def stage_a(m, gdone):
                pe.wait_ge(zt_ld, m * (16 * 13) + 16 * 13)
                for par in range(2):
                    pe.wait_ge(x_ev[par], gdone * 3)
                for ky in range(MODES):
                    if not (isinstance(m, int) and m == 0 and ky < 2):
                        pe.wait_ge(a_ev[ky % 2], m * 6 + ky // 2 + 1)
                    mm(ps_a[ky % 2], ea(ky % 2), zt[:, ky // 2, :], start=True, stop=True).then_inc(a_mm, 1)

            def forward_x(m, adone):
                if not (isinstance(adone, int) and adone == 0):
                    for par in range(2):
                        pe.wait_ge(a_ev[par], adone * 6 + 1)
                for j in range(6):
                    pe.wait_ge(tt_ld[j % 3], m * 64 + 32 * (j // 3) + 32)
                    if not (isinstance(m, int) and m == 0 and j < 2):
                        pe.wait_ge(x_ev[j % 2], m * 3 + j // 2)
                    for g in range(2):
                        last = mm(ps_a[j % 2][64 * g:64 * g + 64, :], d2, tt[:, j % 3, g, :], start=True, stop=True)
                    last.then_inc(x_mm, 1)

            main(0, None, True)
            forward_x(0, 0)

            def spectral(l, first):
                pe.wait_ge(wts, l * 2 + 2)

                m = l * NOCT + 1
                for g in range(2):
                    pe.wait_ge(rt_ok[g], m * XP)
                pe.wait_ge(q_ad, m * XP)
                pe.wait_ge(y_ev, m * XP)

                def step(c, p, i):
                    if inside(c, 0, MODES):
                        pe.wait_ge(rs_ld[p], (l * 6 + i) * 64 + 64)
                        if not (first and isinstance(c, int) and c < 1):
                            pe.wait_ge(f_new, (l * MODES + c) * 2)
                        for a in range(2):
                            last = mm(ps_w2[:, a, :], w2s[:, :], rs[:, p, HC * a:HC * a + HC], start=True, stop=True)
                        last.then_inc(w2_mm, 1)
                    if inside(c, 1, MODES + 1):
                        pe.wait_ge(w_neg, (l * MODES + c) * 2)
                        pe.wait_ge(f_new, (l * MODES + c) * 2)
                        if not (first and isinstance(c, int) and c < 2):
                            pe.wait_ge(zc_ev, l * MODES + c - 1)
                        pe.sem_inc(pe_passed, 1)
                        q = 1 - p
                        for ky in range(MODES):
                            for h in range(2):
                                rows = slice(64 * h, 64 * h + 64)
                                last = mm(ps_mix[rows, ky // 6, B * (ky % 6):B * (ky % 6) + B],
                                          wch[rows, q, 64 * ky:64 * ky + 64], fst[rows, q, B * ky:B * ky + B],
                                          start=True, stop=True)
                        last.then_inc(mix_mm, 1)
                    if inside(c, 2, MODES + 2):
                        pe.wait_ge(zc_ev, l * MODES + c - 1)
                        if not (first and isinstance(c, int) and c < 3):
                            pe.wait_ge(zo_ev, l * MODES + c - 2)
                        for a in range(2):
                            last = mm(ps_w1[:, a, :], w1s[:, :], zc[:, p, HC * a:HC * a + HC], start=True, stop=True)
                        last.then_inc(w1_mm, 1)
                paced(pe, 0, 4, 12, 14, step)

            def octets(l, forward):
                pe.wait_ge(f_new, l * (2 * MODES) + 2 * MODES)
                pe.wait_ge(zc_ev, l * MODES + MODES)
                pe.wait_ge(zo_ev, l * MODES + MODES)
                stage_a(l * NOCT, l * NOCT + 1)

                def one(n, more):
                    m = l * NOCT + n
                    main(m + 1, m, forward)
                    if more:
                        stage_a(m + 1, m + 1 if forward else (L - 1) * NOCT + 1)
                    if forward:
                        forward_x(m + 1, m + 2 if more else m + 1)
                with pe.Fori(0, NOCT - 1) as n:
                    one(n, True)
                one(NOCT - 1, False)

            def epilogue():
                pe.wait_ge(b_ok, 3)
                for par in range(2):
                    pe.wait_ge(a_ev[par], L * NOCT * 6 + 1)
                def step(k, p, i):
                    if not (isinstance(k, int) and k < 2):
                        pe.wait_ge(h_ev, k - 1)
                    pe.wait_ge(q_act, k + 1)
                    mm(ps_a[p][0:32, :], q2m[:, :], qacc[:, k, :], start=True, stop=True).then_inc(q2_mm, 1)
                paced(pe, 0, 2, XP, XP, step)
            layers(pe, octets, spectral, epilogue)


def token_stage(nc, A, h_d, out):
    with ExitStack() as ctx:
        def sb(name, shape, dt=F32):
            return ctx.enter_context(nc.sbuf_tensor(name, shape, dt))

        def sem(name):
            return ctx.enter_context(nc.semaphore(name))

        NG = NT // 4
        NC = NT // 8
        SCALE = 256.0
        WSCALE = 1024.0
        tok = sb("tok", [P, NT, D])
        f = sb("f", [P, NT, D])
        att = sb("att", [P, NT, D])
        tmp = sb("tmp", [P, NT, D])
        z = att
        fhl = sb("fhl", [P, 3, NT, 2, D], F16)
        x = sb("x", [P, 3, NT * P], F16)
        zt = fhl[:, 0, :, :, :].rearrange("p t c d -> p (t c d)").bitcast(F32)
        fj = sb("fj", [P, 2, D])
        e = sb("e", [P, 2, 1024])
        ot = sb("ot", [P, 512])
        rs = sb("rsum", [P, NT, NC])
        st = sb("st", [P, 8, NT])
        idt = sb("idt", [P, P])
        idh = sb("idh", [P, P], F16)
        self32 = sb("self32", [P, E * P])
        sel = sb("sel", [P, E * P], F16)
        w1 = sb("w1", [P, 2, E, HID])
        w2 = sb("w2", [P, E, D])
        wgt = sb("wgt", [P, 2 * E])
        b1 = sb("b1", [P, E])
        b2 = sb("b2", [P, 2, P])
        bgb = sb("bgb", [P, 2, E])
        lg = sb("lg", [P, NT, E])
        cw = sb("cw", [P, NT, E])
        pick = sb("pick", [P, 2, NT, E])
        wt32 = sb("wt32", [P, NT * P])
        wth = sb("wth", [P, NT * P], F16)
        hb = e[:, :, :].rearrange("p a (b n) -> p a b n", b=2)
        hw = sb("hw", [P, 2, 2, 512])
        ps = ctx.enter_context(nc.psum_tensor("ps_tok", [P, 8, 512], F32))

        ld, small, chain, rooted = sem("ld"), sem("small"), sem("chain"), sem("rooted")
        sp_passed = sem("sp_passed_tok")
        to_root, root_ok = sem("to_root"), sem("root_ok")
        idh_ok, split_ok = sem("idh_ok"), sem("split_ok")
        p_mm, p_ev = sem("p_mm"), [sem("p_ev0"), sem("p_ev1")]
        s_mm, exp_ok, fj_ok, pv_mm = (sem(n) for n in ("s_mm", "exp_ok", "fj_ok", "pv_mm"))
        ot_ok, ot_mm, att_ok = (sem(n) for n in ("ot_ok", "ot_mm", "att_ok"))
        z_ok, zt_mm, zt_ok, lg_mm, cw_ok, wt_mm, wt_ok = (sem(n) for n in (
            "z_ok", "zt_mm", "zt_ok", "lg_mm", "cw_ok", "wt_mm", "wt_ok"))
        h_mm, h_ok, wb_mm, hw_ok, y_mm, y_ok, yt_mm, o_ok, o_st = (sem(n) for n in (
            "th_mm", "th_ok", "wb_mm", "hw_ok", "ty_mm", "ty_ok", "yt_mm", "o_ok", "o_st"))
        N_LD, N_SMALL = 4, 11

        def prime(eng, *sems):
            for s in sems:
                eng.sem_inc(s, 1)

        block = ctx.enter_context(nc.Block())

        @block.sync
        def _(sp):
            hv = h_d.rearrange("b x y -> b (x y)")
            tv = A["txt"].rearrange("b s d -> b (s d)")
            tf = tok[:, :, :].rearrange("p t d -> p (t d)")
            sp.dma_start(tf[0:P:2, :], hv[:, 0:NT * D]).then_inc(ld, 16)
            sp.dma_start(tf[1:P:2, 0:16 * D], hv[:, NT * D:S * D]).then_inc(ld, 16)
            sp.dma_start(tf[1:P:2, 16 * D:], tv).then_inc(ld, 16)
            sp.dma_start(idt[:, :], A["table"][:, T_ID:T_ID + P]).then_inc(ld, 16)
            sp.wait_ge(rooted, 1)
            for dst, src in (
                    (self32[:, :], A["table"][:, T_SEL:T_END]),
                    (w1[0:64, 0, :, :], A["ew1"].rearrange("e c h -> c e h")),
                    (w1[64:P, 1, :, :], A["ew1"].rearrange("e c h -> c e h")),
                    (w2[:, :, :], A["ew2"].rearrange("e h c -> h e c")),
                    (wgt[0:64, 0:E], A["wg"]), (wgt[64:P, E:], A["wg"]),
                    (b1[:, :], A["eb1"]), (b2[0:E, 0, 0:D], A["eb2"]), (b2[0:E, 1, D:], A["eb2"]),
                    (bgb[:, 0, :], A["bg"]), (bgb[:, 1, :], A["bias"])):
                sp.dma_start(dst, src).then_inc(small, 16)
            ov = out.rearrange("b (r t) d -> (b r) (t d)", r=2)
            with sp.Fori(0, NC) as q:
                wait_alone(sp, o_ok, q + 1 + 1, sp_passed)
                sp.dma_start(ov[:, bass.ds(q * 8 * D, 8 * D)], tok[:, bass.ds(q * 8, 8), :].rearrange("p t d -> p (t d)")
                             ).then_inc(o_st, 16)
            sp.wait_ge(o_st, 16 * NC)

        @block.gpsimd
        def _(pool):
            g = nc.gpsimd
            g.memset(w1[:, :, :, :], 0.0)
            g.memset(wgt[:, :], 0.0)
            g.memset(b2[:, :, :], 0.0)
            g.memset(wt32[:, :], 0.0)
            g.memset(wth[:, :], 0.0).then_inc(rooted, 1)

        def wide(col, n=D):
            return col[:, :, None].broadcast_to([P, NT, n])

        @block.vector
        def _(dve):
            prime(dve, ot_ok, att_ok, hw_ok, y_ok, o_ok, p_ev[1])
            v = nc.vector
            done = [0]

            def then(ins):
                done[0] += 1
                ins.then_inc(chain, 1)
                dve.wait_ge(chain, done[0])

            n_root = [0]

            def center(src, dst):
                then(v.tensor_reduce(st[:, 0, :], src[:, :, :], AX.X, ALU.add))
                then(v.tensor_scalar(st[:, 0, :], st[:, 0, :], 1.0 / D, None, ALU.mult))
                then(v.tensor_tensor(dst[:, :, :], src[:, :, :], wide(st[:, 0, :]), ALU.subtract))
                then(v.tensor_tensor(tmp[:, :, :], dst[:, :, :], dst[:, :, :], ALU.mult))
                then(v.tensor_reduce(st[:, 1, :], tmp[:, :, :], AX.X, ALU.add))
                v.tensor_scalar(st[:, 2, :], st[:, 1, :], 1.0 / D, 1e-5, ALU.mult, ALU.add).then_inc(to_root, 1)
                n_root[0] += 1
                dve.wait_ge(root_ok, n_root[0])
                then(v.reciprocal(st[:, 3, :], st[:, 2, :]))

            dve.wait_ge(ld, 16 * N_LD)
            v.tensor_copy(idh[:, :], idt[:, :]).then_inc(idh_ok, 1)
            center(tok, f)
            then(v.tensor_tensor(st[:, 4, :], st[:, 1, :], st[:, 3, :], ALU.mult))
            then(v.tensor_scalar(st[:, 4, :], st[:, 4, :], 1e-12, None, ALU.max))
            then(v.reciprocal(st[:, 5, :], st[:, 4, :]))
            then(v.tensor_tensor(st[:, 4, :], st[:, 5, :], st[:, 3, :], ALU.mult))
            then(v.tensor_tensor(f[:, :, :], f[:, :, :], wide(st[:, 4, :]), ALU.mult))
            then(v.tensor_scalar(fhl[:, 0, :, 0, :], f[:, :, :], SCALE, None, ALU.mult))
            then(v.scalar_tensor_tensor(out=fhl[:, 0, :, 1, :], in0=f[:, :, :], scalar=SCALE, in1=fhl[:, 0, :, 0, :],
                                        op0=ALU.mult, op1=ALU.subtract))
            for c in range(2):
                v.tensor_copy(fhl[:, 1, :, c, :], fhl[:, 0, :, 0, :])
                last = v.tensor_copy(fhl[:, 2, :, c, :], fhl[:, 0, :, 1, :])
            last.then_inc(split_ok, 1)

            with dve.Fori(0, NG // 2) as i:
                dve.wait_ge(p_mm, i * 2 + 2)
                v.tensor_copy(x[:, :, bass.ds(i * 1024 + 512, 512)], ps[:, 3:6, :]).then_inc(p_ev[1], 1)

            with dve.Fori(0, NC) as ci:
                def step(j, p, i):
                    if not (isinstance(j, int) and j < 2):
                        dve.wait_ge(pv_mm, ci * NT + j - 1)
                    else:
                        dve.wait_ge(att_ok, ci + 1)
                    v.tensor_copy(fj[:, p, :], f[:, bass.ds(j, 1), :].rearrange("p t d -> p (t d)")
                                  ).then_inc(fj_ok, 1)
                paced(dve, 0, 2, NT, NT, step)
                dve.wait_ge(pv_mm, ci * NT + NT)
                v.tensor_copy(ot[:, :], ps[:, 4, :]).then_inc(ot_ok, 1)
                dve.wait_ge(ot_mm, ci + 1)
                v.tensor_copy(att[:, bass.ds(ci * 8, 8), :].rearrange("p (h s) d -> p s h d", h=2),
                              ps[:, 5, :].rearrange("p (s h d) -> p s h d", s=4, h=2)).then_inc(att_ok, 1)

            dve.wait_ge(exp_ok, NC * NT + 1)
            dve.wait_ge(att_ok, NC + 1)
            then(v.tensor_reduce(st[:, 4, :], rs[:, :, :], AX.X, ALU.add))
            then(v.reciprocal(st[:, 5, :], st[:, 4, :]))
            then(v.tensor_scalar(st[:, 5, :], st[:, 5, :], 1.0 - 0.8, None, ALU.mult))
            then(v.tensor_tensor(att[:, :, :], att[:, :, :], wide(st[:, 5, :]), ALU.mult))
            then(v.scalar_tensor_tensor(out=att[:, :, :], in0=f[:, :, :], scalar=0.8, in1=att[:, :, :],
                                        op0=ALU.mult, op1=ALU.add))
            then(v.tensor_tensor(tmp[:, :, :], att[:, :, :], att[:, :, :], ALU.mult))
            v.tensor_reduce(st[:, 1, :], tmp[:, :, :], AX.X, ALU.add).then_inc(to_root, 1)
            n_root[0] += 1
            dve.wait_ge(root_ok, n_root[0])
            then(v.tensor_scalar(st[:, 4, :], st[:, 1, :], 1e-12, None, ALU.max))
            then(v.reciprocal(st[:, 5, :], st[:, 4, :]))
            then(v.tensor_tensor(att[:, :, :], att[:, :, :], wide(st[:, 5, :]), ALU.mult))
            then(v.tensor_tensor(tok[:, :, :], tok[:, :, :], att[:, :, :], ALU.add))
            center(tok, z)
            v.tensor_tensor(z[:, :, :], z[:, :, :], wide(st[:, 3, :]), ALU.mult).then_inc(z_ok, 1)

            for i in range(NC):
                dve.wait_ge(zt_mm, i + 1)
                v.tensor_copy(zt[:, 512 * i:512 * i + 512], ps[:, i % 2, :]).then_inc(zt_ok, 1)
            dve.wait_ge(small, 16 * N_SMALL)
            then(v.tensor_tensor(bgb[:, 0, :], bgb[:, 0, :], bgb[:, 1, :], ALU.add))
            dve.wait_ge(lg_mm, 1)
            then(v.tensor_tensor(lg[:, :, :], ps[:, 2, 0:NT * E].rearrange("p (t e) -> p t e", e=E),
                                 bgb[:, 0:1, :].broadcast_to([P, NT, E]), ALU.add))
            for n in range(2):
                top = st[:, 4 + n, :]
                then(v.tensor_reduce(top, lg[:, :, :], AX.X, ALU.max))
                then(v.tensor_tensor(pick[:, n, :, :], lg[:, :, :], wide(top, E), ALU.is_equal))
                then(v.memset(st[:, 6, :], 1.0))
                for i in range(E):
                    then(v.tensor_tensor(pick[:, n, :, i], pick[:, n, :, i], st[:, 6, :], ALU.mult))
                    then(v.tensor_tensor(st[:, 6, :], st[:, 6, :], pick[:, n, :, i], ALU.subtract))
                if n == 0:
                    then(v.scalar_tensor_tensor(out=lg[:, :, :], in0=pick[:, 0, :, :], scalar=-3e38,
                                                in1=lg[:, :, :], op0=ALU.mult, op1=ALU.add))
            v.tensor_tensor(st[:, 6, :], st[:, 5, :], st[:, 4, :], ALU.subtract).then_inc(to_root, 1)
            n_root[0] += 1
            dve.wait_ge(root_ok, n_root[0])
            then(v.tensor_scalar(st[:, 0, :], st[:, 6, :], 1.0, None, ALU.add))
            then(v.reciprocal(st[:, 1, :], st[:, 0, :]))
            then(v.tensor_tensor(st[:, 2, :], st[:, 1, :], st[:, 6, :], ALU.mult))
            then(v.tensor_tensor(cw[:, :, :], pick[:, 0, :, :], wide(st[:, 1, :], E), ALU.mult))
            then(v.tensor_tensor(lg[:, :, :], pick[:, 1, :, :], wide(st[:, 2, :], E), ALU.mult))
            v.tensor_tensor(cw[:, :, :], cw[:, :, :], lg[:, :, :], ALU.add).then_inc(cw_ok, 1)
            v.tensor_copy(sel[:, :], self32[:, :]).then_inc(cw_ok, 1)
            dve.wait_ge(rooted, 1)
            for i in range(NG):
                dve.wait_ge(wt_mm, i + 1)
                cols = slice(512 * i, 512 * i + 512)
                src = ps[0:E, 3 + i % 2, :]
                v.tensor_copy(wt32[0:E, cols], src)
                then(v.tensor_scalar(wth[0:E, cols], src, WSCALE, None, ALU.mult))
                v.scalar_tensor_tensor(out=wth[32:32 + E, cols], in0=src, scalar=WSCALE, in1=wth[0:E, cols],
                                       op0=ALU.mult, op1=ALU.subtract).then_inc(wt_ok, 1)

            with dve.Fori(0, NC) as q:
                for i in range(E):
                    for par in range(2):
                        dve.wait_ge(wb_mm, q * (2 * E) + (2 * i + par + 1))
                        dve.wait_ge(h_ok, q * (2 * E) + (2 * i + par + 1) + 1)
                        if i >= 2:
                            dve.wait_ge(y_mm, q * E + (i - 1))
                        v.tensor_tensor(hw[:, i % 2, par, :], ps[:, 4 + par, :], hb[:, i % 2, par, :], ALU.mult
                                        ).then_inc(hw_ok, 1)
                dve.wait_ge(y_mm, q * E + E)
                v.tensor_copy(ot[:, :], ps[:, 6, :]).then_inc(y_ok, 1)
                dve.wait_ge(yt_mm, q + 1)
                chunk = tok[:, bass.ds(q * 8, 8), :].rearrange("p t d -> p (t d)")
                v.tensor_tensor(chunk, ps[:, 7, :], chunk, ALU.add).then_inc(o_ok, 1)

        @block.scalar
        def _(act):
            prime(act, exp_ok, h_ok, p_ev[0])
            def root(n, cols):
                act.wait_ge(to_root, n)
                nc.scalar.activation(st[:, cols, :], st[:, cols, :], ACT.Sqrt).then_inc(root_ok, 1)

            root(1, slice(1, 3))
            with act.Fori(0, NG // 2) as i:
                act.wait_ge(p_mm, i * 2 + 1)
                nc.scalar.copy(x[:, :, bass.ds(i * 1024, 512)], ps[:, 0:3, :]).then_inc(p_ev[0], 1)

            with act.Fori(0, NC) as ci:
                def step(j, p, i):
                    act.wait_ge(s_mm, ci * NT + j + 1)
                    if not (isinstance(j, int) and j < 2):
                        act.wait_ge(pv_mm, ci * NT + j - 1)
                    else:
                        act.wait_ge(ot_ok, ci + 1)
                    nc.scalar.activation(e[:, p, :], ps[:, 2 * p:2 * p + 2, :].rearrange("p a n -> p (a n)"), ACT.Exp,
                                         scale=1.0 / (SCALE * SCALE),
                                         accum_out=rs[:, bass.ds(j, 1), bass.ds(ci, 1)].rearrange("p t c -> p (t c)")
                                         ).then_inc(exp_ok, 1)
                paced(act, 0, 2, NT, NT, step)
            root(2, slice(1, 2))
            root(3, slice(1, 3))
            act.wait_ge(to_root, 4)
            nc.scalar.activation(st[:, 6, :], st[:, 6, :], ACT.Exp).then_inc(root_ok, 1)
            act.wait_ge(small, 16 * N_SMALL)
            with act.Fori(0, NC) as q:
                for i in range(E):
                    for par in range(2):
                        act.wait_ge(h_mm, q * (2 * E) + (2 * i + par + 1))
                        if i >= 2:
                            act.wait_ge(hw_ok, q * (2 * E) + (2 * i + par - 3) + 1)
                        else:
                            act.wait_ge(hw_ok, q * (2 * E) + 1)
                        nc.scalar.activation(hb[:, i % 2, par, :], ps[:, 2 * (i % 2) + par, :], ACT.Relu,
                                             bias=b1[:, i:i + 1]).then_inc(h_ok, 1)

        @block.tensor
        def _(pe):
            mm = nc.tensor.matmul
            pe.wait_ge(idh_ok, 1)
            pe.wait_ge(split_ok, 1)
            with pe.Fori(0, NG // 2) as i:
                for p in range(2):
                    pe.wait_ge(p_ev[p], i + 1)
                    for kind in range(3):
                        for t in range(4):
                            src = fhl[:, kind, bass.ds(i * 8 + (4 * p + t), 1), :, :].rearrange("p t c d -> p (t c d)")
                            last = mm(ps[:, 3 * p + kind, P * t:P * t + P], src, idh[:, :], start=True, stop=True)
                    last.then_inc(p_mm, 1)
            for p in range(2):
                pe.wait_ge(p_ev[p], NG // 2 + 1)

            with pe.Fori(0, NC) as ci:
                def step(j, p, i):
                    if inside(j, 0, NT):
                        if not (isinstance(j, int) and j < 2):
                            pe.wait_ge(exp_ok, ci * NT + j - 1 + 1)
                        else:
                            pe.wait_ge(exp_ok, ci * NT + 1)
                        for h in range(2):
                            for kind in range(2):
                                last = mm(ps[:, 2 * p + h, :], x[:, 1 + kind, bass.ds(j * P, P)],
                                          x[:, 0, bass.ds(ci * 1024 + 512 * h, 512)], start=(kind == 0), stop=(kind == 1))
                        last.then_inc(s_mm, 1)
                    if inside(j, 1, NT + 1):
                        pe.wait_ge(exp_ok, ci * NT + j + 1)
                        pe.wait_ge(fj_ok, ci * NT + j)
                        if isinstance(j, int) and j == 1:
                            pe.wait_ge(ot_ok, ci + 1)
                        q = 1 - p
                        for h in range(2):
                            last = mm(ps[64 * h:64 * h + 64, 4, :], fj[:, q, :], e[:, q, 512 * h:512 * h + 512],
                                      start=isinstance(j, int) and j == 1, stop=isinstance(j, int) and j == NT)
                        last.then_inc(pv_mm, 1)
                paced(pe, 0, 2, NT, NT + 1, step)
                pe.wait_ge(ot_ok, ci + 1 + 1)
                pe.wait_ge(att_ok, ci + 1)
                for s in range(4):
                    last = nc.tensor.transpose(ps[:, 5, P * s:P * s + P], ot[:, P * s:P * s + P], idt[:, :])
                last.then_inc(ot_mm, 1)

            pe.wait_ge(z_ok, 1)
            for i in range(NC):
                if i >= 2:
                    pe.wait_ge(zt_ok, i - 1)
                for s in range(4):
                    t = 8 * i + 2 * s
                    src = z[:, t:t + 2, :].rearrange("p t d -> p (t d)")
                    last = nc.tensor.transpose(ps[:, i % 2, P * s:P * s + P], src, idt[:, :])
                last.then_inc(zt_mm, 1)
            pe.wait_ge(small, 16 * N_SMALL)
            pe.wait_ge(zt_ok, NC)
            for i in range(NT // 2):
                last = mm(ps[:, 2, 2 * E * i:2 * E * i + 2 * E], zt[:, P * i:P * i + P], wgt[:, :], start=True, stop=True)
            last.then_inc(lg_mm, 1)
            pe.wait_ge(cw_ok, 2)
            for i in range(NG):
                if i >= 2:
                    pe.wait_ge(wt_ok, i - 1)
                for s in range(4):
                    t = 8 * (i // 2) + 2 * s + i % 2
                    last = nc.tensor.transpose(ps[0:E, 3 + i % 2, P * s:P * s + P], cw[:, t, :], idt[:, :])
                last.then_inc(wt_mm, 1)
            pe.wait_ge(wt_ok, NG)

            with pe.Fori(0, NC) as q:
                def down(i):
                    for par in range(2):
                        pe.wait_ge(hw_ok, q * (2 * E) + (2 * i + par + 1) + 1)
                        last = mm(ps[64 * par:64 * par + 64, 6, :], w2[:, i, :], hw[:, i % 2, par, :],
                                  start=False, stop=(i == E - 1))
                    last.then_inc(y_mm, 1)

                for i in range(E):
                    for par in range(2):
                        if i >= 2:
                            pe.wait_ge(h_ok, q * (2 * E) + (2 * i + par - 3) + 1)
                        else:
                            pe.wait_ge(h_ok, q * (2 * E) + 1)
                        mm(ps[:, 2 * (i % 2) + par, :], w1[:, par, i, :], zt[:, bass.ds(q * 512, 512)],
                           start=True, stop=True).then_inc(h_mm, 1)
                    for par in range(2):
                        if i >= 1:
                            pe.wait_ge(hw_ok, q * (2 * E) + (2 * i + par - 1) + 1)
                        else:
                            pe.wait_ge(hw_ok, q * (2 * E) + 1)
                        mm(ps[:, 4 + par, :], sel[:, P * i:P * i + P], wth[:, bass.ds(q * 1024 + 512 * par, 512)],
                           start=True, stop=True).then_inc(wb_mm, 1)
                    if i == 0:
                        pe.wait_ge(y_ok, q + 1)
                        for par in range(2):
                            mm(ps[:, 6, :], b2[:, par, :], wt32[:, bass.ds(q * 1024 + 512 * par, 512)],
                               start=(par == 0), stop=False)
                    else:
                        down(i - 1)
                down(E - 1)
                pe.wait_ge(y_ok, q + 1 + 1)
                pe.wait_ge(o_ok, q + 1)
                for s in range(4):
                    last = nc.tensor.transpose(ps[:, 7, P * s:P * s + P], ot[:, P * s:P * s + P], idt[:, :])
                last.then_inc(yt_mm, 1)


def build_kernel(nc, A, out):
    scratch = {
        "z": nc.dram_tensor("modes_scratch", [C, 2 * KX, CH], F32).ap(),
        "r": nc.dram_tensor("new_modes_scratch", [C, 2 * KX, CH], F32).ap(),
        "u": nc.dram_tensor("inverse_scratch", [S, 2, MODES, N], F32).ap(),
        "t": nc.dram_tensor("forward_scratch", [S, 2, MODES, N], F32).ap(),
    }
    h_d = nc.dram_tensor("h_scratch", [B, S, S], F32).ap()
    operator_stage(nc, A, scratch, h_d)
    token_stage(nc, A, h_d, out)


def kernel(**inputs):
    import concourse.bacc as _bacc
    from concourse.bass_utils import run_bass_kernel_spmd as _run

    def get(name):
        return np.asarray(inputs[name])

    def tok(name):
        return get("L0_tok_" + name)

    pw, pb, fw = tok("p_w"), tok("p_b"), tok("fw")
    by_mode = fw.transpose(0, 1, 2, 4, 5, 6, 3)
    arrays = {
        "table": constant_table(),
        "xt": get("x")[..., 0].transpose(1, 2, 0).reshape(32, P, B),
        "w1t": tok("w1_w").transpose(0, 2, 1),
        "w2t": tok("w2_w").transpose(0, 2, 1),
        "w2": tok("w2_w"),
        "pt": np.concatenate([pw.T, pb[None]], 0),
        "pc": np.pad(np.concatenate([pw, pb[:, None]], 1), ((0, 0), (0, OCT - MID))),
        "q1t": tok("q1_w").T,
        "b2t": tok("w2_b").T,
        "q1b": np.tile(np.repeat(tok("q1_b"), 16), 2)[:, None],
        "q2c": np.tile(np.repeat(tok("q2_w")[0], 16), 2)[:, None],
        "q2b": np.broadcast_to(tok("q2_b"), (32, 1)),
        "b1w": np.repeat(tok("w1_b"), B, axis=1),
        "fwt": np.stack([by_mode, by_mode[:, :, :, :, :, ::-1]], 2).reshape(L, P, MODES, CH),
        "txt": get("txt"),
        "ew1": get("L0_ffn_W1"),
        "ew2": get("L0_ffn_W2"),
        "wg": get("L0_ffn_Wg"),
        "eb1": get("L0_ffn_b1").T,
        "eb2": get("L0_ffn_b2"),
        "bg": np.broadcast_to(get("L0_ffn_bg"), (P, E)),
        "bias": np.broadcast_to(get("L0_ffn_bias"), (P, E)),
    }
    arrays = {f"in_{name}": np.ascontiguousarray(a) for name, a in arrays.items()}
    nc = _bacc.Bacc("TRN2", target_bir_lowering=False, num_devices=1)
    A = {name[3:]: nc.dram_tensor(name, a.shape, mybir.dt.from_np(a.dtype), kind="ExternalInput").ap()
         for name, a in arrays.items()}
    out = nc.dram_tensor("out_dram", (B, SEQ, D), F32, kind="ExternalOutput").ap()
    build_kernel(nc, A, out)
    r = _run(nc, [arrays], core_ids=[0])
    return r.results[0]["out_dram"]
```

```python
from contextlib import ExitStack

import numpy as np

import concourse.bass as bass
from concourse import mybir

ALU = mybir.AluOpType
ACT = mybir.ActivationFunctionType
AX = mybir.AxisListType
F32 = mybir.dt.float32
F16 = mybir.dt.float16

P = 128
B = 64
S = 64
C = 32
L = 4
MODES = 12
KX = 2 * MODES
MID = 4
OCT = 8
NOCT = C // OCT
N = OCT * B
XP = 16
CH = MODES * B
HC = CH // 2
TXT = 32
SEQ = S + TXT
D = 64
NT = 48
E = 8
HID = 128

T_DB, T_EA, T_D1, T_D2, T_ID, T_BM, T_M32, T_GX, T_GY, T_SEL, T_END = np.cumsum(
    [0, P, 2 * P, 64, 64, P, 16, 32, 32, 1, E * P]).tolist()


def constant_table():
    t = np.zeros((P, T_END), np.float64)
    y = np.arange(S)
    ky = np.arange(MODES)
    kx = np.r_[np.arange(MODES), np.arange(S - MODES, S)]
    phi = 2 * np.pi * np.outer(ky, y) / S
    theta = 2 * np.pi * np.outer(kx, y) / S
    twice = np.where(ky == 0, 1.0, 2.0)[:, None]
    for x2 in range(2):
        for ro, m in enumerate((twice * np.cos(phi) / 8, -twice * np.sin(phi) / 8)):
            for hl in range(2):
                r = 48 * x2 + 24 * ro + MODES * hl
                t[r:r + MODES, T_DB + S * x2:T_DB + S * x2 + S] = m
    for g in range(2):
        re, im = 64 * g, 64 * g + KX
        c = T_EA + P * g
        t[re:re + KX, c:c + S] = np.cos(theta) / 8
        t[im:im + KX, c:c + S] = -np.sin(theta) / 8
        t[re:re + KX, c + S:c + P] = np.sin(theta) / 8
        if g == 0:
            t[48, c:c + S] = 8.0
        t[im:im + KX, c + S:c + P] = np.cos(theta) / 8
    for x2 in range(2):
        c = T_D1 + 24 * x2
        t[64 * x2:64 * x2 + S, c:c + MODES] = np.cos(phi).T / 8
        t[64 * x2:64 * x2 + S, c + MODES:c + 24] = -np.sin(phi).T / 8
    t[0:S, T_D2:T_D2 + KX] = np.cos(theta).T / 8
    t[S:P, T_D2:T_D2 + KX] = np.sin(theta).T / 8
    t[0:S, T_D2 + KX:T_D2 + 48] = -np.sin(theta).T / 8
    t[S:P, T_D2 + KX:T_D2 + 48] = np.cos(theta).T / 8
    t[:, T_ID:T_ID + P] = np.eye(P)
    p = np.arange(P)
    q = np.arange(32)
    t[:, T_BM:T_BM + 16] = (p[:, None] // 32 == q[:16] // 4) & (p[:, None] % 4 == q[:16] % 4)
    t[:, T_M32:T_M32 + 32] = (p[:, None] // 16 == q // 4) & (p[:, None] % 4 == q % 4)
    for xp in range(32):
        t[:, T_GX + xp] = (2 * xp + p // 64) / (S - 1)
    t[:, T_GY] = (p % 64) / (S - 1)
    for e in range(E):
        t[[e, 32 + e], T_SEL + P * e:T_SEL + P * (e + 1)] = 2.0 ** -10
    return t.astype(np.float32)


def paced(eng, first, lo, hi, last, step):
    for k in range(first, lo):
        step(k, k % 2, k // 2)
    with eng.Fori(lo // 2, hi // 2) as i:
        for p in range(2):
            step(i * 2 + p, p, i)
    for k in range(hi, last):
        step(k, k % 2, k // 2)


def paced4(eng, lo, hi, last, step):
    for k in range(lo):
        step(k, k % 4, k // 2)
    with eng.Fori(0, (hi - lo) // 4) as i:
        for n in range(lo, lo + 4):
            step(i * 4 + n, n % 4, i * 2 + n // 2)
    for k in range(hi, last):
        step(k, k % 4, k // 2)


def wait_alone(eng, sem, value, passed):
    eng.wait_ge(sem, value)
    if not isinstance(value, int):
        eng.sem_inc(passed, 1)


def inside(k, lo, hi):
    return not isinstance(k, int) or lo <= k < hi


def operator_stage(nc, A, scratch, tokens_out):
    with ExitStack() as ctx:
        def sb(name, shape, dt=F32):
            return ctx.enter_context(nc.sbuf_tensor(name, shape, dt))

        def sem(name):
            return ctx.enter_context(nc.semaphore(name))

        TT = 5
        tab = sb("tab", [P, T_SEL])
        spec = sb("spec", [P, MODES, CH])
        field = sb("field", [P, XP * N])
        half = sb("half", [P, XP, N])
        qacc = sb("qacc", [P, XP, N])
        zt = sb("zt", [P, MODES // 2, N])
        u = sb("u", [P, 2, 2, 2, N], F16)
        tt = sb("tt", [P, TT, 2, N])
        rr = sb("rr", [P, 2, N])
        r = sb("r", [P, 2, 2, N])
        rt = sb("rt", [P, 2, 2, N])
        w1all = sb("w1all", [P, L, P])
        w2all = sb("w2all", [P, L, P])
        w1s = sb("w1s", [P, P])
        w2s = sb("w2s", [P, P])
        b2all = sb("b2all", [P, L, MODES])
        gall = sb("gall", [P, 1 + L * NOCT, 4, MID, 4])
        gs = sb("gs", [P, 64])
        wg = sb("wg", [C, 1 + L, C])
        q1t = sb("q1t", [C, MID])
        b1t = sb("b1t", [C, L])
        b2t = sb("b2t", [C, L])
        q1b = sb("q1b", [P, 1])
        q2c = sb("q2c", [P, 1])
        q2m = sb("q2m", [P, 32])
        q2b = sb("q2b", [32, 1])
        qb = sb("qb", [P, 2])
        dbh = sb("dbh", [P, 2, P], F16)
        peak = sb("peak", [P, MODES + 1])
        scl = sb("scl", [P, 8])
        ones = sb("ones", [1, P])
        fst, zc = (field[:, 2 * CH * i:2 * CH * (i + 1)].rearrange("p (s n) -> p s n", s=2) for i in range(2))
        zo = field[:, 4 * CH:8 * CH].rearrange("p (s n) -> p s n", s=4)
        wch, rs = (half[:, :, :].rearrange("p k n -> p (k n)")[:, 4 * CH * i:4 * CH * (i + 1)].rearrange(
            "p (s n) -> p s n", s=4) for i in range(2))
        f16 = field[:, :].bitcast(F16).rearrange("p (k g n) -> p k g n", g=2, k=XP)
        u_first = [u[:, 0, :, :, :], u[:, 1, :, :, :]] + [
            b[:, p, :, :].rearrange("p g n -> p (g n)").bitcast(F16).rearrange("p (h y n) -> p h y n", h=2, y=2)
            for b in (r, rt) for p in range(2)]
        wrep = half[0:C, 0:5, :].rearrange("p k n -> p (k n)")[:, 0:(1 + L * NOCT) * P]
        q1rep = half[0:C, 5, 0:64]
        xs = tt[:, 0:2, :, :].rearrange("p s y n -> p (s y n)").rearrange("p (x b) -> p x b", b=B)

        ps = ctx.enter_context(nc.psum_tensor("ps", [P, 8, 512], F32))
        ps_b = [[ps[:, 2 * p + g, :] for g in range(2)] for p in range(2)]
        ps_q, ps_f = ps[:, 4, :], ps[:, 5, :]
        ps_a = [ps[:, 6, :], ps[:, 7, :]]
        ps_w2, ps_mix, ps_w1 = (ps[:, 2 * i:2 * i + 2, 0:HC] for i in range(3))

        def ea(g):
            return tab[:, T_EA + P * g:T_EA + P * (g + 1)]

        def by_octet(ap):
            return ap.rearrange("p (c o b) -> p o c b", c=16, o=OCT)

        def octets_of(ap):
            return ap.rearrange("p (o c b) -> p o c b", c=16, o=OCT)

        d1, d2 = tab[:, T_D1:T_D1 + 64], tab[:, T_D2:T_D2 + 64]
        ident, bmask = tab[:, T_ID:T_ID + P], tab[:, T_BM:T_BM + 16]
        scale, unscale = scl[:, 4:5], scl[:, 5:6]

        const_ld, zeroed, x_ld = sem("const_ld"), sem("zeroed"), sem("x_ld")
        sp_passed, pool_passed, pe_passed = sem("sp_passed"), sem("pool_passed"), sem("pe_passed")
        g_mm, g_ok, b_ok, qb_mm, qb_ok = (sem(n) for n in ("g_mm", "g_ok", "b_ok", "qb_mm", "qb_ok"))
        w_ld, rs_ld = ([sem(f"{n}{i}") for i in range(4)] for n in ("w_ld", "rs_ld"))
        w_neg, w2_mm, f_new, f_cp = (sem(n) for n in ("w_neg", "w2_mm", "f_new", "f_cp"))
        mix_mm, zc_ev, w1_mm, zo_ev, wts = (sem(n) for n in ("mix_mm", "zc_ev", "w1_mm", "zo_ev", "wts"))
        zo_peak = sem("zo_peak")
        peak_ok, row_mm, one_ok, all_mm, scale_ok = (sem(n) for n in (
            "peak_ok", "row_mm", "one_ok", "all_mm", "scale_ok"))
        z_st = [[sem(f"z_st{h}{i}") for i in range(4)] for h in range(2)]
        zt_ld, a_mm, a_hi, a_lo = (sem(n) for n in ("zt_ld", "a_mm", "a_hi", "a_lo"))
        u_st, ut_ld, b_mm = [sem("u_st0"), sem("u_st1")], [sem("ut_ld0"), sem("ut_ld1")], sem("b_mm")
        r_ok, rt_ok = ([sem(f"{n}{g}") for g in range(2)] for n in ("r_ok", "rt_ok"))
        q_mm, q_ad, y_mm, y_ev = (sem(n) for n in ("q_mm", "q_ad", "y_mm", "y_ev"))
        t_st = [sem(f"t_st{i}") for i in range(3)]
        tt_ld = [sem(f"tt_ld{i}") for i in range(TT)]
        x_mm, x_ev = sem("x_mm"), [sem("x_ev0"), sem("x_ev1")]
        r_st = [[sem(f"r_st{g}{i}") for i in range(2)] for g in range(2)]
        gs_ok = sem("gs_ok")
        q_act, q2_mm, h_ev, h_st = (sem(n) for n in ("q_act", "q2_mm", "h_ev", "h_st"))
        NCONST = 9 + 4 * 3

        z_d, u_d, t_d, r_d = (scratch[n] for n in ("z", "u", "t", "r"))

        def prime(eng, *sems):
            for s in sems:
                eng.sem_inc(s, 1)

        block = ctx.enter_context(nc.Block())

        def layers(eng, octets, spectral, epilogue):
            spectral(0, True)
            with eng.Fori(0, L - 1) as l:
                octets(l, True)
                spectral(l + 1, False)
            octets(L - 1, False)
            epilogue()

        def in_layer(eng, main):
            main(0, True, False)
            with eng.Fori(1, NOCT - 1) as n:
                main(n, True, True)
            main(NOCT - 1, False, True)

        def register(*values):
            return not all(isinstance(v, int) for v in values)

        def new_modes_store(eng, m, j, g, new_modes, passed):
            wait_alone(eng, x_ev[j % 2], m * 3 + j // 2 + 1, passed)
            dst = new_modes[:, :, 64 * (2 * j + g):64 * (2 * j + g) + 64].rearrange("o k b -> k o b")
            eng.dma_start(dst, rr[64 * g:64 * g + 48, j % 2, :].rearrange("p (o b) -> p o b", o=OCT)
                          ).then_inc(r_st[g][j % 2], 16)

        def z_store(eng, l, c, q, h, passed):
            wait_alone(eng, zo_ev, l * MODES + c + 1, passed)
            for ri in range(2):
                row = 64 * h + 32 * ri
                eng.dma_start(z_d[c + (KX * ri + MODES * h), :, :, :].rearrange("y o b -> o y b"),
                              zo[row:row + 32, q, :].rearrange("p (y b) -> p y b", b=B)).then_inc(z_st[h][q], 16)

        A_STEPS = MODES // 2
        T_PARTS = ((0, 8), (8, 12), (12, 16))
        X_STEPS = {14: (0,), 15: (1, 2), 16: (3, 4), 17: (5,)}

        @block.sync
        def _(sp):
            prime(sp, *u_st)

            def const(dst, src):
                sp.dma_start(dst, src).then_inc(const_ld, 16)

            const(tab[:, :], A["table"][:, 0:T_SEL])
            sp.dma_start(xs, A["xt"]).then_inc(x_ld, 16)
            const(q1t[:, :], A["q1t"])
            const(b1t[:, :], A["b1t"])
            const(b2t[:, :], A["b2t"])
            const(q1b[:, :], A["q1b"])
            const(q2c[:, :], A["q2c"])
            const(q2b[:, :], A["q2b"])
            const(wg[:, 1:1 + L, :], A["w2"].rearrange("l o i -> o l i"))
            sp.wait_ge(zeroed, 1)
            const(wg[:, 0, 0:OCT], A["pc"])
            for i in range(4):
                const(w1all[32 * i:32 * i + 32, :, 32 * i:32 * i + 32], A["w1t"].rearrange("l i o -> i l o"))
                const(w2all[32 * i:32 * i + 32, 1:L, 32 * i:32 * i + 32],
                      A["w2t"].rearrange("l i o -> i l o")[:, 0:L - 1, :])
                const(w2all[32 * i:32 * i + MID, 0, 32 * i:32 * i + 32], A["pt"])

            def t_store(m, n, part):
                k0, k1 = T_PARTS[part]
                wait_alone(sp, y_ev, m * XP + k1, sp_passed)
                for g in range(2):
                    for x2 in range(2):
                        row, x0 = 64 * g + 24 * x2, 4 * k0 + 2 * g + x2
                        dst = t_d[bass.ds(n * S + x0, k1 - k0, 4), :, :, :].rearrange("k r y n -> (r y) k n")
                        sp.dma_start(dst, half[row:row + 24, k0:k1, :]).then_inc(t_st[part], 16)

            def tt_load(m, n, j):
                if j == 0:
                    for stored in t_st:
                        wait_alone(sp, stored, m * 64 + 64, sp_passed)
                if j == TT or (j == 0 and (register(m) or m > 0)):
                    wait_alone(sp, x_mm, m * 6 + (1 if j == TT else 0), sp_passed)
                for ri in range(2):
                    sp.dma_start(tt[64 * ri:64 * ri + 64, j % TT, :, :],
                                 t_d[bass.ds(n * S, S), ri, 2 * j:2 * j + 2, :]).then_inc(tt_ld[j % TT], 16)

            for part in range(3):
                t_store(0, 0, part)
            sp.wait_ge(r_ok[0], XP)
            sp.wait_ge(r_ok[1], XP)
            for j in range(TT):
                tt_load(0, 0, j)
            for j in range(6):
                if j + TT < 6:
                    tt_load(0, 0, j + TT)
                new_modes_store(sp, 0, j, 1, r_d[0:OCT], sp_passed)

            def spectral(l, first):
                def w_load(c, q):
                    sp.dma_start(wch[:, q, :], A["fwt"][l, :, c, :]).then_inc(w_ld[q], 16)

                def rs_load(c, q):
                    for h in range(2):
                        for ri in range(2):
                            row, n = 64 * h + 32 * ri, (OCT if first else C)
                            src = r_d[0:n, KX * ri + MODES * h + c, :]
                            sp.dma_start(rs[row:row + n, q, :], src).then_inc(rs_ld[q], 16)

                def load(c, q, i):
                    if isinstance(c, int) and c < 4:
                        rs_load(c, q)
                    elif inside(c, 4, MODES):
                        wait_alone(sp, w2_mm, l * MODES + c - 3, sp_passed)
                        rs_load(c, q)
                        wait_alone(sp, mix_mm, l * MODES + c - 3, sp_passed)
                        w_load(c, q)
                    if inside(c, 4, MODES + 4):
                        z_store(sp, l, c - 4, q, 1, sp_passed)

                for c in range(4):
                    w_load(c, c)
                for s in r_st[0] + r_st[1]:
                    wait_alone(sp, s, 48 if first else l * (48 * NOCT) + 48, sp_passed)
                paced4(sp, 4, 12, MODES + 4, load)

            def octets(l, forward):
                def u_store(n, bt, src=None):
                    m = l * NOCT + n
                    wait_alone(sp, a_lo, m * MODES + 2 * bt + 2 + 1, sp_passed)
                    sp.dma_start(u_d[bass.ds(n * P, P), :, 2 * bt:2 * bt + 2, :],
                                 u[:, bt % 2, :, :, :] if src is None else src).then_inc(u_st[bt % 2], 16)

                def field_load(n, b, first):
                    m = l * NOCT + n
                    if b == 0:
                        for s in range(2):
                            wait_alone(sp, u_st[s], m * 48 + 48 + 1, sp_passed)
                    if not first:
                        wait_alone(sp, b_mm, m * (2 * XP) + (16 * b - 16 + 1), sp_passed)
                    for x2 in range(2):
                        for ri in range(2):
                            row, x0 = 48 * x2 + 24 * ri, n * P + S * ri + 32 * b + x2
                            src = u_d[bass.ds(x0, 16, 2), :, :, :].rearrange("x s y n -> (s y) x n")
                            dst = f16[row:row + 24, 8 * b:8 * b + 8, :, :].rearrange("p k g n -> p (k g) n")
                            sp.dma_start(dst, src).then_inc(ut_ld[b], 16)

                def main(n, more, after):
                    m = l * NOCT + n
                    back = after and forward
                    for bt in range(6):
                        if more:
                            u_store(n + 1, bt)
                        if after and bt == 0:
                            field_load(n, 1, False)
                    if back:
                        for j in range(TT):
                            tt_load(m, n - 1, j)
                    if more:
                        field_load(n + 1, 0, False)
                    if forward:
                        t_store(m + 1, n, 0)
                        t_store(m + 1, n, 1)
                    if back:
                        def r_store(j):
                            new_modes_store(sp, m, j, 1, r_d[bass.ds((n - 1) * OCT, OCT)], sp_passed)
                        tt_load(m, n - 1, TT)
                        for j in range(3):
                            r_store(j)
                    if back:
                        for j in range(3, 5):
                            r_store(j)
                    if forward:
                        t_store(m + 1, n, 2)
                    if back:
                        r_store(5)

                for bt in range(6):
                    u_store(0, bt, u_first[bt])
                wait_alone(sp, f_cp, l * MODES + MODES, sp_passed)
                for s in z_st[0] + z_st[1]:
                    wait_alone(sp, s, l * 96 + 96, sp_passed)
                for b in range(2):
                    field_load(0, b, True)
                in_layer(sp, main)
                if forward:
                    m = l * NOCT + NOCT
                    for j in range(TT):
                        tt_load(m, NOCT - 1, j)
                    for j in range(6):
                        if j + TT < 6:
                            tt_load(m, NOCT - 1, j + TT)
                        new_modes_store(sp, m, j, 1, r_d[C - OCT:C], sp_passed)

            def epilogue():
                sp.wait_ge(h_ev, XP)
                for b in range(4):
                    sp.dma_start(tokens_out[:, :, b, :].rearrange("c k (a y) -> a (c k) y", y=32),
                                 half[b:b + 29:4, :, :].rearrange("p k n -> p (k n)").rearrange(
                                     "p (m y) -> p m y", y=32)).then_inc(h_st, 16)
                sp.wait_ge(h_st, 16 * 4)

            layers(sp, octets, spectral, epilogue)

        @block.gpsimd
        def _(pool):
            g_ = nc.gpsimd
            g_.memset(w1all[:, :, :], 0.0)
            g_.memset(w2all[:, :, :], 0.0)
            g_.memset(wg[:, 0, :], 0.0).then_inc(zeroed, 1)
            g_.memset(b2all[:, :, :], 0.0)
            g_.memset(peak[:, :], 0.0)
            g_.memset(ones[:, :], 1.0)
            g_.memset(zt[:, :, :], 0.0)
            g_.memset(spec[:, 0:6, :], 0.0)
            g_.memset(spec[:, 6:12, :], 0.0).then_inc(zeroed, 1)

            for j in range(6):
                new_modes_store(pool, 0, j, 0, r_d[0:OCT], pool_passed)

            def spectral(l, first):
                def step(c, q, i):
                    z_store(pool, l, c, q, 0, pool_passed)
                paced4(pool, 4, 12, MODES, step)

            def octets(l, forward):
                for s in z_st[0] + z_st[1]:
                    wait_alone(pool, s, l * 96 + 96, pool_passed)
                with pool.Fori(0, NOCT) as n:
                    wait_alone(pool, a_mm, (l * NOCT + n) * MODES + 1, pool_passed)
                    src = z_d[:, :, bass.ds(n * OCT, OCT), :].rearrange("k (i g) o b -> g k i (o b)", g=2)
                    for g in range(2):
                        pool.dma_start(zt[64 * g:64 * g + 48, :, :], src[g]).then_inc(zt_ld, 16)
                    pool.dma_start(zt[48:49, 0, :], A["b1w"][bass.ds(l, 1), bass.ds(n * N, N)]).then_inc(zt_ld, 16)
                if forward:
                    with pool.Fori(0, NOCT) as n:
                        for j in range(6):
                            new_modes_store(pool, l * NOCT + 1 + n, j, 0, r_d[bass.ds(n * OCT, OCT)], pool_passed)

            layers(pool, octets, spectral, lambda: None)

        def forward_x_evac(on, m, j):
            eng = nc.scalar if on == 0 else nc.vector
            if j % 2 == on:
                eng.wait_ge(x_mm, m * 6 + j + 1)
                if register(m) or m > 0 or j >= 2:
                    for g in range(2):
                        eng.wait_ge(r_st[g][on], m * 48 + 16 * (j // 2))
                copy = nc.scalar.copy if on == 0 else nc.vector.tensor_copy
                copy(rr[:, on, :], ps_a[on]).then_inc(x_ev[on], 1)

        @block.scalar
        def _(act):
            prime(act, a_hi)

            def high_half(m, ky, q, to=None):
                act.wait_ge(a_mm, m * MODES + ky + 1 + 1)
                if to is None:
                    act.wait_ge(u_st[q // 2], m * 48 + ((ky - q) * 4 + 1))
                    to = u[:, q // 2, :, :, :]
                nc.scalar.activation(to[:, 0, q % 2, :], ps_a[q % 2], ACT.Copy, scale=scale).then_inc(a_hi, 1)

            def main(m, ob, forward, more, after):
                def step(k, q, i):
                    p = q % 2
                    if inside(k, 0, XP):
                        if register(m, k) or k >= 2:
                            act.wait_ge(rt_ok[0], m * XP + k - 1)
                            act.wait_ge(rt_ok[1], m * XP + k - 1)
                            if forward:
                                act.wait_ge(y_mm, m * XP + k - 1)
                        for g in range(2):
                            if ob is None:
                                rc = by_octet(r[:, p, g, :])
                                nc.scalar.copy(rc[:, 0], xs[:, bass.ds(k * 2 + g, 1), :].rearrange(
                                    "p x (c b) -> p (x c) b", b=4))
                                nc.scalar.activation(rc[:, 1], rc[:, 3], ACT.Copy,
                                                     scale=tab[:, bass.ds(k * 2 + (T_GX + g), 1)]).then_inc(r_ok[g], 1)
                            else:
                                act.wait_ge(b_mm, (ob * XP + k) * 2 + g + 1 + 1)
                                nc.scalar.activation(by_octet(r[:, p, g, :]), octets_of(ps_b[p][g]), ACT.Relu,
                                                     scale=unscale).then_inc(r_ok[g], 1)
                    if forward and inside(k, 1, XP + 1):
                        act.wait_ge(y_mm, m * XP + k)
                        if isinstance(k, int) and k in (1, 5) and (register(m) or m > 0):
                            for stored in (t_st[0:1] if k == 1 else t_st[1:]):
                                act.wait_ge(stored, m * 64)
                        nc.scalar.copy(octets_of(half[:, k - 1, :]), by_octet(ps_f)).then_inc(y_ev, 1)
                    if more and isinstance(k, int) and k < A_STEPS:
                        for ky in (2 * k, 2 * k + 1):
                            high_half(ob + 1, ky, ky % 4)
                    if after and isinstance(k, int):
                        for j in X_STEPS.get(k, ()):
                            forward_x_evac(0, m - 1, j)
                paced4(act, 6, 14, 18, step)

            act.wait_ge(const_ld, 16 * NCONST)
            act.wait_ge(x_ld, 16)
            act.wait_ge(zeroed, 3)
            main(0, None, True, False, False)
            for j in range(6):
                forward_x_evac(0, 0, j)

            def spectral(l, first):
                def step(c, q, i):
                    p = q % 2
                    if inside(c, 1, MODES + 1):
                        act.wait_ge(f_new, (l * MODES + c) * 2)
                        nc.scalar.copy(spec[:, c - 1, :], fst[:, 1 - p, :]).then_inc(f_cp, 1)
                        act.wait_ge(mix_mm, l * MODES + c)
                        if register(l, c) or c >= 3:
                            act.wait_ge(w1_mm, l * MODES + c - 2)
                        nc.scalar.copy(zc[:, 1 - p, :].rearrange("p (a n) -> p a n", a=2), ps_mix).then_inc(zc_ev, 1)
                    if inside(c, 0, MODES):
                        act.wait_ge(w_ld[q], l * 48 + ((c - q) * 4 + 16))
                        for h in range(2):
                            rows = wch[64 * h + 32:64 * h + 64, q, :].rearrange("p (m o) -> p m o", o=64)[:, :, 0:C]
                            nc.scalar.mul(rows, rows, -1.0).then_inc(w_neg, 1)
                paced4(act, 4, 12, 14, step)

            def octets(l, forward):
                act.wait_ge(scale_ok, l + 1)
                for ky in range(MODES):
                    high_half(l * NOCT, ky, ky % 4, u_first[ky // 2])
                in_layer(act, lambda n, more, after:
                         main(l * NOCT + n + 1, l * NOCT + n, forward, more, after and forward))
                if forward:
                    for j in range(6):
                        forward_x_evac(0, l * NOCT + NOCT, j)

            def epilogue():
                act.wait_ge(qb_ok, 1)
                act.wait_ge(q_ad, (1 + L * NOCT) * XP)

                def step(k, p, i):
                    nc.scalar.activation(qacc[:, k, :], qacc[:, k, :], ACT.Relu, bias=qb[:, 0:1]).then_inc(q_act, 1)
                paced(act, 0, 0, XP, XP, step)
            layers(act, octets, spectral, epilogue)

        @block.vector
        def _(dve):
            prime(dve, a_lo)
            v = nc.vector
            for p in range(2):
                for g in range(2):
                    rc = by_octet(r[:, p, g, :])
                    v.memset(r[:, p, g, :], 0.0).then_inc(b_ok, 1)
            dve.wait_ge(b_ok, 4)
            for p in range(2):
                for g in range(2):
                    last = v.memset(by_octet(r[:, p, g, :])[:, 3], 1.0)
            last.then_inc(b_ok, 1)
            dve.wait_ge(const_ld, 16 * NCONST)
            dve.wait_ge(zeroed, 2)
            dve.wait_ge(b_ok, 5)
            for p in range(2):
                for g in range(2):
                    rc = by_octet(r[:, p, g, :])
                    last = v.tensor_scalar(rc[:, 2], rc[:, 3], tab[:, T_GY:T_GY + 1], None, ALU.mult)
            last.then_inc(zeroed, 1)
            v.tensor_scalar(b2all[0:C, 1:L, 0], b2t[:, 0:L - 1], 64.0, None, ALU.mult)
            v.tensor_scalar(dbh[:, 0, :], tab[:, T_DB:T_DB + P], 1024.0, None, ALU.mult).then_inc(b_ok, 1)
            dve.wait_ge(b_ok, 6)
            v.scalar_tensor_tensor(out=dbh[:, 1, :], in0=tab[:, T_DB:T_DB + P], scalar=1024.0, in1=dbh[:, 0, :],
                                   op0=ALU.mult, op1=ALU.subtract)
            for i in range(1 + L * NOCT):
                cols = wg[:, 0, 0:OCT] if i == 0 else wg[:, 1 + (i - 1) // NOCT, (i - 1) % NOCT * OCT:(i - 1) % NOCT * OCT + OCT]
                v.tensor_copy(wrep[:, P * i:P * i + P].rearrange("p (a o b) -> p a o b", a=4, b=4),
                              cols[:, None, :, None].broadcast_to([C, 4, OCT, 4]))
            v.tensor_copy(q1rep.rearrange("p (a o b) -> p a o b", a=4, b=4),
                          q1t[:, None, :, None].broadcast_to([C, 4, MID, 4])).then_inc(b_ok, 1)
            for i in range(1 + L * NOCT):
                dve.wait_ge(g_mm, i + 1)
                gp = ps_b[0][i % 2][:, 0:MID]
                v.tensor_tensor(gall[:, i, :, :, :], gp[:, None, :, None].broadcast_to([P, 4, MID, 4]),
                                bmask.rearrange("p (a b) -> p a b", a=4)[:, :, None, :].broadcast_to([P, 4, MID, 4]),
                                ALU.mult).then_inc(g_ok, 1)
            v.tensor_scalar(q2m[:, :], tab[:, T_M32:T_M32 + 32], q2c[:, 0:1], None, ALU.mult).then_inc(b_ok, 1)
            dve.wait_ge(qb_mm, 1)
            v.tensor_reduce(qb[:, 1:2], ps_q[:, 0:L], AX.X, ALU.add).then_inc(b_ok, 1)
            dve.wait_ge(b_ok, 9)
            v.tensor_tensor(qb[:, 0:1], qb[:, 1:2], q1b[:, :], ALU.add).then_inc(qb_ok, 1)

            def low_half(m, ky, q, to=None):
                dve.wait_ge(a_hi, m * MODES + ky + 1 + 1)
                to = u[:, q // 2, :, :, :] if to is None else to
                v.scalar_tensor_tensor(out=to[:, 1, q % 2, :], in0=ps_a[q % 2], scalar=scale,
                                       in1=to[:, 0, q % 2, :], op0=ALU.mult, op1=ALU.subtract).then_inc(a_lo, 1)

            def main(m, ob, forward, more, after):
                if ob is None:
                    dve.wait_ge(g_ok, 1 + L * NOCT)
                    v.tensor_copy(gs[:, :], gall[:, 0, :, :, :].rearrange("p a o b -> p (a o b)")).then_inc(gs_ok, 1)
                else:
                    dve.wait_ge(q_mm, m * XP)
                    v.tensor_copy(gs[:, :], gall[:, bass.ds(m, 1), :, :, :].rearrange("p m a o b -> p (m a o b)")
                                  ).then_inc(gs_ok, 1)

                def step(k, q, i):
                    p = q % 2
                    if inside(k, 1, XP + 1):
                        for g in range(2):
                            dve.wait_ge(r_ok[g], m * XP + k)
                            if g == 0 and (register(m, k) or k >= 3):
                                dve.wait_ge(q_mm, m * XP + k - 2)
                            v.transpose(rt[:, 1 - p, g, :], r[:, 1 - p, g, :]).then_inc(rt_ok[g], 1)
                    if inside(k, 2, XP + 2):
                        dve.wait_ge(q_mm, m * XP + k - 1)
                        if ob is None:
                            v.tensor_copy(qacc[:, k - 2, :], ps_q).then_inc(q_ad, 1)
                        else:
                            v.tensor_tensor(qacc[:, k - 2, :], ps_q, qacc[:, k - 2, :], ALU.add).then_inc(q_ad, 1)
                    if more and isinstance(k, int) and k < A_STEPS:
                        for ky in (2 * k, 2 * k + 1):
                            low_half(ob + 1, ky, ky % 4)
                    if after and isinstance(k, int):
                        for j in X_STEPS.get(k, ()):
                            forward_x_evac(1, m - 1, j)
                paced4(dve, 6, 14, 18, step)

            main(0, None, True, False, False)
            for j in range(6):
                forward_x_evac(1, 0, j)

            def scale_of_layer(l):
                done = [0]

                def then(ins):
                    done[0] += 1
                    ins.then_inc(peak_ok, 1)
                    dve.wait_ge(peak_ok, l * 7 + done[0])

                then(v.tensor_reduce(peak[0:C, MODES:], b1t[:, bass.ds(l, 1)], AX.X, ALU.max, apply_absolute_value=True))
                then(v.tensor_reduce(scl[:, 0:1], peak[:, :], AX.X, ALU.max))
                dve.wait_ge(row_mm, l + 1)
                v.tensor_reduce(scl[0:1, 1:2], ps_a[0][0:1, 0:P], AX.X, ALU.max).then_inc(one_ok, 1)
                dve.wait_ge(all_mm, l + 1)
                then(v.tensor_scalar(scl[:, 2:3], ps_a[1][:, 0:1], 16.0, 2.0 ** -60, ALU.mult, ALU.max))
                then(v.tensor_scalar(scl[:, 3:4].bitcast(mybir.dt.int32), scl[:, 2:3].bitcast(mybir.dt.int32),
                                     0x7F800000, None, ALU.bitwise_and))
                then(v.reciprocal(scl[:, 6:7], scl[:, 3:4]))
                then(v.tensor_scalar(unscale, scl[:, 3:4], 2.0 ** -24, None, ALU.mult))
                then(v.tensor_scalar(scale, scl[:, 6:7], 2.0 ** 14, None, ALU.mult))
                dve.sem_inc(scale_ok, 1)

            def spectral(l, first):
                if not first:
                    dve.wait_ge(w1_mm, l * MODES)
                v.tensor_copy(w1s[:, :], w1all[:, bass.ds(l, 1), :].rearrange("p l o -> p (l o)")).then_inc(wts, 1)
                v.tensor_copy(w2s[:, :], w2all[:, bass.ds(l, 1), :].rearrange("p l o -> p (l o)")).then_inc(wts, 1)

                def step(c, q, i):
                    p = q % 2
                    if inside(c, 0, MODES):
                        dve.wait_ge(w2_mm, l * MODES + c + 1)
                        if register(l, c) or c >= 2:
                            dve.wait_ge(mix_mm, l * MODES + c - 1)
                            dve.wait_ge(f_cp, l * MODES + c - 1)
                        v.tensor_tensor(fst[:, p, :].rearrange("p (a n) -> p a n", a=2), ps_w2,
                                        spec[:, c, :].rearrange("p (a n) -> p a n", a=2), ALU.add).then_inc(f_new, 1)
                        dve.wait_ge(f_new, (l * MODES + c) * 2 + 1)
                        v.tensor_scalar(fst[:, p, 0:B], fst[:, p, 0:B],
                                        b2all[:, bass.ds(l, 1), bass.ds(c, 1)].rearrange("p l c -> p (l c)"),
                                        None, ALU.add).then_inc(f_new, 1)
                    if inside(c, 2, MODES + 2):
                        dve.wait_ge(w1_mm, l * MODES + c - 1)
                        q2 = (q - 2) % 4
                        if register(l, c) or c >= 6:
                            for h in range(2):
                                dve.wait_ge(z_st[h][q2], l * 96 + (c - 2 - q2) * 8)
                        v.tensor_copy(zo[:, q2, :].rearrange("p (a n) -> p a n", a=2), ps_w1).then_inc(zo_ev, 1)
                        dve.wait_ge(zo_ev, l * MODES + c - 1)
                        v.tensor_reduce(peak[:, bass.ds(c - 2, 1)], zo[:, q2, :], AX.X, ALU.max,
                                        apply_absolute_value=True).then_inc(zo_peak, 1)
                paced4(dve, 4, 12, 14, step)
                dve.wait_ge(zo_peak, l * MODES + MODES)
                scale_of_layer(l)

            def octets(l, forward):
                for ky in range(MODES):
                    low_half(l * NOCT, ky, ky % 4, u_first[ky // 2])
                in_layer(dve, lambda n, more, after:
                         main(l * NOCT + n + 1, l * NOCT + n, forward, more, after and forward))
                if forward:
                    for j in range(6):
                        forward_x_evac(1, l * NOCT + NOCT, j)

            def epilogue():
                def step(k, p, i):
                    dve.wait_ge(q2_mm, k + 1)
                    dst = half[0:32, :, :].rearrange("p k n -> p (k n)").rearrange("p (c k y) -> p k c y", c=16, k=XP)
                    v.tensor_scalar(dst[:, bass.ds(k, 1), :, :].rearrange("p k c y -> p (k c) y"),
                                    ps_a[p][0:32, :].rearrange("p (c y) -> p c y", c=16),
                                    q2b[:, 0:1], None, ALU.add).then_inc(h_ev, 1)
                paced(dve, 0, 0, XP, XP, step)
            layers(dve, octets, spectral, epilogue)

        @block.tensor
        def _(pe):
            prime(pe, a_mm, b_mm)
            mm = nc.tensor.matmul
            pe.wait_ge(const_ld, 16 * NCONST)
            pe.wait_ge(b_ok, 7)
            for i in range(1 + L * NOCT):
                if i >= 2:
                    pe.wait_ge(g_ok, i - 1)
                mm(ps_b[0][i % 2][:, 0:MID], wrep[:, P * i:P * i + P], q1t[:, :], start=True, stop=True).then_inc(g_mm, 1)
            for g in range(2):
                last = mm(ps_q[64 * g:64 * g + 64, 0:L], q1rep, b2t[:, :], start=True, stop=True)
            last.then_inc(qb_mm, 1)
            pe.wait_ge(qb_ok, 1)
            pe.wait_ge(zeroed, 3)

            def stage_a(m, ky):
                pe.wait_ge(a_lo, (m * MODES + ky - 1 if ky >= 2 else m * MODES) + 1)
                mm(ps_a[ky % 2], ea(ky % 2), zt[:, ky // 2, :], start=True, stop=True).then_inc(a_mm, 1)

            def forward_x(m, j, adone):
                if j < 2 and (register(adone) or adone > 0):
                    pe.wait_ge(a_lo, adone * MODES + j)
                pe.wait_ge(tt_ld[j % TT], m * (64 if j % TT == 0 else 32) + 32 * (j // TT) + 32)
                if register(m) or m > 0 or j >= 2:
                    pe.wait_ge(x_ev[j % 2], m * 3 + j // 2)
                for g in range(2):
                    last = mm(ps_a[j % 2][64 * g:64 * g + 64, :], d2, tt[:, j % TT, g, :], start=True, stop=True)
                last.then_inc(x_mm, 1)

            def main(m, ob, forward, more, after, first=True):
                def step(k, q, i):
                    p = q % 2
                    if ob is not None and inside(k, 0, XP):
                        if isinstance(k, int) and k in (0, 5):
                            pe.wait_ge(ut_ld[k // 5], ob * 64 + 64)
                        for g in range(2):
                            if not isinstance(k, int) or k >= 2:
                                pe.wait_ge(r_ok[g], m * XP + k - 1)
                            else:
                                pe.wait_ge(r_ok[g], m * XP)
                            rhs = f16[0:96, bass.ds(k, 1), g, :].rearrange("p k n -> p (k n)")
                            for s in range(2):
                                last = mm(ps_b[p][g], dbh[0:96, s, :], rhs, start=(s == 0), stop=(s == 1))
                            last.then_inc(b_mm, 1)
                    if forward and inside(k, 1, XP + 1):
                        if register(m, k) or k >= 2:
                            pe.wait_ge(y_ev, m * XP + k - 1)
                        for g in range(2):
                            pe.wait_ge(r_ok[g], m * XP + k)
                            last = mm(ps_f[64 * g:64 * g + 64, :], d1, r[:, 1 - p, g, :], start=True, stop=True)
                        last.then_inc(y_mm, 1)
                    if inside(k, 2, XP + 2):
                        if isinstance(k, int) and k == 2:
                            pe.wait_ge(gs_ok, m + 1)
                        if register(m, k) or k >= 3:
                            pe.wait_ge(q_ad, m * XP + k - 2)
                        for g in range(2):
                            pe.wait_ge(rt_ok[g], m * XP + k - 1)
                            last = mm(ps_q[64 * g:64 * g + 64, :], gs[:, :], rt[:, p, g, :], start=True, stop=True)
                        last.then_inc(q_mm, 1)
                    if more and isinstance(k, int) and k < A_STEPS:
                        if k == 0:
                            start_a(ob + 1, gdone_last if not forward else m if first else m - 1)
                        for ky in (2 * k, 2 * k + 1):
                            stage_a(ob + 1, ky)
                    if after and isinstance(k, int):
                        for j in X_STEPS.get(k, ()):
                            forward_x(m - 1, j, ob + 2 if more else ob + 1)
                paced4(pe, 6, 14, 18, step)

            gdone_last = (L - 1) * NOCT + 1

            def start_a(m, gdone):
                pe.wait_ge(zt_ld, m * (16 * 3) + 16 * 3)
                for par in range(2):
                    pe.wait_ge(x_ev[par], gdone * 3)

            main(0, None, True, False, False)
            for j in range(6):
                forward_x(0, j, 0)

            def spectral(l, first):
                pe.wait_ge(wts, l * 2 + 2)
                m = l * NOCT + 1
                for g in range(2):
                    pe.wait_ge(r_ok[g], m * XP)
                pe.wait_ge(q_ad, m * XP)
                pe.wait_ge(y_ev, m * XP)

                def step(c, q, i):
                    p = q % 2
                    if inside(c, 0, MODES):
                        pe.wait_ge(rs_ld[q], l * 192 + ((c - q) * 16 + 64))
                        if register(l, c) or c >= 1:
                            pe.wait_ge(f_new, (l * MODES + c) * 2)
                        for a in range(2):
                            last = mm(ps_w2[:, a, :], w2s[:, :], rs[:, q, HC * a:HC * a + HC], start=True, stop=True)
                        last.then_inc(w2_mm, 1)
                    if inside(c, 1, MODES + 1):
                        pe.wait_ge(w_neg, (l * MODES + c) * 2)
                        pe.wait_ge(f_new, (l * MODES + c) * 2)
                        if register(l, c) or c >= 2:
                            pe.wait_ge(zc_ev, l * MODES + c - 1)
                        pe.sem_inc(pe_passed, 1)
                        for ky in range(MODES):
                            for h in range(2):
                                rows = slice(64 * h, 64 * h + 64)
                                last = mm(ps_mix[rows, ky // 6, B * (ky % 6):B * (ky % 6) + B],
                                          wch[rows, (q - 1) % 4, 64 * ky:64 * ky + 64], fst[rows, 1 - p, B * ky:B * ky + B],
                                          start=True, stop=True)
                        last.then_inc(mix_mm, 1)
                    if inside(c, 2, MODES + 2):
                        pe.wait_ge(zc_ev, l * MODES + c - 1)
                        if register(l, c) or c >= 3:
                            pe.wait_ge(zo_ev, l * MODES + c - 2)
                        for a in range(2):
                            last = mm(ps_w1[:, a, :], w1s[:, :], zc[:, p, HC * a:HC * a + HC], start=True, stop=True)
                        last.then_inc(w1_mm, 1)
                paced4(pe, 4, 12, 14, step)
                pe.wait_ge(peak_ok, l * 7 + 2)
                nc.tensor.transpose(ps_a[0][0:1, 0:P], scl[:, 0:1], ident).then_inc(row_mm, 1)
                pe.wait_ge(one_ok, l + 1)
                mm(ps_a[1][:, 0:1], ones[:, :], scl[0:1, 1:2], start=True, stop=True).then_inc(all_mm, 1)

            def octets(l, forward):
                pe.wait_ge(f_new, l * (2 * MODES) + 2 * MODES)
                pe.wait_ge(zc_ev, l * MODES + MODES)
                pe.wait_ge(zo_ev, l * MODES + MODES)
                pe.wait_ge(scale_ok, l + 1)
                start_a(l * NOCT, l * NOCT + 1)
                for ky in range(MODES):
                    stage_a(l * NOCT, ky)
                in_layer(pe, lambda n, more, after:
                         main(l * NOCT + n + 1, l * NOCT + n, forward, more, after and forward, not after))
                if forward:
                    for j in range(6):
                        forward_x(l * NOCT + NOCT, j, l * NOCT + NOCT)

            def epilogue():
                def step(k, p, i):
                    if not isinstance(k, int) or k >= 2:
                        pe.wait_ge(h_ev, k - 1)
                    pe.wait_ge(q_act, k + 1)
                    mm(ps_a[p][0:32, :], q2m[:, :], qacc[:, k, :], start=True, stop=True).then_inc(q2_mm, 1)
                paced(pe, 0, 2, XP, XP, step)
            layers(pe, octets, spectral, epilogue)


def token_stage(nc, A, h_d, out):
    with ExitStack() as ctx:
        def sb(name, shape, dt=F32):
            return ctx.enter_context(nc.sbuf_tensor(name, shape, dt))

        def sem(name):
            return ctx.enter_context(nc.semaphore(name))

        NG = NT // 4
        NC = NT // 8
        SCALE = 256.0
        WSCALE = 1024.0
        tok = sb("tok", [P, NT, D])
        f = sb("f", [P, NT, D])
        att = sb("att", [P, NT, D])
        tmp = sb("tmp", [P, NT, D])
        z = att
        fhl = sb("fhl", [P, 3, NT, 2, D], F16)
        x = sb("x", [P, 3, NT * P], F16)
        zt = fhl[:, 0, :, :, :].rearrange("p t c d -> p (t c d)").bitcast(F32)
        fj = sb("fj", [P, 2, D])
        e = sb("e", [P, 2, 1024])
        ot = sb("ot", [P, 512])
        rs = sb("rsum", [P, NT, NC])
        st = sb("st", [P, 8, NT])
        idt = sb("idt", [P, P])
        idh = sb("idh", [P, P], F16)
        self32 = sb("self32", [P, E * P])
        sel = sb("sel", [P, E * P], F16)
        w1 = sb("w1", [P, 2, E, HID])
        w2 = sb("w2", [P, E, D])
        wgt = sb("wgt", [P, 2 * E])
        b1 = sb("b1", [P, E])
        b2 = sb("b2", [P, 2, P])
        bgb = sb("bgb", [P, 2, E])
        lg = sb("lg", [P, NT, E])
        cw = sb("cw", [P, NT, E])
        pick = sb("pick", [P, 2, NT, E])
        wt32 = sb("wt32", [P, NT * P])
        wth = sb("wth", [P, NT * P], F16)
        hb = e[:, :, :].rearrange("p a (b n) -> p a b n", b=2)
        hw = sb("hw", [P, 2, 2, 512])
        ps = ctx.enter_context(nc.psum_tensor("ps_tok", [P, 8, 512], F32))

        ld, small, chain, rooted = sem("ld"), sem("small"), sem("chain"), sem("rooted")
        sp_passed = sem("sp_passed_tok")
        to_root, root_ok = sem("to_root"), sem("root_ok")
        idh_ok, split_ok = sem("idh_ok"), sem("split_ok")
        p_mm, p_ev = sem("p_mm"), [sem("p_ev0"), sem("p_ev1")]
        s_mm, exp_ok, fj_ok, pv_mm = (sem(n) for n in ("s_mm", "exp_ok", "fj_ok", "pv_mm"))
        ot_ok, ot_mm, att_ok = (sem(n) for n in ("ot_ok", "ot_mm", "att_ok"))
        z_ok, zt_mm, zt_ok, lg_mm, cw_ok, wt_mm, wt_ok = (sem(n) for n in (
            "z_ok", "zt_mm", "zt_ok", "lg_mm", "cw_ok", "wt_mm", "wt_ok"))
        h_mm, h_ok, wb_mm, hw_ok, y_mm, y_ok, yt_mm, o_ok, o_st = (sem(n) for n in (
            "th_mm", "th_ok", "wb_mm", "hw_ok", "ty_mm", "ty_ok", "yt_mm", "o_ok", "o_st"))
        N_LD, N_SMALL = 10, 11

        def prime(eng, *sems):
            for s in sems:
                eng.sem_inc(s, 1)

        block = ctx.enter_context(nc.Block())

        @block.sync
        def _(sp):
            tv = A["txt"].rearrange("b s d -> b (s d)")
            tf = tok[:, :, :].rearrange("p t d -> p (t d)")
            for b in range(4):
                sp.dma_start(tf[2 * b:2 * b + 121:8, :], h_d[:, 0:12, b, :]).then_inc(ld, 16)
                sp.dma_start(tf[2 * b + 1:2 * b + 122:8, 0:16 * D], h_d[:, 12:16, b, :]).then_inc(ld, 16)
            sp.dma_start(tf[1:P:2, 16 * D:], tv).then_inc(ld, 16)
            sp.dma_start(idt[:, :], A["table"][:, T_ID:T_ID + P]).then_inc(ld, 16)
            sp.wait_ge(rooted, 1)
            for dst, src in (
                    (self32[:, :], A["table"][:, T_SEL:T_END]),
                    (w1[0:64, 0, :, :], A["ew1"].rearrange("e c h -> c e h")),
                    (w1[64:P, 1, :, :], A["ew1"].rearrange("e c h -> c e h")),
                    (w2[:, :, :], A["ew2"].rearrange("e h c -> h e c")),
                    (wgt[0:64, 0:E], A["wg"]), (wgt[64:P, E:], A["wg"]),
                    (b1[:, :], A["eb1"]), (b2[0:E, 0, 0:D], A["eb2"]), (b2[0:E, 1, D:], A["eb2"]),
                    (bgb[:, 0, :], A["bg"]), (bgb[:, 1, :], A["bias"])):
                sp.dma_start(dst, src).then_inc(small, 16)
            ov = out.rearrange("b (r t) d -> (b r) (t d)", r=2)
            with sp.Fori(0, NC) as q:
                wait_alone(sp, o_ok, q + 1 + 1, sp_passed)
                sp.dma_start(ov[:, bass.ds(q * 8 * D, 8 * D)], tok[:, bass.ds(q * 8, 8), :].rearrange("p t d -> p (t d)")
                             ).then_inc(o_st, 16)
            sp.wait_ge(o_st, 16 * NC)

        @block.gpsimd
        def _(pool):
            g = nc.gpsimd
            g.memset(w1[:, :, :, :], 0.0)
            g.memset(wgt[:, :], 0.0)
            g.memset(b2[:, :, :], 0.0)
            g.memset(wt32[:, :], 0.0)
            g.memset(wth[:, :], 0.0).then_inc(rooted, 1)

        def wide(col, n=D):
            return col[:, :, None].broadcast_to([P, NT, n])

        @block.vector
        def _(dve):
            prime(dve, ot_ok, att_ok, hw_ok, y_ok, o_ok, p_ev[1])
            v = nc.vector
            done = [0]

            def then(ins):
                done[0] += 1
                ins.then_inc(chain, 1)
                dve.wait_ge(chain, done[0])

            n_root = [0]

            def center(src, dst):
                then(v.tensor_reduce(st[:, 0, :], src[:, :, :], AX.X, ALU.add))
                then(v.tensor_scalar(st[:, 0, :], st[:, 0, :], 1.0 / D, None, ALU.mult))
                then(v.tensor_tensor(dst[:, :, :], src[:, :, :], wide(st[:, 0, :]), ALU.subtract))
                then(v.tensor_tensor(tmp[:, :, :], dst[:, :, :], dst[:, :, :], ALU.mult))
                then(v.tensor_reduce(st[:, 1, :], tmp[:, :, :], AX.X, ALU.add))
                v.tensor_scalar(st[:, 2, :], st[:, 1, :], 1.0 / D, 1e-5, ALU.mult, ALU.add).then_inc(to_root, 1)
                n_root[0] += 1
                dve.wait_ge(root_ok, n_root[0])
                then(v.reciprocal(st[:, 3, :], st[:, 2, :]))

            dve.wait_ge(ld, 16 * N_LD)
            v.tensor_copy(idh[:, :], idt[:, :]).then_inc(idh_ok, 1)
            center(tok, f)
            then(v.tensor_tensor(st[:, 4, :], st[:, 1, :], st[:, 3, :], ALU.mult))
            then(v.tensor_scalar(st[:, 4, :], st[:, 4, :], 1e-12, None, ALU.max))
            then(v.reciprocal(st[:, 5, :], st[:, 4, :]))
            then(v.tensor_tensor(st[:, 4, :], st[:, 5, :], st[:, 3, :], ALU.mult))
            then(v.tensor_tensor(f[:, :, :], f[:, :, :], wide(st[:, 4, :]), ALU.mult))
            then(v.tensor_scalar(fhl[:, 0, :, 0, :], f[:, :, :], SCALE, None, ALU.mult))
            then(v.scalar_tensor_tensor(out=fhl[:, 0, :, 1, :], in0=f[:, :, :], scalar=SCALE, in1=fhl[:, 0, :, 0, :],
                                        op0=ALU.mult, op1=ALU.subtract))
            for c in range(2):
                v.tensor_copy(fhl[:, 1, :, c, :], fhl[:, 0, :, 0, :])
                last = v.tensor_copy(fhl[:, 2, :, c, :], fhl[:, 0, :, 1, :])
            last.then_inc(split_ok, 1)

            with dve.Fori(0, NG // 2) as i:
                dve.wait_ge(p_mm, i * 2 + 2)
                v.tensor_copy(x[:, :, bass.ds(i * 1024 + 512, 512)], ps[:, 3:6, :]).then_inc(p_ev[1], 1)

            with dve.Fori(0, NC) as ci:
                def step(j, p, i):
                    if not (isinstance(j, int) and j < 2):
                        dve.wait_ge(pv_mm, ci * NT + j - 1)
                    else:
                        dve.wait_ge(att_ok, ci + 1)
                    v.tensor_copy(fj[:, p, :], f[:, bass.ds(j, 1), :].rearrange("p t d -> p (t d)")
                                  ).then_inc(fj_ok, 1)
                paced(dve, 0, 2, NT, NT, step)
                dve.wait_ge(pv_mm, ci * NT + NT)
                v.tensor_copy(ot[:, :], ps[:, 4, :]).then_inc(ot_ok, 1)
                dve.wait_ge(ot_mm, ci + 1)
                v.tensor_copy(att[:, bass.ds(ci * 8, 8), :].rearrange("p (h s) d -> p s h d", h=2),
                              ps[:, 5, :].rearrange("p (s h d) -> p s h d", s=4, h=2)).then_inc(att_ok, 1)

            dve.wait_ge(exp_ok, NC * NT + 1)
            dve.wait_ge(att_ok, NC + 1)
            then(v.tensor_reduce(st[:, 4, :], rs[:, :, :], AX.X, ALU.add))
            then(v.reciprocal(st[:, 5, :], st[:, 4, :]))
            then(v.tensor_scalar(st[:, 5, :], st[:, 5, :], 1.0 - 0.8, None, ALU.mult))
            then(v.tensor_tensor(att[:, :, :], att[:, :, :], wide(st[:, 5, :]), ALU.mult))
            then(v.scalar_tensor_tensor(out=att[:, :, :], in0=f[:, :, :], scalar=0.8, in1=att[:, :, :],
                                        op0=ALU.mult, op1=ALU.add))
            then(v.tensor_tensor(tmp[:, :, :], att[:, :, :], att[:, :, :], ALU.mult))
            v.tensor_reduce(st[:, 1, :], tmp[:, :, :], AX.X, ALU.add).then_inc(to_root, 1)
            n_root[0] += 1
            dve.wait_ge(root_ok, n_root[0])
            then(v.tensor_scalar(st[:, 4, :], st[:, 1, :], 1e-12, None, ALU.max))
            then(v.reciprocal(st[:, 5, :], st[:, 4, :]))
            then(v.tensor_tensor(att[:, :, :], att[:, :, :], wide(st[:, 5, :]), ALU.mult))
            then(v.tensor_tensor(tok[:, :, :], tok[:, :, :], att[:, :, :], ALU.add))
            center(tok, z)
            v.tensor_tensor(z[:, :, :], z[:, :, :], wide(st[:, 3, :]), ALU.mult).then_inc(z_ok, 1)

            for i in range(NC):
                dve.wait_ge(zt_mm, i + 1)
                v.tensor_copy(zt[:, 512 * i:512 * i + 512], ps[:, i % 2, :]).then_inc(zt_ok, 1)
            dve.wait_ge(small, 16 * N_SMALL)
            then(v.tensor_tensor(bgb[:, 0, :], bgb[:, 0, :], bgb[:, 1, :], ALU.add))
            dve.wait_ge(lg_mm, 1)
            then(v.tensor_tensor(lg[:, :, :], ps[:, 2, 0:NT * E].rearrange("p (t e) -> p t e", e=E),
                                 bgb[:, 0:1, :].broadcast_to([P, NT, E]), ALU.add))
            for n in range(2):
                top = st[:, 4 + n, :]
                then(v.tensor_reduce(top, lg[:, :, :], AX.X, ALU.max))
                then(v.tensor_tensor(pick[:, n, :, :], lg[:, :, :], wide(top, E), ALU.is_equal))
                then(v.memset(st[:, 6, :], 1.0))
                for i in range(E):
                    then(v.tensor_tensor(pick[:, n, :, i], pick[:, n, :, i], st[:, 6, :], ALU.mult))
                    then(v.tensor_tensor(st[:, 6, :], st[:, 6, :], pick[:, n, :, i], ALU.subtract))
                if n == 0:
                    then(v.scalar_tensor_tensor(out=lg[:, :, :], in0=pick[:, 0, :, :], scalar=-3e38,
                                                in1=lg[:, :, :], op0=ALU.mult, op1=ALU.add))
            v.tensor_tensor(st[:, 6, :], st[:, 5, :], st[:, 4, :], ALU.subtract).then_inc(to_root, 1)
            n_root[0] += 1
            dve.wait_ge(root_ok, n_root[0])
            then(v.tensor_scalar(st[:, 0, :], st[:, 6, :], 1.0, None, ALU.add))
            then(v.reciprocal(st[:, 1, :], st[:, 0, :]))
            then(v.tensor_tensor(st[:, 2, :], st[:, 1, :], st[:, 6, :], ALU.mult))
            then(v.tensor_tensor(cw[:, :, :], pick[:, 0, :, :], wide(st[:, 1, :], E), ALU.mult))
            then(v.tensor_tensor(lg[:, :, :], pick[:, 1, :, :], wide(st[:, 2, :], E), ALU.mult))
            v.tensor_tensor(cw[:, :, :], cw[:, :, :], lg[:, :, :], ALU.add).then_inc(cw_ok, 1)
            v.tensor_copy(sel[:, :], self32[:, :]).then_inc(cw_ok, 1)
            dve.wait_ge(rooted, 1)
            for i in range(NG):
                dve.wait_ge(wt_mm, i + 1)
                cols = slice(512 * i, 512 * i + 512)
                src = ps[0:E, 3 + i % 2, :]
                v.tensor_copy(wt32[0:E, cols], src)
                then(v.tensor_scalar(wth[0:E, cols], src, WSCALE, None, ALU.mult))
                v.scalar_tensor_tensor(out=wth[32:32 + E, cols], in0=src, scalar=WSCALE, in1=wth[0:E, cols],
                                       op0=ALU.mult, op1=ALU.subtract).then_inc(wt_ok, 1)

            with dve.Fori(0, NC) as q:
                for i in range(E):
                    for par in range(2):
                        dve.wait_ge(wb_mm, q * (2 * E) + (2 * i + par + 1))
                        dve.wait_ge(h_ok, q * (2 * E) + (2 * i + par + 1) + 1)
                        if i >= 2:
                            dve.wait_ge(y_mm, q * E + (i - 1))
                        v.tensor_tensor(hw[:, i % 2, par, :], ps[:, 4 + par, :], hb[:, i % 2, par, :], ALU.mult
                                        ).then_inc(hw_ok, 1)
                dve.wait_ge(y_mm, q * E + E)
                v.tensor_copy(ot[:, :], ps[:, 6, :]).then_inc(y_ok, 1)
                dve.wait_ge(yt_mm, q + 1)
                chunk = tok[:, bass.ds(q * 8, 8), :].rearrange("p t d -> p (t d)")
                v.tensor_tensor(chunk, ps[:, 7, :], chunk, ALU.add).then_inc(o_ok, 1)

        @block.scalar
        def _(act):
            prime(act, exp_ok, h_ok, p_ev[0])
            def root(n, cols):
                act.wait_ge(to_root, n)
                nc.scalar.activation(st[:, cols, :], st[:, cols, :], ACT.Sqrt).then_inc(root_ok, 1)

            root(1, slice(1, 3))
            with act.Fori(0, NG // 2) as i:
                act.wait_ge(p_mm, i * 2 + 1)
                nc.scalar.copy(x[:, :, bass.ds(i * 1024, 512)], ps[:, 0:3, :]).then_inc(p_ev[0], 1)

            with act.Fori(0, NC) as ci:
                def step(j, p, i):
                    act.wait_ge(s_mm, ci * NT + j + 1)
                    if not (isinstance(j, int) and j < 2):
                        act.wait_ge(pv_mm, ci * NT + j - 1)
                    else:
                        act.wait_ge(ot_ok, ci + 1)
                    nc.scalar.activation(e[:, p, :], ps[:, 2 * p:2 * p + 2, :].rearrange("p a n -> p (a n)"), ACT.Exp,
                                         scale=1.0 / (SCALE * SCALE),
                                         accum_out=rs[:, bass.ds(j, 1), bass.ds(ci, 1)].rearrange("p t c -> p (t c)")
                                         ).then_inc(exp_ok, 1)
                paced(act, 0, 2, NT, NT, step)
            root(2, slice(1, 2))
            root(3, slice(1, 3))
            act.wait_ge(to_root, 4)
            nc.scalar.activation(st[:, 6, :], st[:, 6, :], ACT.Exp).then_inc(root_ok, 1)
            act.wait_ge(small, 16 * N_SMALL)
            with act.Fori(0, NC) as q:
                for i in range(E):
                    for par in range(2):
                        act.wait_ge(h_mm, q * (2 * E) + (2 * i + par + 1))
                        if i >= 2:
                            act.wait_ge(hw_ok, q * (2 * E) + (2 * i + par - 3) + 1)
                        else:
                            act.wait_ge(hw_ok, q * (2 * E) + 1)
                        nc.scalar.activation(hb[:, i % 2, par, :], ps[:, 2 * (i % 2) + par, :], ACT.Relu,
                                             bias=b1[:, i:i + 1]).then_inc(h_ok, 1)

        @block.tensor
        def _(pe):
            mm = nc.tensor.matmul
            pe.wait_ge(idh_ok, 1)
            pe.wait_ge(split_ok, 1)
            with pe.Fori(0, NG // 2) as i:
                for p in range(2):
                    pe.wait_ge(p_ev[p], i + 1)
                    for kind in range(3):
                        for t in range(4):
                            src = fhl[:, kind, bass.ds(i * 8 + (4 * p + t), 1), :, :].rearrange("p t c d -> p (t c d)")
                            last = mm(ps[:, 3 * p + kind, P * t:P * t + P], src, idh[:, :], start=True, stop=True)
                    last.then_inc(p_mm, 1)
            for p in range(2):
                pe.wait_ge(p_ev[p], NG // 2 + 1)

            with pe.Fori(0, NC) as ci:
                def step(j, p, i):
                    if inside(j, 0, NT):
                        if not (isinstance(j, int) and j < 2):
                            pe.wait_ge(exp_ok, ci * NT + j - 1 + 1)
                        else:
                            pe.wait_ge(exp_ok, ci * NT + 1)
                        for h in range(2):
                            for kind in range(2):
                                last = mm(ps[:, 2 * p + h, :], x[:, 1 + kind, bass.ds(j * P, P)],
                                          x[:, 0, bass.ds(ci * 1024 + 512 * h, 512)], start=(kind == 0), stop=(kind == 1))
                        last.then_inc(s_mm, 1)
                    if inside(j, 1, NT + 1):
                        pe.wait_ge(exp_ok, ci * NT + j + 1)
                        pe.wait_ge(fj_ok, ci * NT + j)
                        if isinstance(j, int) and j == 1:
                            pe.wait_ge(ot_ok, ci + 1)
                        q = 1 - p
                        for h in range(2):
                            last = mm(ps[64 * h:64 * h + 64, 4, :], fj[:, q, :], e[:, q, 512 * h:512 * h + 512],
                                      start=isinstance(j, int) and j == 1, stop=isinstance(j, int) and j == NT)
                        last.then_inc(pv_mm, 1)
                paced(pe, 0, 2, NT, NT + 1, step)
                pe.wait_ge(ot_ok, ci + 1 + 1)
                pe.wait_ge(att_ok, ci + 1)
                for s in range(4):
                    last = nc.tensor.transpose(ps[:, 5, P * s:P * s + P], ot[:, P * s:P * s + P], idt[:, :])
                last.then_inc(ot_mm, 1)

            pe.wait_ge(z_ok, 1)
            for i in range(NC):
                if i >= 2:
                    pe.wait_ge(zt_ok, i - 1)
                for s in range(4):
                    t = 8 * i + 2 * s
                    src = z[:, t:t + 2, :].rearrange("p t d -> p (t d)")
                    last = nc.tensor.transpose(ps[:, i % 2, P * s:P * s + P], src, idt[:, :])
                last.then_inc(zt_mm, 1)
            pe.wait_ge(small, 16 * N_SMALL)
            pe.wait_ge(zt_ok, NC)
            for i in range(NT // 2):
                last = mm(ps[:, 2, 2 * E * i:2 * E * i + 2 * E], zt[:, P * i:P * i + P], wgt[:, :], start=True, stop=True)
            last.then_inc(lg_mm, 1)
            pe.wait_ge(cw_ok, 2)
            for i in range(NG):
                if i >= 2:
                    pe.wait_ge(wt_ok, i - 1)
                for s in range(4):
                    t = 8 * (i // 2) + 2 * s + i % 2
                    last = nc.tensor.transpose(ps[0:E, 3 + i % 2, P * s:P * s + P], cw[:, t, :], idt[:, :])
                last.then_inc(wt_mm, 1)
            pe.wait_ge(wt_ok, NG)

            with pe.Fori(0, NC) as q:
                def down(i):
                    for par in range(2):
                        pe.wait_ge(hw_ok, q * (2 * E) + (2 * i + par + 1) + 1)
                        last = mm(ps[64 * par:64 * par + 64, 6, :], w2[:, i, :], hw[:, i % 2, par, :],
                                  start=False, stop=(i == E - 1))
                    last.then_inc(y_mm, 1)

                for i in range(E):
                    for par in range(2):
                        if i >= 2:
                            pe.wait_ge(h_ok, q * (2 * E) + (2 * i + par - 3) + 1)
                        else:
                            pe.wait_ge(h_ok, q * (2 * E) + 1)
                        mm(ps[:, 2 * (i % 2) + par, :], w1[:, par, i, :], zt[:, bass.ds(q * 512, 512)],
                           start=True, stop=True).then_inc(h_mm, 1)
                    for par in range(2):
                        if i >= 1:
                            pe.wait_ge(hw_ok, q * (2 * E) + (2 * i + par - 1) + 1)
                        else:
                            pe.wait_ge(hw_ok, q * (2 * E) + 1)
                        mm(ps[:, 4 + par, :], sel[:, P * i:P * i + P], wth[:, bass.ds(q * 1024 + 512 * par, 512)],
                           start=True, stop=True).then_inc(wb_mm, 1)
                    if i == 0:
                        pe.wait_ge(y_ok, q + 1)
                        for par in range(2):
                            mm(ps[:, 6, :], b2[:, par, :], wt32[:, bass.ds(q * 1024 + 512 * par, 512)],
                               start=(par == 0), stop=False)
                    else:
                        down(i - 1)
                down(E - 1)
                pe.wait_ge(y_ok, q + 1 + 1)
                pe.wait_ge(o_ok, q + 1)
                for s in range(4):
                    last = nc.tensor.transpose(ps[:, 7, P * s:P * s + P], ot[:, P * s:P * s + P], idt[:, :])
                last.then_inc(yt_mm, 1)


def build_kernel(nc, A, out):
    scratch = {
        "z": nc.dram_tensor("modes_scratch", [2 * KX, MODES, C, B], F32).ap(),
        "r": nc.dram_tensor("new_modes_scratch", [C, 2 * KX, CH], F32).ap(),
        "u": nc.dram_tensor("inverse_scratch", [NOCT * P, 2, MODES, N], F16).ap(),
        "t": nc.dram_tensor("forward_scratch", [NOCT * S, 2, MODES, N], F32).ap(),
    }
    h_d = nc.dram_tensor("h_scratch", [16, XP, 4, 4 * S], F32).ap()
    operator_stage(nc, A, scratch, h_d)
    token_stage(nc, A, h_d, out)


def kernel(**inputs):
    import concourse.bacc as _bacc
    from concourse.bass_utils import run_bass_kernel_spmd as _run

    def get(name):
        return np.asarray(inputs[name])

    def tok(name):
        return get("L0_tok_" + name)

    pw, pb, fw = tok("p_w"), tok("p_b"), tok("fw")
    by_mode = fw.transpose(0, 1, 2, 4, 5, 6, 3)
    arrays = {
        "table": constant_table(),
        "xt": get("x")[..., 0].transpose(1, 2, 0).reshape(32, P, B).transpose(1, 0, 2),
        "w1t": tok("w1_w").transpose(0, 2, 1),
        "w2t": tok("w2_w").transpose(0, 2, 1),
        "w2": tok("w2_w"),
        "pt": np.concatenate([pw.T, pb[None]], 0),
        "pc": np.pad(np.concatenate([pw, pb[:, None]], 1), ((0, 0), (0, OCT - MID))),
        "q1t": tok("q1_w").T,
        "b2t": tok("w2_b").T,
        "b1t": tok("w1_b").T,
        "q1b": np.tile(np.repeat(tok("q1_b"), 4), 8)[:, None],
        "q2c": np.tile(np.repeat(tok("q2_w")[0], 4), 8)[:, None],
        "q2b": np.broadcast_to(tok("q2_b"), (32, 1)),
        "b1w": np.repeat(tok("w1_b"), B, axis=1),
        "fwt": np.stack([by_mode, by_mode[:, :, :, :, :, ::-1]], 2).reshape(L, P, MODES, CH),
        "txt": get("txt"),
        "ew1": get("L0_ffn_W1"),
        "ew2": get("L0_ffn_W2"),
        "wg": get("L0_ffn_Wg"),
        "eb1": get("L0_ffn_b1").T,
        "eb2": get("L0_ffn_b2"),
        "bg": np.broadcast_to(get("L0_ffn_bg"), (P, E)),
        "bias": np.broadcast_to(get("L0_ffn_bias"), (P, E)),
    }
    arrays = {f"in_{name}": np.ascontiguousarray(a) for name, a in arrays.items()}
    nc = _bacc.Bacc("TRN2", target_bir_lowering=False, num_devices=1)
    A = {name[3:]: nc.dram_tensor(name, a.shape, mybir.dt.from_np(a.dtype), kind="ExternalInput").ap()
         for name, a in arrays.items()}
    out = nc.dram_tensor("out_dram", (B, SEQ, D), F32, kind="ExternalOutput").ap()
    build_kernel(nc, A, out)
    r = _run(nc, [arrays], core_ids=[0])
    return r.results[0]["out_dram"]
```

```python
from contextlib import ExitStack

import numpy as np

import concourse.bass as bass
from concourse import mybir

ALU = mybir.AluOpType
ACT = mybir.ActivationFunctionType
AX = mybir.AxisListType
F32 = mybir.dt.float32
F16 = mybir.dt.float16

P = 128
B = 64
S = 64
C = 32
L = 4
MODES = 12
KX = 2 * MODES
MID = 4
OCT = 8
NOCT = C // OCT
N = OCT * B
XP = 16
CH = MODES * B
HC = CH // 2
TXT = 32
SEQ = S + TXT
D = 64
NT = 48
E = 8
HID = 128

T_DB, T_EA, T_D1, T_D2, T_ID, T_BM, T_M32, T_GX, T_GY, T_SEL, T_END = np.cumsum(
    [0, P, 2 * P, 64, 64, P, 16, 32, 32, 1, E * P]).tolist()


def constant_table():
    t = np.zeros((P, T_END), np.float64)
    y = np.arange(S)
    ky = np.arange(MODES)
    kx = np.r_[np.arange(MODES), np.arange(S - MODES, S)]
    phi = 2 * np.pi * np.outer(ky, y) / S
    theta = 2 * np.pi * np.outer(kx, y) / S
    twice = np.where(ky == 0, 1.0, 2.0)[:, None]
    for x2 in range(2):
        for ro, m in enumerate((twice * np.cos(phi) / 8, -twice * np.sin(phi) / 8)):
            for hl in range(2):
                r = 48 * x2 + 24 * ro + MODES * hl
                t[r:r + MODES, T_DB + S * x2:T_DB + S * x2 + S] = m
    for g in range(2):
        re, im = 64 * g, 64 * g + KX
        c = T_EA + P * g
        t[re:re + KX, c:c + S] = np.cos(theta) / 8
        t[im:im + KX, c:c + S] = -np.sin(theta) / 8
        t[re:re + KX, c + S:c + P] = np.sin(theta) / 8
        if g == 0:
            t[48, c:c + S] = 8.0
        t[im:im + KX, c + S:c + P] = np.cos(theta) / 8
    for x2 in range(2):
        c = T_D1 + 24 * x2
        t[64 * x2:64 * x2 + S, c:c + MODES] = np.cos(phi).T / 8
        t[64 * x2:64 * x2 + S, c + MODES:c + 24] = -np.sin(phi).T / 8
    t[0:S, T_D2:T_D2 + KX] = np.cos(theta).T / 8
    t[S:P, T_D2:T_D2 + KX] = np.sin(theta).T / 8
    t[0:S, T_D2 + KX:T_D2 + 48] = -np.sin(theta).T / 8
    t[S:P, T_D2 + KX:T_D2 + 48] = np.cos(theta).T / 8
    t[:, T_ID:T_ID + P] = np.eye(P)
    p = np.arange(P)
    q = np.arange(32)
    t[:, T_BM:T_BM + 16] = (p[:, None] // 32 == q[:16] // 4) & (p[:, None] % 4 == q[:16] % 4)
    t[:, T_M32:T_M32 + 32] = (p[:, None] // 16 == q // 4) & (p[:, None] % 4 == q % 4)
    for xp in range(32):
        t[:, T_GX + xp] = (2 * xp + p // 64) / (S - 1)
    t[:, T_GY] = (p % 64) / (S - 1)
    for e in range(E):
        t[[e, 32 + e], T_SEL + P * e:T_SEL + P * (e + 1)] = 2.0 ** -10
    return t.astype(np.float32)


def paced(eng, first, lo, hi, last, step):
    for k in range(first, lo):
        step(k, k % 2, k // 2)
    with eng.Fori(lo // 2, hi // 2) as i:
        for p in range(2):
            step(i * 2 + p, p, i)
    for k in range(hi, last):
        step(k, k % 2, k // 2)


def paced4(eng, lo, hi, last, step):
    for k in range(lo):
        step(k, k % 4, k // 2)
    with eng.Fori(0, (hi - lo) // 4) as i:
        for n in range(lo, lo + 4):
            step(i * 4 + n, n % 4, i * 2 + n // 2)
    for k in range(hi, last):
        step(k, k % 4, k // 2)


def wait_alone(eng, sem, value, passed):
    eng.wait_ge(sem, value)
    if not isinstance(value, int):
        eng.sem_inc(passed, 1)


def inside(k, lo, hi):
    return not isinstance(k, int) or lo <= k < hi


def operator_stage(nc, A, scratch, tokens_out):
    with ExitStack() as ctx:
        def sb(name, shape, dt=F32):
            return ctx.enter_context(nc.sbuf_tensor(name, shape, dt))

        def sem(name):
            return ctx.enter_context(nc.semaphore(name))

        TT = 5
        tab = sb("tab", [P, T_SEL])
        spec = sb("spec", [P, MODES, CH])
        field = sb("field", [P, XP * N])
        half = sb("half", [P, XP, N])
        qacc = sb("qacc", [P, XP, N])
        zt = sb("zt", [P, MODES // 2, N])
        u = sb("u", [P, 2, 2, 2, N], F16)
        tt = sb("tt", [P, TT, 2, N])
        rr = sb("rr", [P, 2, N])
        r = sb("r", [P, 2, 2, N])
        rt = sb("rt", [P, 2, 2, N])
        w1all = sb("w1all", [P, L, P])
        w2all = sb("w2all", [P, L, P])
        w1s = sb("w1s", [P, P])
        w2s = sb("w2s", [P, P])
        b2all = sb("b2all", [P, L, MODES])
        gall = sb("gall", [P, 1 + L * NOCT, 4, MID, 4])
        gs = sb("gs", [P, 64])
        wg = sb("wg", [C, 1 + L, C])
        q1t = sb("q1t", [C, MID])
        b1t = sb("b1t", [C, L])
        b2t = sb("b2t", [C, L])
        q1b = sb("q1b", [P, 1])
        q2c = sb("q2c", [P, 1])
        q2m = sb("q2m", [P, 32])
        q2b = sb("q2b", [32, 1])
        qb = sb("qb", [P, 2])
        dbh = sb("dbh", [P, 2, P], F16)
        peak = sb("peak", [P, MODES + 1])
        scl = sb("scl", [P, 8])
        ones = sb("ones", [1, P])
        fst, zc = (field[:, 2 * CH * i:2 * CH * (i + 1)].rearrange("p (s n) -> p s n", s=2) for i in range(2))
        zo = field[:, 4 * CH:8 * CH].rearrange("p (s n) -> p s n", s=4)
        wch, rs = (half[:, :, :].rearrange("p k n -> p (k n)")[:, 4 * CH * i:4 * CH * (i + 1)].rearrange(
            "p (s n) -> p s n", s=4) for i in range(2))
        f16 = field[:, :].bitcast(F16).rearrange("p (k g n) -> p k g n", g=2, k=XP)
        u_first = [u[:, 0, :, :, :], u[:, 1, :, :, :]] + [
            b[:, p, :, :].rearrange("p g n -> p (g n)").bitcast(F16).rearrange("p (h y n) -> p h y n", h=2, y=2)
            for b in (r, rt) for p in range(2)]
        wrep = half[0:C, 0:5, :].rearrange("p k n -> p (k n)")[:, 0:(1 + L * NOCT) * P]
        q1rep = half[0:C, 5, 0:64]
        xs = tt[:, 0:2, :, :].rearrange("p s y n -> p (s y n)").rearrange("p (x b) -> p x b", b=B)

        ps = ctx.enter_context(nc.psum_tensor("ps", [P, 8, 512], F32))
        ps_b = [[ps[:, 2 * p + g, :] for g in range(2)] for p in range(2)]
        ps_q, ps_f = ps[:, 4, :], ps[:, 5, :]
        ps_a = [ps[:, 6, :], ps[:, 7, :]]
        ps_first = ps_a + [ps_q, ps_f]
        ps_w2, ps_mix, ps_w1 = (ps[:, 2 * i:2 * i + 2, 0:HC] for i in range(3))

        def ea(g):
            return tab[:, T_EA + P * g:T_EA + P * (g + 1)]

        def by_octet(ap):
            return ap.rearrange("p (c o b) -> p o c b", c=16, o=OCT)

        def octets_of(ap):
            return ap.rearrange("p (o c b) -> p o c b", c=16, o=OCT)

        d1, d2 = tab[:, T_D1:T_D1 + 64], tab[:, T_D2:T_D2 + 64]
        ident, bmask = tab[:, T_ID:T_ID + P], tab[:, T_BM:T_BM + 16]
        scale, unscale = scl[:, 4:5], scl[:, 5:6]

        const_ld, zeroed, x_ld = sem("const_ld"), sem("zeroed"), sem("x_ld")
        sp_passed, pool_passed, pe_passed = sem("sp_passed"), sem("pool_passed"), sem("pe_passed")
        g_mm, g_ok, b_ok, qb_mm, qb_ok = (sem(n) for n in ("g_mm", "g_ok", "b_ok", "qb_mm", "qb_ok"))
        w_ld, rs_ld = ([sem(f"{n}{i}") for i in range(4)] for n in ("w_ld", "rs_ld"))
        w_neg, w2_mm, f_new, f_cp = (sem(n) for n in ("w_neg", "w2_mm", "f_new", "f_cp"))
        mix_mm, zc_ev, w1_mm, zo_ev, wts = (sem(n) for n in ("mix_mm", "zc_ev", "w1_mm", "zo_ev", "wts"))
        zo_peak = sem("zo_peak")
        peak_ok, row_mm, one_ok, all_mm, scale_ok = (sem(n) for n in (
            "peak_ok", "row_mm", "one_ok", "all_mm", "scale_ok"))
        z_st = [[sem(f"z_st{h}{i}") for i in range(4)] for h in range(2)]
        zt_ld, a_mm, a_hi, a_lo = (sem(n) for n in ("zt_ld", "a_mm", "a_hi", "a_lo"))
        u_st, ut_ld, b_mm = [sem("u_st0"), sem("u_st1")], [sem("ut_ld0"), sem("ut_ld1")], sem("b_mm")
        r_ok, rt_ok = ([sem(f"{n}{g}") for g in range(2)] for n in ("r_ok", "rt_ok"))
        q_mm, q_ad, y_mm, y_ev = (sem(n) for n in ("q_mm", "q_ad", "y_mm", "y_ev"))
        t_st = [sem(f"t_st{i}") for i in range(3)]
        tt_ld = [sem(f"tt_ld{i}") for i in range(TT)]
        x_mm, x_ev = sem("x_mm"), [sem("x_ev0"), sem("x_ev1")]
        r_st = [[sem(f"r_st{g}{i}") for i in range(2)] for g in range(2)]
        gs_ok = sem("gs_ok")
        q_act, q2_mm, h_ev, h_st = (sem(n) for n in ("q_act", "q2_mm", "h_ev", "h_st"))
        NCONST = 9 + 4 * 3

        z_d, u_d, t_d, r_d = (scratch[n] for n in ("z", "u", "t", "r"))

        def prime(eng, *sems):
            for s in sems:
                eng.sem_inc(s, 1)

        block = ctx.enter_context(nc.Block())

        def layers(eng, octets, spectral, epilogue):
            spectral(0, True)
            with eng.Fori(0, L - 1) as l:
                octets(l, True)
                spectral(l + 1, False)
            octets(L - 1, False)
            epilogue()

        def in_layer(eng, main):
            main(0, True, False)
            with eng.Fori(1, NOCT - 1) as n:
                main(n, True, True)
            main(NOCT - 1, False, True)

        def register(*values):
            return not all(isinstance(v, int) for v in values)

        def new_modes_store(eng, m, j, g, new_modes, passed):
            wait_alone(eng, x_ev[j % 2], m * 3 + j // 2 + 1, passed)
            dst = new_modes[:, :, 64 * (2 * j + g):64 * (2 * j + g) + 64].rearrange("o k b -> k o b")
            eng.dma_start(dst, rr[64 * g:64 * g + 48, j % 2, :].rearrange("p (o b) -> p o b", o=OCT)
                          ).then_inc(r_st[g][j % 2], 16)

        def z_store(eng, l, c, q, h, passed):
            wait_alone(eng, zo_ev, l * MODES + c + 1, passed)
            for ri in range(2):
                row = 64 * h + 32 * ri
                eng.dma_start(z_d[c + (KX * ri + MODES * h), :, :, :].rearrange("y o b -> o y b"),
                              zo[row:row + 32, q, :].rearrange("p (y b) -> p y b", b=B)).then_inc(z_st[h][q], 16)

        A_STEPS = MODES // 2
        T_PARTS = ((0, 8), (8, 12), (12, 16))
        X_STEPS = {14: (0,), 15: (1, 2), 16: (3, 4), 17: (5,)}

        @block.sync
        def _(sp):
            prime(sp, *u_st)

            def const(dst, src):
                sp.dma_start(dst, src).then_inc(const_ld, 16)

            const(tab[:, :], A["table"][:, 0:T_SEL])
            sp.dma_start(xs, A["xt"]).then_inc(x_ld, 16)
            const(q1t[:, :], A["q1t"])
            const(b1t[:, :], A["b1t"])
            const(b2t[:, :], A["b2t"])
            const(q1b[:, :], A["q1b"])
            const(q2c[:, :], A["q2c"])
            const(q2b[:, :], A["q2b"])
            const(wg[:, 1:1 + L, :], A["w2"].rearrange("l o i -> o l i"))
            sp.wait_ge(zeroed, 1)
            const(wg[:, 0, 0:OCT], A["pc"])
            for i in range(4):
                const(w1all[32 * i:32 * i + 32, :, 32 * i:32 * i + 32], A["w1t"].rearrange("l i o -> i l o"))
                const(w2all[32 * i:32 * i + 32, 1:L, 32 * i:32 * i + 32],
                      A["w2t"].rearrange("l i o -> i l o")[:, 0:L - 1, :])
                const(w2all[32 * i:32 * i + MID, 0, 32 * i:32 * i + 32], A["pt"])

            def t_store(m, n, part):
                k0, k1 = T_PARTS[part]
                wait_alone(sp, y_ev, m * XP + k1, sp_passed)
                for g in range(2):
                    for x2 in range(2):
                        row, x0 = 64 * g + 24 * x2, 4 * k0 + 2 * g + x2
                        dst = t_d[bass.ds(n * S + x0, k1 - k0, 4), :, :, :].rearrange("k r y n -> (r y) k n")
                        sp.dma_start(dst, half[row:row + 24, k0:k1, :]).then_inc(t_st[part], 16)

            def tt_load(m, n, j):
                if j == 0:
                    for stored in t_st:
                        wait_alone(sp, stored, m * 64 + 64, sp_passed)
                if j == TT or (j == 0 and (register(m) or m > 0)):
                    wait_alone(sp, x_mm, m * 6 + (1 if j == TT else 0), sp_passed)
                for ri in range(2):
                    sp.dma_start(tt[64 * ri:64 * ri + 64, j % TT, :, :],
                                 t_d[bass.ds(n * S, S), ri, 2 * j:2 * j + 2, :]).then_inc(tt_ld[j % TT], 16)

            for part in range(3):
                t_store(0, 0, part)
            sp.wait_ge(r_ok[0], XP)
            sp.wait_ge(r_ok[1], XP)
            for j in range(TT):
                tt_load(0, 0, j)
            for j in range(6):
                if j + TT < 6:
                    tt_load(0, 0, j + TT)
                new_modes_store(sp, 0, j, 1, r_d[0:OCT], sp_passed)

            def spectral(l, first):
                def w_load(c, q):
                    sp.dma_start(wch[:, q, :], A["fwt"][l, :, c, :]).then_inc(w_ld[q], 16)

                def rs_load(c, q):
                    for h in range(2):
                        for ri in range(2):
                            row, n = 64 * h + 32 * ri, (OCT if first else C)
                            src = r_d[0:n, KX * ri + MODES * h + c, :]
                            sp.dma_start(rs[row:row + n, q, :], src).then_inc(rs_ld[q], 16)

                def load(c, q, i):
                    if isinstance(c, int) and c < 4:
                        rs_load(c, q)
                    elif inside(c, 4, MODES):
                        wait_alone(sp, w2_mm, l * MODES + c - 3, sp_passed)
                        rs_load(c, q)
                        wait_alone(sp, mix_mm, l * MODES + c - 3, sp_passed)
                        w_load(c, q)
                    if inside(c, 4, MODES + 4):
                        z_store(sp, l, c - 4, q, 1, sp_passed)

                for c in range(4):
                    w_load(c, c)
                for s in r_st[0] + r_st[1]:
                    wait_alone(sp, s, 48 if first else l * (48 * NOCT) + 48, sp_passed)
                paced4(sp, 4, 12, MODES + 4, load)

            def octets(l, forward):
                def u_store(n, bt, src=None):
                    m = l * NOCT + n
                    wait_alone(sp, a_lo, m * MODES + 2 * bt + 2 + 1, sp_passed)
                    sp.dma_start(u_d[bass.ds(n * P, P), :, 2 * bt:2 * bt + 2, :],
                                 u[:, bt % 2, :, :, :] if src is None else src).then_inc(u_st[bt % 2], 16)

                def field_load(n, b, first):
                    m = l * NOCT + n
                    if b == 0:
                        for s in range(2):
                            wait_alone(sp, u_st[s], m * 48 + 48 + 1, sp_passed)
                    if not first:
                        wait_alone(sp, b_mm, m * (2 * XP) + (16 * b - 16 + 1), sp_passed)
                    for x2 in range(2):
                        for ri in range(2):
                            row, x0 = 48 * x2 + 24 * ri, n * P + S * ri + 32 * b + x2
                            src = u_d[bass.ds(x0, 16, 2), :, :, :].rearrange("x s y n -> (s y) x n")
                            dst = f16[row:row + 24, 8 * b:8 * b + 8, :, :].rearrange("p k g n -> p (k g) n")
                            sp.dma_start(dst, src).then_inc(ut_ld[b], 16)

                def main(n, more, after):
                    m = l * NOCT + n
                    back = after and forward
                    for bt in range(6):
                        if more:
                            u_store(n + 1, bt)
                        if after and bt == 0:
                            field_load(n, 1, False)
                    if back:
                        for j in range(TT):
                            tt_load(m, n - 1, j)
                    if more:
                        field_load(n + 1, 0, False)
                    if forward:
                        t_store(m + 1, n, 0)
                        t_store(m + 1, n, 1)
                    if back:
                        def r_store(j):
                            new_modes_store(sp, m, j, 1, r_d[bass.ds((n - 1) * OCT, OCT)], sp_passed)
                        tt_load(m, n - 1, TT)
                        for j in range(3):
                            r_store(j)
                    if back:
                        for j in range(3, 5):
                            r_store(j)
                    if forward:
                        t_store(m + 1, n, 2)
                    if back:
                        r_store(5)

                for bt in range(6):
                    u_store(0, bt, u_first[bt])
                wait_alone(sp, f_cp, l * MODES + MODES, sp_passed)
                for s in z_st[0] + z_st[1]:
                    wait_alone(sp, s, l * 96 + 96, sp_passed)
                for b in range(2):
                    field_load(0, b, True)
                in_layer(sp, main)
                if forward:
                    m = l * NOCT + NOCT
                    for j in range(TT):
                        tt_load(m, NOCT - 1, j)
                    for j in range(6):
                        if j + TT < 6:
                            tt_load(m, NOCT - 1, j + TT)
                        new_modes_store(sp, m, j, 1, r_d[C - OCT:C], sp_passed)

            def epilogue():
                for k0 in (0, XP // 2):
                    sp.wait_ge(h_ev, k0 + XP // 2)
                    for b in range(4):
                        sp.dma_start(tokens_out[k0:k0 + XP // 2, :, b, :].rearrange("k c (a y) -> a (k c) y", y=32),
                                     half[b:b + 29:4, k0:k0 + XP // 2, :].rearrange("p k n -> p (k n)").rearrange(
                                         "p (m y) -> p m y", y=32)).then_inc(h_st, 16)
                sp.wait_ge(h_st, 16 * 8)

            layers(sp, octets, spectral, epilogue)

        @block.gpsimd
        def _(pool):
            g_ = nc.gpsimd
            g_.memset(w1all[:, :, :], 0.0)
            g_.memset(w2all[:, :, :], 0.0)
            g_.memset(wg[:, 0, :], 0.0).then_inc(zeroed, 1)
            g_.memset(b2all[:, :, :], 0.0)
            g_.memset(peak[:, :], 0.0)
            g_.memset(ones[:, :], 1.0)
            g_.memset(zt[:, :, :], 0.0)
            g_.memset(spec[:, 0:6, :], 0.0)
            g_.memset(spec[:, 6:12, :], 0.0).then_inc(zeroed, 1)

            for j in range(6):
                new_modes_store(pool, 0, j, 0, r_d[0:OCT], pool_passed)

            def spectral(l, first):
                def step(c, q, i):
                    z_store(pool, l, c, q, 0, pool_passed)
                paced4(pool, 4, 12, MODES, step)

            def octets(l, forward):
                def zt_load(n, stored=()):
                    wait_alone(pool, a_mm, (l * NOCT + n) * MODES + 1, pool_passed)
                    pool.dma_start(zt[48:49, 0, :], A["b1w"][bass.ds(l, 1), bass.ds(n * N, N)]).then_inc(zt_ld, 16)
                    for s in stored:
                        wait_alone(pool, s, l * 96 + 96, pool_passed)
                    src = z_d[:, :, bass.ds(n * OCT, OCT), :].rearrange("k (i g) o b -> g k i (o b)", g=2)
                    for g in range(2):
                        pool.dma_start(zt[64 * g:64 * g + 48, :, :], src[g]).then_inc(zt_ld, 16)

                zt_load(0, z_st[0] + z_st[1])
                with pool.Fori(1, NOCT) as n:
                    zt_load(n)
                if forward:
                    with pool.Fori(0, NOCT) as n:
                        for j in range(6):
                            new_modes_store(pool, l * NOCT + 1 + n, j, 0, r_d[bass.ds(n * OCT, OCT)], pool_passed)

            layers(pool, octets, spectral, lambda: None)

        def forward_x_evac(on, m, j):
            eng = nc.scalar if on == 0 else nc.vector
            if j % 2 == on:
                eng.wait_ge(x_mm, m * 6 + j + 1)
                if register(m) or m > 0 or j >= 2:
                    for g in range(2):
                        eng.wait_ge(r_st[g][on], m * 48 + 16 * (j // 2))
                copy = nc.scalar.copy if on == 0 else nc.vector.tensor_copy
                copy(rr[:, on, :], ps_a[on]).then_inc(x_ev[on], 1)

        @block.scalar
        def _(act):
            prime(act, a_hi)

            def high_half(m, ky, q, to=None, banks=ps_a):
                act.wait_ge(a_mm, m * MODES + ky + 1 + 1)
                if to is None:
                    act.wait_ge(u_st[q // 2], m * 48 + ((ky - q) * 4 + 1))
                    to = u[:, q // 2, :, :, :]
                nc.scalar.activation(to[:, 0, q % 2, :], banks[ky % len(banks)], ACT.Copy, scale=scale).then_inc(a_hi, 1)

            def main(m, ob, forward, more, after):
                def step(k, q, i):
                    p = q % 2
                    if inside(k, 0, XP):
                        if register(m, k) or k >= 2:
                            act.wait_ge(rt_ok[0], m * XP + k - 1)
                            act.wait_ge(rt_ok[1], m * XP + k - 1)
                            if forward:
                                act.wait_ge(y_mm, m * XP + k - 1)
                        for g in range(2):
                            if ob is None:
                                rc = by_octet(r[:, p, g, :])
                                nc.scalar.copy(rc[:, 0], xs[:, bass.ds(k * 2 + g, 1), :].rearrange(
                                    "p x (c b) -> p (x c) b", b=4))
                                nc.scalar.activation(rc[:, 1], rc[:, 3], ACT.Copy,
                                                     scale=tab[:, bass.ds(k * 2 + (T_GX + g), 1)]).then_inc(r_ok[g], 1)
                            else:
                                act.wait_ge(b_mm, (ob * XP + k) * 2 + g + 1 + 1)
                                nc.scalar.activation(by_octet(r[:, p, g, :]), octets_of(ps_b[p][g]), ACT.Relu,
                                                     scale=unscale).then_inc(r_ok[g], 1)
                    if forward and inside(k, 1, XP + 1):
                        act.wait_ge(y_mm, m * XP + k)
                        if isinstance(k, int) and k in (1, 5) and (register(m) or m > 0):
                            for stored in (t_st[0:1] if k == 1 else t_st[1:]):
                                act.wait_ge(stored, m * 64)
                        nc.scalar.copy(octets_of(half[:, k - 1, :]), by_octet(ps_f)).then_inc(y_ev, 1)
                    if more and isinstance(k, int) and k < A_STEPS:
                        for ky in (2 * k, 2 * k + 1):
                            high_half(ob + 1, ky, ky % 4)
                    if after and isinstance(k, int):
                        for j in X_STEPS.get(k, ()):
                            forward_x_evac(0, m - 1, j)
                paced4(act, 6, 14, 18, step)

            act.wait_ge(const_ld, 16 * NCONST)
            act.wait_ge(x_ld, 16)
            act.wait_ge(zeroed, 3)
            main(0, None, True, False, False)
            for j in range(6):
                forward_x_evac(0, 0, j)

            def spectral(l, first):
                def step(c, q, i):
                    p = q % 2
                    if inside(c, 1, MODES + 1):
                        act.wait_ge(f_new, (l * MODES + c) * 2)
                        nc.scalar.copy(spec[:, c - 1, :], fst[:, 1 - p, :]).then_inc(f_cp, 1)
                        act.wait_ge(mix_mm, l * MODES + c)
                        if register(l, c) or c >= 3:
                            act.wait_ge(w1_mm, l * MODES + c - 2)
                        nc.scalar.copy(zc[:, 1 - p, :].rearrange("p (a n) -> p a n", a=2), ps_mix).then_inc(zc_ev, 1)
                    if inside(c, 0, MODES):
                        act.wait_ge(w_ld[q], l * 48 + ((c - q) * 4 + 16))
                        for h in range(2):
                            rows = wch[64 * h + 32:64 * h + 64, q, :].rearrange("p (m o) -> p m o", o=64)[:, :, 0:C]
                            nc.scalar.mul(rows, rows, -1.0).then_inc(w_neg, 1)
                paced4(act, 4, 12, 14, step)

            def octets(l, forward):
                act.wait_ge(scale_ok, l + 1)
                for ky in range(MODES):
                    high_half(l * NOCT, ky, ky % 4, u_first[ky // 2], ps_first)
                in_layer(act, lambda n, more, after:
                         main(l * NOCT + n + 1, l * NOCT + n, forward, more, after and forward))
                if forward:
                    for j in range(6):
                        forward_x_evac(0, l * NOCT + NOCT, j)

            def epilogue():
                act.wait_ge(qb_ok, 1)
                act.wait_ge(q_ad, (1 + L * NOCT) * XP)

                def step(k, p, i):
                    nc.scalar.activation(qacc[:, k, :], qacc[:, k, :], ACT.Relu, bias=qb[:, 0:1]).then_inc(q_act, 1)
                paced(act, 0, 0, XP, XP, step)
            layers(act, octets, spectral, epilogue)

        @block.vector
        def _(dve):
            prime(dve, a_lo)
            v = nc.vector
            for p in range(2):
                for g in range(2):
                    rc = by_octet(r[:, p, g, :])
                    v.memset(r[:, p, g, :], 0.0).then_inc(b_ok, 1)
            dve.wait_ge(b_ok, 4)
            for p in range(2):
                for g in range(2):
                    last = v.memset(by_octet(r[:, p, g, :])[:, 3], 1.0)
            last.then_inc(b_ok, 1)
            dve.wait_ge(const_ld, 16 * NCONST)
            dve.wait_ge(zeroed, 2)
            dve.wait_ge(b_ok, 5)
            for p in range(2):
                for g in range(2):
                    rc = by_octet(r[:, p, g, :])
                    last = v.tensor_scalar(rc[:, 2], rc[:, 3], tab[:, T_GY:T_GY + 1], None, ALU.mult)
            last.then_inc(zeroed, 1)
            v.tensor_scalar(b2all[0:C, 1:L, 0], b2t[:, 0:L - 1], 64.0, None, ALU.mult)
            v.tensor_scalar(dbh[:, 0, :], tab[:, T_DB:T_DB + P], 1024.0, None, ALU.mult).then_inc(b_ok, 1)
            dve.wait_ge(b_ok, 6)
            v.scalar_tensor_tensor(out=dbh[:, 1, :], in0=tab[:, T_DB:T_DB + P], scalar=1024.0, in1=dbh[:, 0, :],
                                   op0=ALU.mult, op1=ALU.subtract)
            for i in range(1 + L * NOCT):
                cols = wg[:, 0, 0:OCT] if i == 0 else wg[:, 1 + (i - 1) // NOCT, (i - 1) % NOCT * OCT:(i - 1) % NOCT * OCT + OCT]
                v.tensor_copy(wrep[:, P * i:P * i + P].rearrange("p (a o b) -> p a o b", a=4, b=4),
                              cols[:, None, :, None].broadcast_to([C, 4, OCT, 4]))
            v.tensor_copy(q1rep.rearrange("p (a o b) -> p a o b", a=4, b=4),
                          q1t[:, None, :, None].broadcast_to([C, 4, MID, 4])).then_inc(b_ok, 1)
            for i in range(1 + L * NOCT):
                dve.wait_ge(g_mm, i + 1)
                gp = ps_b[0][i % 2][:, 0:MID]
                v.tensor_tensor(gall[:, i, :, :, :], gp[:, None, :, None].broadcast_to([P, 4, MID, 4]),
                                bmask.rearrange("p (a b) -> p a b", a=4)[:, :, None, :].broadcast_to([P, 4, MID, 4]),
                                ALU.mult).then_inc(g_ok, 1)
            v.tensor_scalar(q2m[:, :], tab[:, T_M32:T_M32 + 32], q2c[:, 0:1], None, ALU.mult).then_inc(b_ok, 1)
            dve.wait_ge(qb_mm, 1)
            v.tensor_reduce(qb[:, 1:2], ps_q[:, 0:L], AX.X, ALU.add).then_inc(b_ok, 1)
            dve.wait_ge(b_ok, 9)
            v.tensor_tensor(qb[:, 0:1], qb[:, 1:2], q1b[:, :], ALU.add).then_inc(qb_ok, 1)

            def low_half(m, ky, q, to=None, banks=ps_a):
                dve.wait_ge(a_hi, m * MODES + ky + 1 + 1)
                to = u[:, q // 2, :, :, :] if to is None else to
                v.scalar_tensor_tensor(out=to[:, 1, q % 2, :], in0=banks[ky % len(banks)], scalar=scale,
                                       in1=to[:, 0, q % 2, :], op0=ALU.mult, op1=ALU.subtract).then_inc(a_lo, 1)

            def main(m, ob, forward, more, after):
                if ob is None:
                    dve.wait_ge(g_ok, 1 + L * NOCT)
                    v.tensor_copy(gs[:, :], gall[:, 0, :, :, :].rearrange("p a o b -> p (a o b)")).then_inc(gs_ok, 1)
                else:
                    dve.wait_ge(q_mm, m * XP)
                    v.tensor_copy(gs[:, :], gall[:, bass.ds(m, 1), :, :, :].rearrange("p m a o b -> p (m a o b)")
                                  ).then_inc(gs_ok, 1)

                def step(k, q, i):
                    p = q % 2
                    if inside(k, 1, XP + 1):
                        for g in range(2):
                            dve.wait_ge(r_ok[g], m * XP + k)
                            if g == 0 and (register(m, k) or k >= 3):
                                dve.wait_ge(q_mm, m * XP + k - 2)
                            v.transpose(rt[:, 1 - p, g, :], r[:, 1 - p, g, :]).then_inc(rt_ok[g], 1)
                    if inside(k, 2, XP + 2):
                        dve.wait_ge(q_mm, m * XP + k - 1)
                        if ob is None:
                            v.tensor_copy(qacc[:, k - 2, :], ps_q).then_inc(q_ad, 1)
                        else:
                            v.tensor_tensor(qacc[:, k - 2, :], ps_q, qacc[:, k - 2, :], ALU.add).then_inc(q_ad, 1)
                    if more and isinstance(k, int) and k < A_STEPS:
                        for ky in (2 * k, 2 * k + 1):
                            low_half(ob + 1, ky, ky % 4)
                    if after and isinstance(k, int):
                        for j in X_STEPS.get(k, ()):
                            forward_x_evac(1, m - 1, j)
                paced4(dve, 6, 14, 18, step)

            main(0, None, True, False, False)
            for j in range(6):
                forward_x_evac(1, 0, j)

            def scale_of_layer(l):
                done = [0]

                def then(ins):
                    done[0] += 1
                    ins.then_inc(peak_ok, 1)
                    dve.wait_ge(peak_ok, l * 7 + done[0])

                then(v.tensor_reduce(peak[0:C, MODES:], b1t[:, bass.ds(l, 1)], AX.X, ALU.max, apply_absolute_value=True))
                then(v.tensor_reduce(scl[:, 0:1], peak[:, :], AX.X, ALU.max))
                dve.wait_ge(row_mm, l + 1)
                v.tensor_reduce(scl[0:1, 1:2], ps_a[0][0:1, 0:P], AX.X, ALU.max).then_inc(one_ok, 1)
                dve.wait_ge(all_mm, l + 1)
                then(v.tensor_scalar(scl[:, 2:3], ps_a[1][:, 0:1], 16.0, 2.0 ** -60, ALU.mult, ALU.max))
                then(v.tensor_scalar(scl[:, 3:4].bitcast(mybir.dt.int32), scl[:, 2:3].bitcast(mybir.dt.int32),
                                     0x7F800000, None, ALU.bitwise_and))
                then(v.reciprocal(scl[:, 6:7], scl[:, 3:4]))
                then(v.tensor_scalar(unscale, scl[:, 3:4], 2.0 ** -24, None, ALU.mult))
                then(v.tensor_scalar(scale, scl[:, 6:7], 2.0 ** 14, None, ALU.mult))
                dve.sem_inc(scale_ok, 1)

            def spectral(l, first):
                if not first:
                    dve.wait_ge(w1_mm, l * MODES)
                v.tensor_copy(w1s[:, :], w1all[:, bass.ds(l, 1), :].rearrange("p l o -> p (l o)")).then_inc(wts, 1)
                v.tensor_copy(w2s[:, :], w2all[:, bass.ds(l, 1), :].rearrange("p l o -> p (l o)")).then_inc(wts, 1)

                def step(c, q, i):
                    p = q % 2
                    if inside(c, 0, MODES):
                        dve.wait_ge(w2_mm, l * MODES + c + 1)
                        if register(l, c) or c >= 2:
                            dve.wait_ge(mix_mm, l * MODES + c - 1)
                            dve.wait_ge(f_cp, l * MODES + c - 1)
                        v.tensor_tensor(fst[:, p, :].rearrange("p (a n) -> p a n", a=2), ps_w2,
                                        spec[:, c, :].rearrange("p (a n) -> p a n", a=2), ALU.add).then_inc(f_new, 1)
                        dve.wait_ge(f_new, (l * MODES + c) * 2 + 1)
                        v.tensor_scalar(fst[:, p, 0:B], fst[:, p, 0:B],
                                        b2all[:, bass.ds(l, 1), bass.ds(c, 1)].rearrange("p l c -> p (l c)"),
                                        None, ALU.add).then_inc(f_new, 1)
                    if inside(c, 2, MODES + 2):
                        dve.wait_ge(w1_mm, l * MODES + c - 1)
                        q2 = (q - 2) % 4
                        if register(l, c) or c >= 6:
                            for h in range(2):
                                dve.wait_ge(z_st[h][q2], l * 96 + (c - 2 - q2) * 8)
                        v.tensor_copy(zo[:, q2, :].rearrange("p (a n) -> p a n", a=2), ps_w1).then_inc(zo_ev, 1)
                        dve.wait_ge(zo_ev, l * MODES + c - 1)
                        v.tensor_reduce(peak[:, bass.ds(c - 2, 1)], zo[:, q2, :], AX.X, ALU.max,
                                        apply_absolute_value=True).then_inc(zo_peak, 1)
                paced4(dve, 4, 12, 14, step)
                dve.wait_ge(zo_peak, l * MODES + MODES)
                scale_of_layer(l)

            def octets(l, forward):
                for ky in range(MODES):
                    low_half(l * NOCT, ky, ky % 4, u_first[ky // 2], ps_first)
                in_layer(dve, lambda n, more, after:
                         main(l * NOCT + n + 1, l * NOCT + n, forward, more, after and forward))
                if forward:
                    for j in range(6):
                        forward_x_evac(1, l * NOCT + NOCT, j)

            def epilogue():
                def step(k, p, i):
                    dve.wait_ge(q2_mm, k + 1)
                    v.tensor_scalar(half[0:32, k, :], ps_a[p][0:32, :], q2b[:, 0:1], None, ALU.add).then_inc(h_ev, 1)
                paced(dve, 0, 0, XP, XP, step)
            layers(dve, octets, spectral, epilogue)

        @block.tensor
        def _(pe):
            prime(pe, a_mm, b_mm)
            mm = nc.tensor.matmul
            pe.wait_ge(const_ld, 16 * NCONST)
            pe.wait_ge(b_ok, 7)
            for i in range(1 + L * NOCT):
                if i >= 2:
                    pe.wait_ge(g_ok, i - 1)
                mm(ps_b[0][i % 2][:, 0:MID], wrep[:, P * i:P * i + P], q1t[:, :], start=True, stop=True).then_inc(g_mm, 1)
            for g in range(2):
                last = mm(ps_q[64 * g:64 * g + 64, 0:L], q1rep, b2t[:, :], start=True, stop=True)
            last.then_inc(qb_mm, 1)
            pe.wait_ge(qb_ok, 1)
            pe.wait_ge(zeroed, 3)

            def stage_a(m, ky, banks=ps_a):
                pe.wait_ge(a_lo, m * MODES + max(ky + 1 - len(banks), 0) + 1)
                mm(banks[ky % len(banks)], ea(ky % 2), zt[:, ky // 2, :], start=True, stop=True).then_inc(a_mm, 1)

            def forward_x(m, j, adone):
                if j < 2 and (register(adone) or adone > 0):
                    pe.wait_ge(a_lo, adone * MODES + j)
                pe.wait_ge(tt_ld[j % TT], m * (64 if j % TT == 0 else 32) + 32 * (j // TT) + 32)
                if register(m) or m > 0 or j >= 2:
                    pe.wait_ge(x_ev[j % 2], m * 3 + j // 2)
                for g in range(2):
                    last = mm(ps_a[j % 2][64 * g:64 * g + 64, :], d2, tt[:, j % TT, g, :], start=True, stop=True)
                last.then_inc(x_mm, 1)

            def main(m, ob, forward, more, after, first=True):
                def step(k, q, i):
                    p = q % 2
                    if ob is not None and inside(k, 0, XP):
                        if isinstance(k, int) and k in (0, 5):
                            pe.wait_ge(ut_ld[k // 5], ob * 64 + 64)
                        for g in range(2):
                            if not isinstance(k, int) or k >= 2:
                                pe.wait_ge(r_ok[g], m * XP + k - 1)
                            else:
                                pe.wait_ge(r_ok[g], m * XP)
                            rhs = f16[0:96, bass.ds(k, 1), g, :].rearrange("p k n -> p (k n)")
                            for s in range(2):
                                last = mm(ps_b[p][g], dbh[0:96, s, :], rhs, start=(s == 0), stop=(s == 1))
                            last.then_inc(b_mm, 1)
                    if forward and inside(k, 1, XP + 1):
                        if register(m, k) or k >= 2:
                            pe.wait_ge(y_ev, m * XP + k - 1)
                        for g in range(2):
                            pe.wait_ge(r_ok[g], m * XP + k)
                            last = mm(ps_f[64 * g:64 * g + 64, :], d1, r[:, 1 - p, g, :], start=True, stop=True)
                        last.then_inc(y_mm, 1)
                    if inside(k, 2, XP + 2):
                        if isinstance(k, int) and k == 2:
                            pe.wait_ge(gs_ok, m + 1)
                        if register(m, k) or k >= 3:
                            pe.wait_ge(q_ad, m * XP + k - 2)
                        for g in range(2):
                            pe.wait_ge(rt_ok[g], m * XP + k - 1)
                            last = mm(ps_q[64 * g:64 * g + 64, :], gs[:, :], rt[:, p, g, :], start=True, stop=True)
                        last.then_inc(q_mm, 1)
                    if more and isinstance(k, int) and k < A_STEPS:
                        if k == 0:
                            start_a(ob + 1, gdone_last if not forward else m if first else m - 1)
                        for ky in (2 * k, 2 * k + 1):
                            stage_a(ob + 1, ky)
                    if after and isinstance(k, int):
                        for j in X_STEPS.get(k, ()):
                            forward_x(m - 1, j, ob + 2 if more else ob + 1)
                paced4(pe, 6, 14, 18, step)

            gdone_last = (L - 1) * NOCT + 1

            def start_a(m, gdone):
                pe.wait_ge(zt_ld, m * (16 * 3) + 16 * 3)
                for par in range(2):
                    pe.wait_ge(x_ev[par], gdone * 3)

            main(0, None, True, False, False)
            for j in range(6):
                forward_x(0, j, 0)

            def spectral(l, first):
                pe.wait_ge(wts, l * 2 + 2)
                m = l * NOCT + 1
                for g in range(2):
                    pe.wait_ge(r_ok[g], m * XP)
                pe.wait_ge(q_ad, m * XP)
                pe.wait_ge(y_ev, m * XP)

                def step(c, q, i):
                    p = q % 2
                    if inside(c, 0, MODES):
                        pe.wait_ge(rs_ld[q], l * 192 + ((c - q) * 16 + 64))
                        if register(l, c) or c >= 1:
                            pe.wait_ge(f_new, (l * MODES + c) * 2)
                        for a in range(2):
                            last = mm(ps_w2[:, a, :], w2s[:, :], rs[:, q, HC * a:HC * a + HC], start=True, stop=True)
                        last.then_inc(w2_mm, 1)
                    if inside(c, 1, MODES + 1):
                        pe.wait_ge(w_neg, (l * MODES + c) * 2)
                        pe.wait_ge(f_new, (l * MODES + c) * 2)
                        if register(l, c) or c >= 2:
                            pe.wait_ge(zc_ev, l * MODES + c - 1)
                        pe.sem_inc(pe_passed, 1)
                        for ky in range(MODES):
                            for h in range(2):
                                rows = slice(64 * h, 64 * h + 64)
                                last = mm(ps_mix[rows, ky // 6, B * (ky % 6):B * (ky % 6) + B],
                                          wch[rows, (q - 1) % 4, 64 * ky:64 * ky + 64], fst[rows, 1 - p, B * ky:B * ky + B],
                                          start=True, stop=True)
                        last.then_inc(mix_mm, 1)
                    if inside(c, 2, MODES + 2):
                        pe.wait_ge(zc_ev, l * MODES + c - 1)
                        if register(l, c) or c >= 3:
                            pe.wait_ge(zo_ev, l * MODES + c - 2)
                        for a in range(2):
                            last = mm(ps_w1[:, a, :], w1s[:, :], zc[:, p, HC * a:HC * a + HC], start=True, stop=True)
                        last.then_inc(w1_mm, 1)
                paced4(pe, 4, 12, 14, step)
                pe.wait_ge(peak_ok, l * 7 + 2)
                nc.tensor.transpose(ps_a[0][0:1, 0:P], scl[:, 0:1], ident).then_inc(row_mm, 1)
                pe.wait_ge(one_ok, l + 1)
                mm(ps_a[1][:, 0:1], ones[:, :], scl[0:1, 1:2], start=True, stop=True).then_inc(all_mm, 1)

            def octets(l, forward):
                pe.wait_ge(f_new, l * (2 * MODES) + 2 * MODES)
                pe.wait_ge(zc_ev, l * MODES + MODES)
                pe.wait_ge(zo_ev, l * MODES + MODES)
                pe.wait_ge(scale_ok, l + 1)
                start_a(l * NOCT, l * NOCT + 1)
                for ky in range(MODES):
                    stage_a(l * NOCT, ky, ps_first)
                in_layer(pe, lambda n, more, after:
                         main(l * NOCT + n + 1, l * NOCT + n, forward, more, after and forward, not after))
                if forward:
                    for j in range(6):
                        forward_x(l * NOCT + NOCT, j, l * NOCT + NOCT)

            def epilogue():
                def step(k, p, i):
                    if not isinstance(k, int) or k >= 2:
                        pe.wait_ge(h_ev, k - 1)
                    pe.wait_ge(q_act, k + 1)
                    mm(ps_a[p][0:32, :], q2m[:, :], qacc[:, k, :], start=True, stop=True).then_inc(q2_mm, 1)
                paced(pe, 0, 2, XP, XP, step)
            layers(pe, octets, spectral, epilogue)


def token_stage(nc, A, h_d, out):
    with ExitStack() as ctx:
        def sb(name, shape, dt=F32):
            return ctx.enter_context(nc.sbuf_tensor(name, shape, dt))

        def sem(name):
            return ctx.enter_context(nc.semaphore(name))

        NG = NT // 4
        HALVES = slice(0, NT // 2), slice(NT // 2, NT)
        NC = NT // 8
        SCALE = 256.0
        WSCALE = 1024.0
        tok = sb("tok", [P, NT, D])
        f = sb("f", [P, NT, D])
        att = sb("att", [P, NT, D])
        tmp = sb("tmp", [P, NT, D])
        z = att
        fhl = sb("fhl", [P, 3, NT, 2, D], F16)
        x = sb("x", [P, 3, NT * P], F16)
        zhl, zx = fhl[:, 0, :, :, :], x[:, 0, :]
        fj = sb("fj", [P, 2, D])
        e = sb("e", [P, 2, 1024])
        ot = sb("ot", [P, 512])
        rs = sb("rsum", [P, NT, NC])
        st = sb("st", [P, 8, NT])
        idt = sb("idt", [P, P])
        idh = sb("idh", [P, P], F16)
        self32 = sb("self32", [P, E * P])
        sel = sb("sel", [P, E * P], F16)
        w1 = sb("w1", [P, E, HID])
        w1h = sb("w1h", [P, 2, E, HID], F16)
        w2 = sb("w2", [P, E, D])
        wgt = sb("wgt", [P, E])
        wgh = sb("wgh", [P, 2, E], F16)
        wscl = sb("wscl", [P, 8])
        ones = sb("ones_tok", [1, P])
        b1 = sb("b1", [P, E])
        b2 = sb("b2", [P, 2, P])
        bgb = sb("bgb", [P, 2, E])
        order = sb("order", [P, E])
        lg = sb("lg", [P, NT, E])
        cw = sb("cw", [P, NT, E])
        pick = sb("pick", [P, 2, NT, E])
        wt32 = sb("wt32", [P, NT * P])
        wth = sb("wth", [P, NT * P], F16)
        wscale, wunscale = wscl[:, 5:6], wscl[:, 6:7]
        hb = e[:, :, :].rearrange("p a (b n) -> p a b n", b=2)
        hw = sb("hw", [P, 2, 2, 512])
        ps = ctx.enter_context(nc.psum_tensor("ps_tok", [P, 8, 512], F32))

        ld, small, chain, rooted = sem("ld"), sem("small"), sem("chain"), sem("rooted")
        sp_passed = sem("sp_passed_tok")
        to_root, root_ok = sem("to_root"), sem("root_ok")
        to_square, square_ok = sem("to_square"), sem("square_ok")
        peak_ok, row_mm, one_ok, all_mm, w1_ok = (sem(n) for n in (
            "wpeak_ok", "wrow_mm", "wone_ok", "wall_mm", "w1_ok"))
        wt_hi = sem("wt_hi")
        idh_ok, split_ok = sem("idh_ok"), sem("split_ok")
        p_mm, p_ev = sem("p_mm"), [sem("p_ev0"), sem("p_ev1")]
        s_mm, exp_ok, fj_ok, pv_mm = (sem(n) for n in ("s_mm", "exp_ok", "fj_ok", "pv_mm"))
        ot_ok, ot_mm, att_ok = (sem(n) for n in ("ot_ok", "ot_mm", "att_ok"))
        zt_ok = [sem("zt_ok0"), sem("zt_ok1")]
        z_ok, zt_mm, lg_mm, cw_ok, wt_mm, wt_ok = (sem(n) for n in (
            "z_ok", "zt_mm", "lg_mm", "cw_ok", "wt_mm", "wt_ok"))
        h_mm, h_ok, wb_mm, hw_ok, y_mm, y_ok, yt_mm, o_ok, o_st = (sem(n) for n in (
            "th_mm", "th_ok", "wb_mm", "hw_ok", "ty_mm", "ty_ok", "yt_mm", "o_ok", "o_st"))
        N_LD, N_SMALL = 10, 11

        def prime(eng, *sems):
            for s in sems:
                eng.sem_inc(s, 1)

        block = ctx.enter_context(nc.Block())

        @block.sync
        def _(sp):
            tv = A["txt"].rearrange("b s d -> b (s d)")
            tf = tok[:, :, :].rearrange("p t d -> p (t d)")
            for b in range(4):
                sp.dma_start(tf[2 * b:2 * b + 121:8, :].rearrange("p (k n) -> p k n", k=12),
                             h_d[0:12, :, b, :].rearrange("k c n -> c k n")).then_inc(ld, 16)
                sp.dma_start(tf[2 * b + 1:2 * b + 122:8, 0:16 * D].rearrange("p (k n) -> p k n", k=4),
                             h_d[12:16, :, b, :].rearrange("k c n -> c k n")).then_inc(ld, 16)
            sp.dma_start(tf[1:P:2, 16 * D:], tv).then_inc(ld, 16)
            sp.dma_start(idt[:, :], A["table"][:, T_ID:T_ID + P]).then_inc(ld, 16)
            sp.wait_ge(rooted, 1)
            for dst, src in (
                    (self32[:, :], A["table"][:, T_SEL:T_END]),
                    (w1[0:64, :, :], A["ew1"].rearrange("e c h -> c e h")),
                    (w1[64:P, :, :], A["ew1"].rearrange("e c h -> c e h")),
                    (w2[:, :, :], A["ew2"].rearrange("e h c -> h e c")),
                    (wgt[0:64, :], A["wg"]), (wgt[64:P, :], A["wg"]),
                    (b1[:, :], A["eb1"]), (b2[0:E, 0, 0:D], A["eb2"]), (b2[0:E, 1, D:], A["eb2"]),
                    (bgb[:, 0, :], A["bg"]), (bgb[:, 1, :], A["bias"])):
                sp.dma_start(dst, src).then_inc(small, 16)
            ov = out.rearrange("b (r t) d -> (b r) (t d)", r=2)
            with sp.Fori(0, NC) as q:
                wait_alone(sp, o_ok, q + 1 + 1, sp_passed)
                sp.dma_start(ov[:, bass.ds(q * 8 * D, 8 * D)], tok[:, bass.ds(q * 8, 8), :].rearrange("p t d -> p (t d)")
                             ).then_inc(o_st, 16)
            sp.wait_ge(o_st, 16 * NC)

        @block.gpsimd
        def _(pool):
            g = nc.gpsimd
            g.memset(b2[:, :, :], 0.0)
            g.memset(wt32[:, :], 0.0)
            g.memset(wth[:, :], 0.0).then_inc(rooted, 1)

        def wide(col, n=D):
            return col[:, :, None].broadcast_to([P, col.shape[1], n])

        @block.vector
        def _(dve):
            prime(dve, ot_ok, att_ok, hw_ok, y_ok, o_ok)
            v = nc.vector
            done = [0]

            def then(ins):
                done[0] += 1
                ins.then_inc(chain, 1)
                dve.wait_ge(chain, done[0])

            n_root = [0]

            def root(ins):
                n_root[0] += 1
                ins.then_inc(to_root, 1)

            def center(src, dst, T):
                then(v.tensor_reduce(st[:, 0, T], src[:, T, :], AX.X, ALU.add))
                then(v.tensor_scalar(st[:, 0, T], st[:, 0, T], 1.0 / D, None, ALU.mult))
                v.tensor_tensor(dst[:, T, :], src[:, T, :], wide(st[:, 0, T]), ALU.subtract).then_inc(to_square, 1)

            n_square = [0]

            def squares(T):
                n_square[0] += 1
                dve.wait_ge(square_ok, n_square[0])
                return v.tensor_reduce(st[:, 1, T], tmp[:, T, :], AX.X, ALU.add)

            def variance(T):
                then(squares(T))
                root(v.tensor_scalar(st[:, 2, T], st[:, 1, T], 1.0 / D, 1e-5, ALU.mult, ALU.add))

            dve.wait_ge(ld, 16 * N_LD)
            v.tensor_copy(idh[:, :], idt[:, :]).then_inc(idh_ok, 1)
            for T in HALVES:
                center(tok, f, T)
            for T in HALVES:
                variance(T)
            for half, T in enumerate(HALVES):
                dve.wait_ge(root_ok, half + 1)
                then(v.reciprocal(st[:, 3, T], st[:, 2, T]))
                then(v.tensor_tensor(st[:, 4, T], st[:, 1, T], st[:, 3, T], ALU.mult))
                then(v.tensor_scalar(st[:, 4, T], st[:, 4, T], 1e-12, None, ALU.max))
                then(v.reciprocal(st[:, 5, T], st[:, 4, T]))
                then(v.tensor_tensor(st[:, 4, T], st[:, 5, T], st[:, 3, T], ALU.mult))
                then(v.tensor_tensor(f[:, T, :], f[:, T, :], wide(st[:, 4, T]), ALU.mult))
                then(v.tensor_scalar(fhl[:, 0, T, 0, :], f[:, T, :], SCALE, None, ALU.mult))
                for c in range(2):
                    v.tensor_copy(fhl[:, 1, T, c, :], fhl[:, 0, T, 0, :])
                then(v.scalar_tensor_tensor(out=fhl[:, 0, T, 1, :], in0=f[:, T, :], scalar=SCALE,
                                            in1=fhl[:, 0, T, 0, :], op0=ALU.mult, op1=ALU.subtract))
                for c in range(2):
                    last = v.tensor_copy(fhl[:, 2, T, c, :], fhl[:, 0, T, 1, :])
                last.then_inc(split_ok, 1)
            for i in range(E):
                v.memset(order[:, i:i + 1], float(E - i))

            with dve.Fori(NG // 4, NG // 2) as i:
                dve.wait_ge(p_mm, i * 2 + 2)
                v.tensor_copy(x[:, :, bass.ds(i * 1024 + 512, 512)], ps[:, 3:6, :]).then_inc(p_ev[1], 1)

            def scale_of_weights():
                dve.wait_ge(small, 16 * N_SMALL)
                then(v.tensor_reduce(wscl[:, 1:2], w1[:, :, :].rearrange("p e h -> p (e h)"), AX.X, ALU.max,
                                     apply_absolute_value=True))
                then(v.tensor_reduce(wscl[:, 2:3], wgt[:, :], AX.X, ALU.max, apply_absolute_value=True))
                v.memset(ones[:, :], 1.0)
                v.tensor_reduce(wscl[:, 0:1], wscl[:, 1:3], AX.X, ALU.max).then_inc(peak_ok, 1)
                dve.wait_ge(row_mm, 1)
                v.tensor_reduce(wscl[0:1, 3:4], ps[0:1, 7, 0:P], AX.X, ALU.max).then_inc(one_ok, 1)
                dve.wait_ge(all_mm, 1)
                then(v.tensor_scalar(wscl[:, 1:2], ps[:, 7, P:P + 1], 2.0 ** -60, None, ALU.max))
                then(v.tensor_scalar(wscl[:, 2:3].bitcast(mybir.dt.int32), wscl[:, 1:2].bitcast(mybir.dt.int32),
                                     0x7F800000, None, ALU.bitwise_and))
                then(v.reciprocal(wscl[:, 4:5], wscl[:, 2:3]))
                then(v.tensor_scalar(wunscale, wscl[:, 2:3], 2.0 ** -14 / SCALE, None, ALU.mult))
                then(v.tensor_scalar(wscale, wscl[:, 4:5], 2.0 ** 14, None, ALU.mult))
                for w, wh in ((w1[:, :, :], w1h), (wgt[:, :], wgh)):
                    then(v.tensor_scalar(wh[:, 0], w, wscale, None, ALU.mult))
                    v.scalar_tensor_tensor(out=wh[:, 1], in0=w, scalar=wscale, in1=wh[:, 0],
                                           op0=ALU.mult, op1=ALU.subtract).then_inc(w1_ok, 1)

            scale_of_weights()

            with dve.Fori(0, NC) as ci:
                def step(j, p, i):
                    if not (isinstance(j, int) and j < 2):
                        dve.wait_ge(pv_mm, ci * NT + j - 1)
                    else:
                        dve.wait_ge(att_ok, ci + 1)
                    v.tensor_copy(fj[:, p, :], f[:, bass.ds(j, 1), :].rearrange("p t d -> p (t d)")
                                  ).then_inc(fj_ok, 1)
                paced(dve, 0, 2, NT, NT, step)
                dve.wait_ge(pv_mm, ci * NT + NT)
                v.tensor_copy(ot[:, :], ps[:, 4, :]).then_inc(ot_ok, 1)
                dve.wait_ge(ot_mm, ci + 1)
                v.tensor_copy(att[:, bass.ds(ci * 8, 8), :].rearrange("p (h s) d -> p s h d", h=2),
                              ps[:, 5, :].rearrange("p (s h d) -> p s h d", s=4, h=2)).then_inc(att_ok, 1)

            dve.wait_ge(exp_ok, NC * NT + 1)
            dve.wait_ge(att_ok, NC + 1)
            then(v.tensor_reduce(st[:, 4, :], rs[:, :, :], AX.X, ALU.add))
            then(v.reciprocal(st[:, 5, :], st[:, 4, :]))
            then(v.tensor_scalar(st[:, 5, :], st[:, 5, :], 1.0 - 0.8, None, ALU.mult))
            for T in HALVES:
                then(v.tensor_tensor(att[:, T, :], att[:, T, :], wide(st[:, 5, T]), ALU.mult))
                v.scalar_tensor_tensor(out=att[:, T, :], in0=f[:, T, :], scalar=0.8, in1=att[:, T, :],
                                       op0=ALU.mult, op1=ALU.add).then_inc(to_square, 1)
            for T in HALVES:
                root(squares(T))
            for half, T in enumerate(HALVES):
                dve.wait_ge(root_ok, 2 + half + 1)
                then(v.tensor_scalar(st[:, 4, T], st[:, 1, T], 1e-12, None, ALU.max))
                then(v.reciprocal(st[:, 5, T], st[:, 4, T]))
                then(v.tensor_tensor(att[:, T, :], att[:, T, :], wide(st[:, 5, T]), ALU.mult))
                then(v.tensor_tensor(tok[:, T, :], tok[:, T, :], att[:, T, :], ALU.add))
                center(tok, z, T)
            for T in HALVES:
                variance(T)
            for half, T in enumerate(HALVES):
                dve.wait_ge(root_ok, 4 + half + 1)
                then(v.reciprocal(st[:, 3, T], st[:, 2, T]))
                then(v.tensor_tensor(z[:, T, :], z[:, T, :], wide(st[:, 3, T]), ALU.mult))
                then(v.tensor_scalar(zhl[:, T, 0, :], z[:, T, :], SCALE, None, ALU.mult))
                v.scalar_tensor_tensor(out=zhl[:, T, 1, :], in0=z[:, T, :], scalar=SCALE, in1=zhl[:, T, 0, :],
                                       op0=ALU.mult, op1=ALU.subtract).then_inc(z_ok, 1)

            for i in range(NG // 2 + 1, NG, 2):
                dve.wait_ge(zt_mm, i + 1)
                v.tensor_copy(zx[:, 512 * i:512 * i + 512], ps[:, i % 2, :]).then_inc(zt_ok[1], 1)
            then(v.tensor_tensor(bgb[:, 0, :], bgb[:, 0, :], bgb[:, 1, :], ALU.add))
            dve.wait_ge(lg_mm, 1)
            then(v.scalar_tensor_tensor(out=lg[:, :, :], in0=ps[:, 2, 0:NT * E].rearrange("p (t e) -> p t e", e=E),
                                        scalar=wunscale, in1=bgb[:, 0:1, :].broadcast_to([P, NT, E]),
                                        op0=ALU.mult, op1=ALU.add))
            for n in range(2):
                top = st[:, 4 + n, :]
                then(v.tensor_reduce(top, lg[:, :, :], AX.X, ALU.max))
                then(v.tensor_tensor(pick[:, n, :, :], lg[:, :, :], wide(top, E), ALU.is_equal))
                then(v.tensor_tensor(pick[:, n, :, :], pick[:, n, :, :], order[:, None, :].broadcast_to([P, NT, E]),
                                     ALU.mult))
                then(v.tensor_reduce(st[:, 6, :], pick[:, n, :, :], AX.X, ALU.max))
                then(v.tensor_tensor(pick[:, n, :, :], pick[:, n, :, :], wide(st[:, 6, :], E), ALU.is_equal))
                if n == 0:
                    then(v.scalar_tensor_tensor(out=lg[:, :, :], in0=pick[:, 0, :, :], scalar=-3e38,
                                                in1=lg[:, :, :], op0=ALU.mult, op1=ALU.add))
            root(v.tensor_tensor(st[:, 6, :], st[:, 5, :], st[:, 4, :], ALU.subtract))
            dve.wait_ge(root_ok, n_root[0])
            then(v.tensor_scalar(st[:, 0, :], st[:, 6, :], 1.0, None, ALU.add))
            then(v.reciprocal(st[:, 1, :], st[:, 0, :]))
            then(v.tensor_tensor(st[:, 2, :], st[:, 1, :], st[:, 6, :], ALU.mult))
            then(v.tensor_tensor(cw[:, :, :], pick[:, 0, :, :], wide(st[:, 1, :], E), ALU.mult))
            then(v.tensor_tensor(lg[:, :, :], pick[:, 1, :, :], wide(st[:, 2, :], E), ALU.mult))
            v.tensor_tensor(cw[:, :, :], cw[:, :, :], lg[:, :, :], ALU.add).then_inc(cw_ok, 1)
            v.tensor_copy(sel[:, :], self32[:, :]).then_inc(cw_ok, 1)
            dve.wait_ge(rooted, 1)
            for i in range(NG):
                cols = slice(512 * i, 512 * i + 512)
                src = ps[0:E, 3 + i % 4, :]
                dve.wait_ge(wt_hi, i + 1)
                if i % 2:
                    v.tensor_copy(wt32[0:E, cols], src)
                v.scalar_tensor_tensor(out=wth[32:32 + E, cols], in0=src, scalar=WSCALE, in1=wth[0:E, cols],
                                       op0=ALU.mult, op1=ALU.subtract).then_inc(wt_ok, 1)

            with dve.Fori(0, NC) as q:
                for i in range(E):
                    for par in range(2):
                        dve.wait_ge(wb_mm, q * (2 * E) + (2 * i + par + 1))
                        dve.wait_ge(h_ok, q * (2 * E) + (2 * i + par + 1) + 1)
                        if i >= 2:
                            dve.wait_ge(y_mm, q * E + (i - 1))
                        v.tensor_tensor(hw[:, i % 2, par, :], ps[:, 4 + par, :], hb[:, i % 2, par, :], ALU.mult
                                        ).then_inc(hw_ok, 1)
                dve.wait_ge(y_mm, q * E + E)
                v.tensor_copy(ot[:, :], ps[:, 6, :]).then_inc(y_ok, 1)
                dve.wait_ge(yt_mm, q + 1)
                chunk = tok[:, bass.ds(q * 8, 8), :].rearrange("p (h s) d -> p s h d", h=2)
                v.tensor_tensor(chunk, ps[:, 7, :].rearrange("p (s h d) -> p s h d", s=4, h=2), chunk, ALU.add
                                ).then_inc(o_ok, 1)

        @block.scalar
        def _(act):
            prime(act, exp_ok, h_ok, *p_ev)
            def root(n, cols, T):
                act.wait_ge(to_root, n)
                nc.scalar.activation(st[:, cols, T], st[:, cols, T], ACT.Sqrt).then_inc(root_ok, 1)

            def square(n, src, T):
                act.wait_ge(to_square, n)
                nc.scalar.activation(tmp[:, T, :], src[:, T, :], ACT.Square).then_inc(square_ok, 1)

            for half, T in enumerate(HALVES):
                square(half + 1, f, T)
            for half, T in enumerate(HALVES):
                root(half + 1, slice(1, 3), T)
            with act.Fori(0, NG // 4) as i:
                for p in range(2):
                    act.wait_ge(p_mm, i * 2 + p + 1)
                    nc.scalar.copy(x[:, :, bass.ds(i * 1024 + 512 * p, 512)], ps[:, 3 * p:3 * p + 3, :]).then_inc(p_ev[p], 1)
            with act.Fori(NG // 4, NG // 2) as i:
                act.wait_ge(p_mm, i * 2 + 1)
                nc.scalar.copy(x[:, :, bass.ds(i * 1024, 512)], ps[:, 0:3, :]).then_inc(p_ev[0], 1)

            with act.Fori(0, NC) as ci:
                def step(j, p, i):
                    act.wait_ge(s_mm, ci * NT + j + 1)
                    if not (isinstance(j, int) and j < 2):
                        act.wait_ge(pv_mm, ci * NT + j - 1)
                    else:
                        act.wait_ge(ot_ok, ci + 1)
                    nc.scalar.activation(e[:, p, :], ps[:, 2 * p:2 * p + 2, :].rearrange("p a n -> p (a n)"), ACT.Exp,
                                         scale=1.0 / (SCALE * SCALE),
                                         accum_out=rs[:, bass.ds(j, 1), bass.ds(ci, 1)].rearrange("p t c -> p (t c)")
                                         ).then_inc(exp_ok, 1)
                paced(act, 0, 2, NT, NT, step)
            for src, cols, before in ((att, slice(1, 2), 2), (z, slice(1, 3), 4)):
                for half, T in enumerate(HALVES):
                    square(before + half + 1, src, T)
                for half, T in enumerate(HALVES):
                    root(before + half + 1, cols, T)
            for i in [*range(NG // 2), *range(NG // 2, NG, 2)]:
                act.wait_ge(zt_mm, i + 1)
                nc.scalar.copy(zx[:, 512 * i:512 * i + 512], ps[:, i % 2, :]).then_inc(zt_ok[0], 1)
            act.wait_ge(to_root, 7)
            nc.scalar.activation(st[:, 6, :], st[:, 6, :], ACT.Exp).then_inc(root_ok, 1)
            act.wait_ge(rooted, 1)
            for i in range(NG):
                cols = slice(512 * i, 512 * i + 512)
                act.wait_ge(wt_mm, i + 1)
                if i % 2 == 0:
                    nc.scalar.copy(wt32[0:E, cols], ps[0:E, 3 + i % 4, :])
                nc.scalar.activation(wth[0:E, cols], ps[0:E, 3 + i % 4, :], ACT.Copy, scale=WSCALE).then_inc(wt_hi, 1)
            act.wait_ge(small, 16 * N_SMALL)
            act.wait_ge(w1_ok, 2)
            with act.Fori(0, NC) as q:
                for i in range(E):
                    for par in range(2):
                        act.wait_ge(h_mm, q * (2 * E) + (2 * i + par + 1))
                        if i >= 2:
                            act.wait_ge(hw_ok, q * (2 * E) + (2 * i + par - 3) + 1)
                        else:
                            act.wait_ge(hw_ok, q * (2 * E) + 1)
                        nc.scalar.activation(hb[:, i % 2, par, :], ps[:, 2 * (i % 2) + par, :], ACT.Relu,
                                             bias=b1[:, i:i + 1], scale=wunscale).then_inc(h_ok, 1)

        @block.tensor
        def _(pe):
            mm = nc.tensor.matmul
            pe.wait_ge(idh_ok, 1)
            def transposes(i):
                for p in range(2):
                    pe.wait_ge(p_ev[p], i + 1)
                    for kind in range(3):
                        for t in range(4):
                            src = fhl[:, kind, bass.ds(i * 8 + (4 * p + t), 1), :, :].rearrange("p t c d -> p (t c d)")
                            last = mm(ps[:, 3 * p + kind, P * t:P * t + P], src, idh[:, :], start=True, stop=True)
                    last.then_inc(p_mm, 1)

            for half in range(2):
                pe.wait_ge(split_ok, half + 1)
                with pe.Fori(NG // 4 * half, NG // 4 * (half + 1)) as i:
                    transposes(i)
            for p in range(2):
                pe.wait_ge(p_ev[p], NG // 2 + 1)
            pe.wait_ge(peak_ok, 1)
            nc.tensor.transpose(ps[0:1, 7, 0:P], wscl[:, 0:1], idt[:, :]).then_inc(row_mm, 1)
            pe.wait_ge(one_ok, 1)
            mm(ps[:, 7, P:P + 1], ones[:, :], wscl[0:1, 3:4], start=True, stop=True).then_inc(all_mm, 1)

            with pe.Fori(0, NC) as ci:
                def step(j, p, i):
                    if inside(j, 0, NT):
                        if not (isinstance(j, int) and j < 2):
                            pe.wait_ge(exp_ok, ci * NT + j - 1 + 1)
                        else:
                            pe.wait_ge(exp_ok, ci * NT + 1)
                        for h in range(2):
                            for kind in range(2):
                                last = mm(ps[:, 2 * p + h, :], x[:, 1 + kind, bass.ds(j * P, P)],
                                          x[:, 0, bass.ds(ci * 1024 + 512 * h, 512)], start=(kind == 0), stop=(kind == 1))
                        last.then_inc(s_mm, 1)
                    if inside(j, 1, NT + 1):
                        pe.wait_ge(exp_ok, ci * NT + j + 1)
                        pe.wait_ge(fj_ok, ci * NT + j)
                        if isinstance(j, int) and j == 1:
                            pe.wait_ge(ot_ok, ci + 1)
                        q = 1 - p
                        for h in range(2):
                            last = mm(ps[64 * h:64 * h + 64, 4, :], fj[:, q, :], e[:, q, 512 * h:512 * h + 512],
                                      start=isinstance(j, int) and j == 1, stop=isinstance(j, int) and j == NT)
                        last.then_inc(pv_mm, 1)
                paced(pe, 0, 2, NT, NT + 1, step)
                pe.wait_ge(ot_ok, ci + 1 + 1)
                pe.wait_ge(att_ok, ci + 1)
                for s in range(4):
                    last = nc.tensor.transpose(ps[:, 5, P * s:P * s + P], ot[:, P * s:P * s + P], idt[:, :])
                last.then_inc(ot_mm, 1)

            for i in range(NG):
                pe.wait_ge(z_ok, i // (NG // 2) + 1)
                if i >= 2:
                    late = max(i - 2 - NG // 2, 0)
                    if late % 2:
                        pe.wait_ge(zt_ok[1], late // 2 + 1)
                    else:
                        pe.wait_ge(zt_ok[0], i - 1 - late + late // 2)
                for s in range(4):
                    src = zhl[:, 4 * i + s, :, :].rearrange("p c d -> p (c d)")
                    last = mm(ps[:, i % 2, P * s:P * s + P], src, idh[:, :], start=True, stop=True)
                last.then_inc(zt_mm, 1)
            pe.wait_ge(w1_ok, 2)
            pe.wait_ge(zt_ok[0], NG // 2 + NG // 4)
            pe.wait_ge(zt_ok[1], NG // 4)
            for t in range(NT):
                for c in range(2):
                    last = mm(ps[:, 2, E * t:E * t + E], zx[:, P * t:P * t + P], wgh[:, c, :],
                              start=(c == 0), stop=(c == 1))
            last.then_inc(lg_mm, 1)
            pe.wait_ge(cw_ok, 2)
            for i in range(NG):
                if i >= 4:
                    pe.wait_ge(wt_ok, i - 3)
                for s in range(4):
                    last = nc.tensor.transpose(ps[0:E, 3 + i % 4, P * s:P * s + P], cw[:, 4 * i + s, :], idt[:, :])
                last.then_inc(wt_mm, 1)
            pe.wait_ge(wt_ok, NG)

            with pe.Fori(0, NC) as q:
                def down(i):
                    for par in range(2):
                        pe.wait_ge(hw_ok, q * (2 * E) + (2 * i + par + 1) + 1)
                        last = mm(ps[64 * par:64 * par + 64, 6, :], w2[:, i, :], hw[:, i % 2, par, :],
                                  start=False, stop=(i == E - 1))
                    last.then_inc(y_mm, 1)

                for i in range(E):
                    for par in range(2):
                        if i >= 2:
                            pe.wait_ge(h_ok, q * (2 * E) + (2 * i + par - 3) + 1)
                        else:
                            pe.wait_ge(h_ok, q * (2 * E) + 1)
                        for c in range(2):
                            last = mm(ps[:, 2 * (i % 2) + par, :], w1h[:, c, i, :],
                                      zx[:, bass.ds(q * 1024 + 512 * par, 512)], start=(c == 0), stop=(c == 1))
                        last.then_inc(h_mm, 1)
                    for par in range(2):
                        if i >= 1:
                            pe.wait_ge(hw_ok, q * (2 * E) + (2 * i + par - 1) + 1)
                        else:
                            pe.wait_ge(hw_ok, q * (2 * E) + 1)
                        mm(ps[:, 4 + par, :], sel[:, P * i:P * i + P], wth[:, bass.ds(q * 1024 + 512 * par, 512)],
                           start=True, stop=True).then_inc(wb_mm, 1)
                    if i == 0:
                        pe.wait_ge(y_ok, q + 1)
                        for par in range(2):
                            mm(ps[:, 6, :], b2[:, par, :], wt32[:, bass.ds(q * 1024 + 512 * par, 512)],
                               start=(par == 0), stop=False)
                    else:
                        down(i - 1)
                down(E - 1)
                pe.wait_ge(y_ok, q + 1 + 1)
                pe.wait_ge(o_ok, q + 1)
                for s in range(4):
                    last = nc.tensor.transpose(ps[:, 7, P * s:P * s + P], ot[:, P * s:P * s + P], idt[:, :])
                last.then_inc(yt_mm, 1)


def build_kernel(nc, A, out):
    scratch = {
        "z": nc.dram_tensor("modes_scratch", [2 * KX, MODES, C, B], F32).ap(),
        "r": nc.dram_tensor("new_modes_scratch", [C, 2 * KX, CH], F32).ap(),
        "u": nc.dram_tensor("inverse_scratch", [NOCT * P, 2, MODES, N], F16).ap(),
        "t": nc.dram_tensor("forward_scratch", [NOCT * S, 2, MODES, N], F32).ap(),
    }
    h_d = nc.dram_tensor("h_scratch", [XP, 16, 4, 4 * S], F32).ap()
    operator_stage(nc, A, scratch, h_d)
    token_stage(nc, A, h_d, out)


def kernel(**inputs):
    import concourse.bacc as _bacc
    from concourse.bass_utils import run_bass_kernel_spmd as _run

    def get(name):
        return np.asarray(inputs[name])

    def tok(name):
        return get("L0_tok_" + name)

    pw, pb, fw = tok("p_w"), tok("p_b"), tok("fw")
    by_mode = fw.transpose(0, 1, 2, 4, 5, 6, 3)
    arrays = {
        "table": constant_table(),
        "xt": get("x")[..., 0].transpose(1, 2, 0).reshape(32, P, B).transpose(1, 0, 2),
        "w1t": tok("w1_w").transpose(0, 2, 1),
        "w2t": tok("w2_w").transpose(0, 2, 1),
        "w2": tok("w2_w"),
        "pt": np.concatenate([pw.T, pb[None]], 0),
        "pc": np.pad(np.concatenate([pw, pb[:, None]], 1), ((0, 0), (0, OCT - MID))),
        "q1t": tok("q1_w").T,
        "b2t": tok("w2_b").T,
        "b1t": tok("w1_b").T,
        "q1b": np.tile(np.repeat(tok("q1_b"), 4), 8)[:, None],
        "q2c": np.tile(np.repeat(tok("q2_w")[0], 4), 8)[:, None],
        "q2b": np.broadcast_to(tok("q2_b"), (32, 1)),
        "b1w": np.repeat(tok("w1_b"), B, axis=1),
        "fwt": np.stack([by_mode, by_mode[:, :, :, :, :, ::-1]], 2).reshape(L, P, MODES, CH),
        "txt": get("txt"),
        "ew1": get("L0_ffn_W1"),
        "ew2": get("L0_ffn_W2"),
        "wg": get("L0_ffn_Wg"),
        "eb1": get("L0_ffn_b1").T,
        "eb2": get("L0_ffn_b2"),
        "bg": np.broadcast_to(get("L0_ffn_bg"), (P, E)),
        "bias": np.broadcast_to(get("L0_ffn_bias"), (P, E)),
    }
    arrays = {f"in_{name}": np.ascontiguousarray(a) for name, a in arrays.items()}
    nc = _bacc.Bacc("TRN2", target_bir_lowering=False, num_devices=1)
    A = {name[3:]: nc.dram_tensor(name, a.shape, mybir.dt.from_np(a.dtype), kind="ExternalInput").ap()
         for name, a in arrays.items()}
    out = nc.dram_tensor("out_dram", (B, SEQ, D), F32, kind="ExternalOutput").ap()
    build_kernel(nc, A, out)
    r = _run(nc, [arrays], core_ids=[0])
    return r.results[0]["out_dram"]
```
